# Optimizing a Trainium2 kernel written in Bass

```python
import numpy as np
import jax
import jax.numpy as jnp

def _softmax(x, axis=-1):
    return jax.nn.softmax(x, axis=axis)

def _gelu(x):
    return jax.nn.gelu(x, approximate=True)

def _silu(x):
    return jax.nn.silu(x)

def _sigmoid(x):
    return jax.nn.sigmoid(x)

def _layernorm(x, axis=-1, eps=1e-05):
    m = jnp.mean(x, axis=axis, keepdims=True)
    v = jnp.var(x, axis=axis, keepdims=True)
    return (x - m) / jnp.sqrt(v + eps)

def _scatter_add(tgt, idx, src, axis=0):
    return tgt.at[idx].add(src)

def _segment_sum(src, seg, n):
    return jax.ops.segment_sum(src, seg, n)
kernel_name = 'mk_adaln_ffn_d2_seqx_r8_2a28cb'

def setup_inputs(seed: int=0):
    np.random.seed(seed)
    _w = jnp.asarray

    def _rec_inputs():
        import jax
        import jax.numpy as jnp
        _rk = jax.random.key(seed)
        x = -0.0003929 + 0.9999 * jax.random.normal(jax.random.fold_in(_rk, 1), (8, 128, 128), jnp.float32)
        _lenS = 128 - jax.random.randint(jax.random.fold_in(_rk, 7), (8,), 0, max(1, 128 // 4) + 1, jnp.int32)
        _lenS2 = 128 - jax.random.randint(jax.random.fold_in(_rk, 8), (8,), 0, max(1, 128 // 4) + 1, jnp.int32)
        cond_1024 = 0.00513981 + 1.0024 * jax.random.normal(jax.random.fold_in(_rk, 11), (8, 128), jnp.float32)
        return (x, cond_1024)
    x, cond_1024 = _rec_inputs()

    def _L0_cond_setup():
        import jax, jax.numpy as jnp
        import numpy as np
        EMBED = 128
        HID = 128
        B, T = (32, 64)

        def _gru_layer(x, Wih, Whh, bih, bhh):
            H = Whh.shape[1]
            xg = jnp.einsum('bti,gi->tbg', x, Wih) + bih

            def step(h, xt):
                hg = h @ Whh.T + bhh
                xr, xz, xn = jnp.split(xt, 3, axis=-1)
                hr, hz, hn = jnp.split(hg, 3, axis=-1)
                r = jax.nn.sigmoid(xr + hr)
                z = jax.nn.sigmoid(xz + hz)
                n = jnp.tanh(xn + r * hn)
                h_new = (1.0 - z) * n + z * h
                return (h_new, h_new)
            h0 = jnp.zeros((x.shape[0], H), dtype=x.dtype)
            _, ys = jax.lax.scan(step, h0, xg)
            return jnp.transpose(ys, (1, 0, 2))
        key = jax.random.key(seed)
        ks = jax.random.split(key, 16)
        s_in = 1.0 / np.sqrt(EMBED)
        s_h = 1.0 / np.sqrt(HID)
        return {'x': jax.random.normal(ks[0], (B, T, EMBED), jnp.float32), 'context': jax.random.normal(ks[1], (B, HID), jnp.float32), 'W_in': jax.random.uniform(ks[2], (HID, EMBED), jnp.float32, -s_in, s_in), 'b_in': jax.random.uniform(ks[3], (HID,), jnp.float32, -s_in, s_in), 'Wih0': jax.random.uniform(ks[4], (3 * HID, HID), jnp.float32, -s_h, s_h), 'Whh0': jax.random.uniform(ks[5], (3 * HID, HID), jnp.float32, -s_h, s_h), 'bih0': jax.random.uniform(ks[6], (3 * HID,), jnp.float32, -s_h, s_h), 'bhh0': jax.random.uniform(ks[7], (3 * HID,), jnp.float32, -s_h, s_h), 'Wih1': jax.random.uniform(ks[8], (3 * HID, HID), jnp.float32, -s_h, s_h), 'Whh1': jax.random.uniform(ks[9], (3 * HID, HID), jnp.float32, -s_h, s_h), 'bih1': jax.random.uniform(ks[10], (3 * HID,), jnp.float32, -s_h, s_h), 'bhh1': jax.random.uniform(ks[11], (3 * HID,), jnp.float32, -s_h, s_h), 'W_out': jax.random.uniform(ks[12], (EMBED, HID), jnp.float32, -s_h, s_h), 'b_out': jax.random.uniform(ks[13], (EMBED,), jnp.float32, -s_h, s_h), 'W_gate': jax.random.uniform(ks[14], (HID, HID), jnp.float32, -s_h, s_h), 'b_gate': jax.random.uniform(ks[15], (HID,), jnp.float32, -s_h, s_h)}
    _L0_cond_all = _L0_cond_setup()
    _L0_cond_in = {k: v for k, v in _L0_cond_all.items() if k in ('W_in', 'b_in', 'Wih0', 'Whh0', 'bih0', 'bhh0', 'Wih1', 'Whh1', 'bih1', 'bhh1', 'W_out', 'b_out', 'W_gate', 'b_gate')}
    del _L0_cond_all

    def _L0_ffn_setup():
        import jax, jax.numpy as jnp
        import numpy as np
        B, S, D, F, E, TOPK = (4, 256, 128, 512, 8, 2)

        def _moe_forward(x, W_router, W_gate, W_up, W_down):
            logits = jnp.einsum('bsd,ed->bse', x, W_router)
            probs = jax.nn.softmax(logits, axis=-1)
            gates, indices = jax.lax.top_k(probs, TOPK)
            gates = gates / jnp.sum(gates, axis=-1, keepdims=True)
            weights = jnp.sum(gates[..., None] * jax.nn.one_hot(indices, E, dtype=x.dtype), axis=-2)
            weights_e = jnp.moveaxis(weights, -1, 0)

            def body(acc, params):
                wg, wu, wd, wt = params
                gate = jax.nn.silu(jnp.einsum('bsd,fd->bsf', x, wg))
                up = jnp.einsum('bsd,fd->bsf', x, wu)
                y = jnp.einsum('bsf,df->bsd', gate * up, wd)
                return (acc + wt[..., None] * y, None)
            out, _ = jax.lax.scan(body, jnp.zeros_like(x), (W_gate, W_up, W_down, weights_e))
            return out
        key = jax.random.key(seed)
        k1, k2, k3, k4, k5 = jax.random.split(key, 5)
        x = jax.random.normal(k1, (B, S, D), dtype=jnp.float32)
        W_router = jax.random.normal(k2, (E, D), dtype=jnp.float32) / np.sqrt(D)
        W_gate = jax.random.normal(k3, (E, F, D), dtype=jnp.float32) / np.sqrt(D)
        W_up = jax.random.normal(k4, (E, F, D), dtype=jnp.float32) / np.sqrt(D)
        W_down = jax.random.normal(k5, (E, D, F), dtype=jnp.float32) / np.sqrt(F)
        return {'x': x, 'W_router': W_router, 'W_gate': W_gate, 'W_up': W_up, 'W_down': W_down}
    _L0_ffn_all = _L0_ffn_setup()
    _L0_ffn_in = {k: v for k, v in _L0_ffn_all.items() if k in ('W_router', 'W_gate', 'W_up', 'W_down')}
    del _L0_ffn_all

    def _L1_cond_setup():
        import jax, jax.numpy as jnp
        import numpy as np
        B, T, D = (128, 32, 128)
        ADA, INTER, RANK = (128, 128, 8)
        LN_EPS = 1e-05

        def _layernorm(x, g, b):
            mu = jnp.mean(x, axis=-1, keepdims=True)
            var = jnp.var(x, axis=-1, keepdims=True)
            return (x - mu) * jax.lax.rsqrt(var + LN_EPS) * g + b
        key = jax.random.key(seed)
        ks = jax.random.split(key, 9)
        return {'x': jax.random.normal(ks[0], (B, T, D), dtype=jnp.float32), 'ada_emb': jax.random.normal(ks[1], (B, ADA), dtype=jnp.float32), 'base_layer': jax.random.normal(ks[2], (D, D), dtype=jnp.float32), 'w1': jax.random.normal(ks[3], (ADA, INTER), dtype=jnp.float32) * 0.02, 'b1': jnp.zeros((INTER,), dtype=jnp.float32), 'w2': jax.random.normal(ks[4], (INTER, 2 * D * RANK), dtype=jnp.float32) * 0.02, 'b2': jnp.zeros((2 * D * RANK,), dtype=jnp.float32), 'ln_g': jnp.ones((ADA,), dtype=jnp.float32), 'ln_b': jnp.zeros((ADA,), dtype=jnp.float32)}
    _L1_cond_all = _L1_cond_setup()
    _L1_cond_in = {k: v for k, v in _L1_cond_all.items() if k in ('base_layer', 'w1', 'b1', 'w2', 'b2', 'ln_g', 'ln_b')}
    del _L1_cond_all

    def _L1_ffn_setup():
        import jax, jax.numpy as jnp
        import numpy as np
        QP = 127.0
        MIN_RANGE = 1e-06

        def _ste_round(x):
            return x + jax.lax.stop_gradient(jnp.round(x) - x)

        def _quant_per_tensor(x):
            scale = jnp.maximum(jnp.max(jnp.abs(x)), MIN_RANGE) / QP
            return (_ste_round(x / scale), scale)

        def _qlinear(x2d, w, b):
            xq, sx = _quant_per_tensor(x2d)
            wq, sw = _quant_per_tensor(w)
            out = jnp.matmul(xq, wq.T) + b[None, :]
            return out * (sw * sx)
        key = jax.random.key(seed)
        k = jax.random.split(key, 5)
        B, N, D, H = (8, 128, 128, 512)
        return {'x': jax.random.normal(k[0], (B, N, D), dtype=jnp.float32), 'w1': jax.random.normal(k[1], (H, D), dtype=jnp.float32) * 0.02, 'b1': jax.random.normal(k[2], (H,), dtype=jnp.float32) * 0.02, 'w2': jax.random.normal(k[3], (D, H), dtype=jnp.float32) * 0.02, 'b2': jax.random.normal(k[4], (D,), dtype=jnp.float32) * 0.02}
    _L1_ffn_all = _L1_ffn_setup()
    _L1_ffn_in = {k: v for k, v in _L1_ffn_all.items() if k in ('w1', 'b1', 'w2', 'b2')}
    del _L1_ffn_all
    return {'x': x, 'cond_1024': cond_1024, 'L0_cond_W_in': _L0_cond_in['W_in'], 'L0_cond_b_in': _L0_cond_in['b_in'], 'L0_cond_Wih0': _L0_cond_in['Wih0'], 'L0_cond_Whh0': _L0_cond_in['Whh0'], 'L0_cond_bih0': _L0_cond_in['bih0'], 'L0_cond_bhh0': _L0_cond_in['bhh0'], 'L0_cond_Wih1': _L0_cond_in['Wih1'], 'L0_cond_Whh1': _L0_cond_in['Whh1'], 'L0_cond_bih1': _L0_cond_in['bih1'], 'L0_cond_bhh1': _L0_cond_in['bhh1'], 'L0_cond_W_out': _L0_cond_in['W_out'], 'L0_cond_b_out': _L0_cond_in['b_out'], 'L0_cond_W_gate': _L0_cond_in['W_gate'], 'L0_cond_b_gate': _L0_cond_in['b_gate'], 'L0_ffn_W_router': _L0_ffn_in['W_router'], 'L0_ffn_W_gate': _L0_ffn_in['W_gate'], 'L0_ffn_W_up': _L0_ffn_in['W_up'], 'L0_ffn_W_down': _L0_ffn_in['W_down'], 'L1_cond_base_layer': _L1_cond_in['base_layer'], 'L1_cond_w1': _L1_cond_in['w1'], 'L1_cond_b1': _L1_cond_in['b1'], 'L1_cond_w2': _L1_cond_in['w2'], 'L1_cond_b2': _L1_cond_in['b2'], 'L1_cond_ln_g': _L1_cond_in['ln_g'], 'L1_cond_ln_b': _L1_cond_in['ln_b'], 'L1_ffn_w1': _L1_ffn_in['w1'], 'L1_ffn_b1': _L1_ffn_in['b1'], 'L1_ffn_w2': _L1_ffn_in['w2'], 'L1_ffn_b2': _L1_ffn_in['b2']}

def reference(x, cond_1024, L0_cond_W_in, L0_cond_b_in, L0_cond_Wih0, L0_cond_Whh0, L0_cond_bih0, L0_cond_bhh0, L0_cond_Wih1, L0_cond_Whh1, L0_cond_bih1, L0_cond_bhh1, L0_cond_W_out, L0_cond_b_out, L0_cond_W_gate, L0_cond_b_gate, L0_ffn_W_router, L0_ffn_W_gate, L0_ffn_W_up, L0_ffn_W_down, L1_cond_base_layer, L1_cond_w1, L1_cond_b1, L1_cond_w2, L1_cond_b2, L1_cond_ln_g, L1_cond_ln_b, L1_ffn_w1, L1_ffn_b1, L1_ffn_w2, L1_ffn_b2):
    import jax
    import jax.numpy as jnp

    def _L0_cond_ref(x, context, W_in, b_in, Wih0, Whh0, bih0, bhh0, Wih1, Whh1, bih1, bhh1, W_out, b_out, W_gate, b_gate):
        import jax, jax.numpy as jnp
        import numpy as np
        EMBED = 128
        HID = 128
        B, T = (32, 64)

        def _gru_layer(x, Wih, Whh, bih, bhh):
            H = Whh.shape[1]
            xg = jnp.einsum('bti,gi->tbg', x, Wih) + bih

            def step(h, xt):
                hg = h @ Whh.T + bhh
                xr, xz, xn = jnp.split(xt, 3, axis=-1)
                hr, hz, hn = jnp.split(hg, 3, axis=-1)
                r = jax.nn.sigmoid(xr + hr)
                z = jax.nn.sigmoid(xz + hz)
                n = jnp.tanh(xn + r * hn)
                h_new = (1.0 - z) * n + z * h
                return (h_new, h_new)
            h0 = jnp.zeros((x.shape[0], H), dtype=x.dtype)
            _, ys = jax.lax.scan(step, h0, xg)
            return jnp.transpose(ys, (1, 0, 2))
        ctx = context[:, None, :]
        mixed = jnp.tanh(jnp.einsum('bte,he->bth', x, W_in) + b_in + ctx)
        h1 = _gru_layer(mixed, Wih0, Whh0, bih0, bhh0)
        h2 = _gru_layer(h1, Wih1, Whh1, bih1, bhh1)
        gate = jax.nn.sigmoid(jnp.einsum('bh,gh->bg', context, W_gate) + b_gate)
        gated = gate[:, None, :] * h2 + h2
        return jnp.einsum('bth,eh->bte', gated, W_out) + b_out

    def _L0_ffn_ref(x, W_router, W_gate, W_up, W_down):
        import jax, jax.numpy as jnp
        import numpy as np
        B, S, D, F, E, TOPK = (4, 256, 128, 512, 8, 2)

        def _moe_forward(x, W_router, W_gate, W_up, W_down):
            logits = jnp.einsum('bsd,ed->bse', x, W_router)
            probs = jax.nn.softmax(logits, axis=-1)
            gates, indices = jax.lax.top_k(probs, TOPK)
            gates = gates / jnp.sum(gates, axis=-1, keepdims=True)
            weights = jnp.sum(gates[..., None] * jax.nn.one_hot(indices, E, dtype=x.dtype), axis=-2)
            weights_e = jnp.moveaxis(weights, -1, 0)

            def body(acc, params):
                wg, wu, wd, wt = params
                gate = jax.nn.silu(jnp.einsum('bsd,fd->bsf', x, wg))
                up = jnp.einsum('bsd,fd->bsf', x, wu)
                y = jnp.einsum('bsf,df->bsd', gate * up, wd)
                return (acc + wt[..., None] * y, None)
            out, _ = jax.lax.scan(body, jnp.zeros_like(x), (W_gate, W_up, W_down, weights_e))
            return out
        return _moe_forward(x, W_router, W_gate, W_up, W_down)

    def _L1_cond_ref(x, ada_emb, base_layer, w1, b1, w2, b2, ln_g, ln_b):
        import jax, jax.numpy as jnp
        import numpy as np
        B, T, D = (128, 32, 128)
        ADA, INTER, RANK = (128, 128, 8)
        LN_EPS = 1e-05

        def _layernorm(x, g, b):
            mu = jnp.mean(x, axis=-1, keepdims=True)
            var = jnp.var(x, axis=-1, keepdims=True)
            return (x - mu) * jax.lax.rsqrt(var + LN_EPS) * g + b
        b, t, d = x.shape
        ae = _layernorm(ada_emb, ln_g, ln_b)
        h = jax.nn.gelu(ae @ w1 + b1, approximate=False)
        xw = h @ w2 + b2
        x_a, x_b = jnp.split(xw, 2, axis=-1)
        x_a = x_a.reshape(b, d, RANK)
        x_b = x_b.reshape(b, d, RANK)
        layer = base_layer[None, :, :] + jnp.einsum('bdr,bkr->bdk', x_a, x_b)
        out = jnp.einsum('btc,bco->bto', x, layer)
        return x + out

    def _L1_ffn_ref(x, w1, b1, w2, b2):
        import jax, jax.numpy as jnp
        import numpy as np
        QP = 127.0
        MIN_RANGE = 1e-06

        def _ste_round(x):
            return x + jax.lax.stop_gradient(jnp.round(x) - x)

        def _quant_per_tensor(x):
            scale = jnp.maximum(jnp.max(jnp.abs(x)), MIN_RANGE) / QP
            return (_ste_round(x / scale), scale)

        def _qlinear(x2d, w, b):
            xq, sx = _quant_per_tensor(x2d)
            wq, sw = _quant_per_tensor(w)
            out = jnp.matmul(xq, wq.T) + b[None, :]
            return out * (sw * sx)
        B, N, D = x.shape
        h = _qlinear(x.reshape(-1, D), w1, b1)
        h = jax.nn.gelu(h, approximate=False)
        o = _qlinear(h, w2, b2)
        return o.reshape(B, N, -1)
    x = x + _L0_ffn_ref(_L0_cond_ref(x, cond_1024, L0_cond_W_in, L0_cond_b_in, L0_cond_Wih0, L0_cond_Whh0, L0_cond_bih0, L0_cond_bhh0, L0_cond_Wih1, L0_cond_Whh1, L0_cond_bih1, L0_cond_bhh1, L0_cond_W_out, L0_cond_b_out, L0_cond_W_gate, L0_cond_b_gate), L0_ffn_W_router, L0_ffn_W_gate, L0_ffn_W_up, L0_ffn_W_down)
    x = x + _L1_ffn_ref(_L1_cond_ref(x, cond_1024, L1_cond_base_layer, L1_cond_w1, L1_cond_b1, L1_cond_w2, L1_cond_b2, L1_cond_ln_g, L1_cond_ln_b), L1_ffn_w1, L1_ffn_b1, L1_ffn_w2, L1_ffn_b2)
    return x

_drawn_inputs = setup_inputs


def setup_inputs(seed=0):
    import zlib

    import numpy as np

    out = dict(_drawn_inputs(seed))
    spreads = {'L1_cond_b1': (0.0, 0.624),
     'L1_cond_b2': (0.0, 0.33),
     'L1_cond_ln_g': (1.0, 0.6),
     'L1_cond_ln_b': (0.0, 0.8)}
    factors = {'cond_1024': 3.395,
     'L0_cond_W_in': 5.452,
     'L0_cond_b_in': 8.0,
     'L0_cond_Wih0': 3.822,
     'L0_cond_Whh0': 5.549,
     'L0_cond_bih0': 5.606,
     'L0_cond_bhh0': 8.0,
     'L0_cond_Wih1': 3.863,
     'L0_cond_Whh1': 5.246,
     'L0_cond_bih1': 5.718,
     'L0_cond_bhh1': 6.043,
     'L0_cond_W_out': 3.805,
     'L0_cond_b_out': 4.863,
     'L0_cond_W_gate': 7.367,
     'L0_cond_b_gate': 8.0,
     'L0_ffn_W_router': 4.097,
     'L0_ffn_W_gate': 3.899,
     'L0_ffn_W_up': 3.747,
     'L0_ffn_W_down': 3.898,
     'L1_cond_w1': 4.635,
     'L1_cond_w2': 4.45,
     'L1_ffn_b1': 8.0,
     'L1_ffn_b2': 8.0}
    for name, (base, spread) in spreads.items():
        noise = np.random.default_rng([zlib.crc32(name.encode()), seed]).standard_normal(out[name].shape)
        drawn = base * np.exp(spread * noise) if base else spread * noise
        out[name] = jnp.asarray(drawn.astype(out[name].dtype))
    for name, factor in factors.items():
        out[name] = (out[name] * factor).astype(out[name].dtype)
    return out
```

```python
from contextlib import ExitStack

import concourse.bass as bass
from concourse import mybir

ALU = mybir.AluOpType
ACT = mybir.ActivationFunctionType
F32 = mybir.dt.float32
F16 = mybir.dt.float16
BF16 = mybir.dt.bfloat16
AX_X = mybir.AxisListType.X

B = 8
T = 128
D = 128
E = 8
F = 512
FB = F // D
R = 8
STEPS = 16
TOK = STEPS * B
CHUNKS = T // STEPS
N = T * B
LAG = 4
START = 6
PIECE = 256

W_SCALE = 2.0 ** 12
H_SCALE = 2.0 ** 14
GRU_UNSCALE = 1.0 / (W_SCALE * H_SCALE)
EW_SCALE = 2.0 ** 10
O_SCALE = 2.0 ** 8
MOE_UNSCALE = 1.0 / (EW_SCALE * O_SCALE)
ROUND = 1.5 * 2.0 ** 23
EPS = 1e-5
MIN_RANGE = 1e-6
QP = 127.0

V_BIN, V_BGATE, V_BOUT, V_LNG, V_LNB, V_CB1, V_B1, V_CB2 = 0, 1, 2, 3, 4, 5, 6, 10
VECS = 26
R_, Z_, N_ = 0, 1, 2
IH, HH = 0, 1


def wait_count(eng, semaphore, count):
    if not isinstance(count, int) or count > 0:
        eng.wait_ge(semaphore, count)


def expert_of(c, s):
    k = (s - START) % 16
    return (c - 1 if s >= START else c - 2), k // 2, k % 2


def is_chunk(c):
    return not isinstance(c, int) or 0 <= c < CHUNKS


def has_l1(c, s):
    return not isinstance(c, int) or 0 <= c * STEPS + s - LAG < T


def misc_before(c):
    return CHUNKS + (3 * c - 4 if c > 1 else 0) if isinstance(c, int) else c * 3 + (CHUNKS + 2 - 6)


def pieces_of(c, s):
    k = c * STEPS + s - 4
    return range(2 * k, 2 * k + 2) if 0 <= k < E * 2 * F // PIECE // 2 else ()


COND_PE = {0: {4: (0,), 5: (1,)}, CHUNKS: {8: (2,), 10: (3,), 12: (4,), 13: (5,)}}
COND_DVE = {0: {2: (0,), 3: (1,), 4: (2,), 5: (3,)}, CHUNKS: {9: (4,), 11: (5,), 13: (6, 7), 14: (8, 9)}}
COND_GELU = 7
QUANT_DVE = {0: 0, 2: 1, 3: 2, 4: 3, 5: 4, 6: 5}


def build(nc, xT, x_tok, first, gru0, gru1, proj, gate_up, down, cond_rows, biases, cond_w2, ffn, out):
    with ExitStack() as ctx:
        def sb(name, shape, dt=F32):
            return ctx.enter_context(nc.sbuf_tensor(name, shape, dt))

        def bank(name):
            return ctx.enter_context(nc.psum_tensor(name, [D, 512], F32))

        def sem(name):
            return ctx.enter_context(nc.semaphore(name))

        first_sb = sb("first_sb", [D, D + B + VECS])
        w_in = first_sb[:, 0:D]
        condT = first_sb[:, D:D + B]

        def vec(k, n=1):
            return first_sb[:, D + B + k:D + B + k + n]

        xT_sb = sb("xT_sb", [D, N])
        x1_tok = sb("x1_tok", [D, CHUNKS, D])
        gru_f = [sb(f"gru_f{i}", [D, 2, 3 * D]) for i in range(2)]
        proj_sb = sb("proj_sb", [D, 4 * D + E])
        w_gate, w_out, c_w1, base = (proj_sb[:, k * D:(k + 1) * D] for k in range(4))
        w_router = proj_sb[:, 4 * D:4 * D + E]
        gu_f = sb("gu_f", [D, E, 2 * F])
        down_f = sb("down_f", [D, E, FB, D])
        cond_sb = sb("cond_sb", [B, D])
        bias_raw = sb("bias_raw", [D, 2, 2, 3 * D])
        c_w2 = sb("c_w2", [D, 2 * R, D])
        ffn_sb = sb("ffn_sb", [D, 2 * F + D])
        ffn_b2 = ffn_sb[:, 2 * F:2 * F + D]

        ones_bf = sb("ones_bf", [D, TOK], BF16)
        ones_f = sb("ones_f", [1, D])
        ident = sb("ident", [D, D])
        batch_mask = sb("batch_mask", [B * R, B])
        expert_no = sb("expert_no", [D, E])
        expert_no_i = sb("expert_no_i", [D, E], mybir.dt.int32)
        pow_half = sb("pow_half", [B, 1])
        warm = sb("warm", [D, 1])

        gru_hi = [sb(f"gru_hi{i}", [D, 2, 3 * D], F16) for i in range(2)]
        gru_lo = [sb(f"gru_lo{i}", [D, 2, 3 * D], F16) for i in range(2)]
        bias_f = [sb(f"bias_f{i}", [D, 4 * D]) for i in range(2)]
        bias_p1 = [sb(f"bias_p1{i}", [D, 4 * D], BF16) for i in range(2)]
        bias_r1 = [sb(f"bias_r1{i}", [D, 4 * D]) for i in range(2)]
        bias_p2 = [sb(f"bias_p2{i}", [D, 4 * D], BF16) for i in range(2)]
        bias3 = [sb(f"bias3{i}", [D, 4 * D], BF16) for i in range(2)]
        mix_sum = sb("mix_sum", [D, TOK])
        mix = sb("mix", [D, TOK])
        mix_hi = sb("mix_hi", [D, N], F16)
        mix_lo = sb("mix_lo", [D, N], F16)
        factors = [sb(f"factors{i}", [D, 48]) for i in range(2)]
        pre = [sb(f"pre{i}", [D, 24]) for i in range(2)]
        state = [sb(f"state{i}", [D, 2, 24]) for i in range(2)]
        parts = [sb("parts0", [D, 8, 24], F16), sb("parts1", [D, 2, 24], F16)]
        gated = sb("gated", [D, STEPS, B])
        cond_gate = sb("cond_gate", [D, B])
        gain = sb("gain", [D, B])

        gu_hi = sb("gu_hi", [D, E, 2 * F], F16)
        gu_lo = sb("gu_lo", [D, E, 2 * F], F16)
        oT = sb("oT", [D, TOK])
        o_hi = sb("o_hi", [D, N], F16)
        o_lo = sb("o_lo", [D, N], F16)
        logits = sb("logits", [D, E])
        top8 = sb("top8", [D, 8])
        top8_at = sb("top8_at", [D, 8], mybir.dt.uint32)
        top8_no = sb("top8_no", [D, 8])
        top_gap = sb("top_gap", [D, 1])
        top_w = sb("top_w", [D, 2])
        share = sb("share", [D, 2, E])
        shares = sb("shares", [D, E])
        sig = sb("sig", [D, F])
        gate_c = sb("gate_c", [D, F])
        silu = sb("silu", [D, F])
        hidden = sb("hidden", [D, 2, F])
        acc = sb("acc", [D, D])
        x1T = sb("x1T", [D, N])

        ln_sum = sb("ln_sum", [B, 1])
        ln_x = sb("ln_x", [B, D])
        ln_sq = sb("ln_sq", [B, D])
        ln_var = sb("ln_var", [B, 1])
        ln_rstd = sb("ln_rstd", [B, 1])
        ae = sb("ae", [D, B])
        cv = sb("cv", [D, B])
        ch = sb("ch", [D, B])
        ab = sb("ab", [D, 2, B, R])
        a_T = sb("a_T", [B * R, D])
        b_T = sb("b_T", [B * R, B, D])
        layer = sb("layer", [D, B, D])

        w_max = sb("w_max", [D, 2])
        w_amax = sb("w_amax", [D, 2])
        w_step = sb("w_step", [D, 2])
        w_inv = sb("w_inv", [D, 2])
        w_round = sb("w_round", [D, 2, F])
        w_q = sb("w_q", [D, 2, F], BF16)
        yT = sb("yT", [D, N])
        y_q = sb("y_q", [D, N], BF16)
        ffn_h = gu_f[:, 0:FB, :]
        q_round = gu_f[:, FB:2 * FB, :]
        ffn_q = sb("ffn_q", [D, FB, N], BF16)
        part_max = sb("part_max", [D, 2 * FB])
        part_top = sb("part_top", [D, 2])
        row_top = sb("row_top", [1, 2])
        q_step = sb("q_step", [D, 2])
        q_inv = sb("q_inv", [D, 2])
        out_step = sb("out_step", [D, 2])
        gelu_bias = sb("gelu_bias", [D, FB])
        o_sb = sb("o_sb", [D, CHUNKS, D])

        p_rz = [bank("p_rz0"), bank("p_rz1")]
        p_n = [bank("p_n0"), bank("p_n1")]
        p_gate, p_up, p_y, p_misc = bank("p_gate"), bank("p_up"), bank("p_y"), bank("p_misc")

        ffn1_banks = [p_rz[0], p_n[0], p_rz[1], p_n[1]]

        got = {k: sem(f"got_{k}") for k in
               ("first", "x0", "x", "gru0", "gru1", "proj", "cond", "c_w2", "ffn", "x_tok", "bias", "down")}
        got_gu = [sem(f"got_gu{e}") for e in range(E)]
        bias_cleared = sem("bias_cleared")
        const_ready = sem("const_ready")
        iota_ready = sem("iota_ready")
        split_hi = sem("split_hi")
        split_lo = sem("split_lo")
        bias_step = [sem("bias_step0"), sem("bias_step1")]
        cleared = sem("cleared")
        init_done = sem("init_done")
        gate_done = sem("gate_done")
        gain_ready = sem("gain_ready")
        misc_written = sem("misc_written")
        misc_taken = sem("misc_taken")
        mix_done = sem("mix_done")
        mix_hi_ready = sem("mix_hi_ready")
        mix_ready = sem("mix_ready")
        rz_ready = [sem("rz_ready0"), sem("rz_ready1")]
        nsum_ready = [sem("nsum_ready0"), sem("nsum_ready1")]
        gates_ready = [sem("gates_ready0"), sem("gates_ready1")]
        pre_ready = [sem("pre_ready0"), sem("pre_ready1")]
        cand_ready = [sem("cand_ready0"), sem("cand_ready1")]
        neg_ready = [sem("neg_ready0"), sem("neg_ready1")]
        hi_ready = [sem("hi_ready0"), sem("hi_ready1")]
        state_ready = [sem("state_ready0"), sem("state_ready1")]
        lo_ready = [sem("lo_ready0"), sem("lo_ready1")]
        gated_ready = sem("gated_ready")
        o_projected = sem("o_projected")
        o_hi_ready = sem("o_hi_ready")
        o_lo_ready = sem("o_lo_ready")
        logits_ready = sem("logits_ready")
        router_step = sem("router_step")
        gap_ready = sem("gap_ready")
        top_w_ready = sem("top_w_ready")
        gu_hi_ready = sem("gu_hi_ready")
        gu_lo_ready = sem("gu_lo_ready")
        gate_ready = sem("gate_ready")
        up_ready = sem("up_ready")
        gate_read = sem("gate_read")
        silu_ready = sem("silu_ready")
        hidden_ready = sem("hidden_ready")
        y_ready = sem("y_ready")
        acc_ready = sem("acc_ready")
        x1_transposed = sem("x1_transposed")
        x1_kept = sem("x1_kept")
        c_dve = sem("c_dve")
        c_pe = sem("c_pe")
        c_act = sem("c_act")
        c_pool = sem("c_pool")
        wq_dve = sem("wq_dve")
        wq_pool = sem("wq_pool")
        layer_applied = sem("layer_applied")
        y_added = sem("y_added")
        part_max_ready = sem("part_max_ready")
        max_turned = sem("max_turned")
        row_max_ready = sem("row_max_ready")
        max_spread = sem("max_spread")
        step_ready = sem("step_ready")
        y_rounded = sem("y_rounded")
        y_q_ready = sem("y_q_ready")
        gelu_bias_ready = sem("gelu_bias_ready")
        ffn1_ready = sem("ffn1_ready")
        gelu_ready = sem("gelu_ready")
        tile_max_ready = sem("tile_max_ready")
        h_rounded_act = sem("h_rounded_act")
        h_rounded_dve = sem("h_rounded_dve")
        ffn_q_ready = sem("ffn_q_ready")
        ffn2_ready = sem("ffn2_ready")
        out_biased = sem("out_biased")
        out_ready = sem("out_ready")
        out_stored = sem("out_stored")

        block = ctx.enter_context(nc.Block())

        @block.sync
        def _(sp):
            sp.dma_start(first_sb[:, :], first).then_inc(got["first"], 16)
            sp.dma_start(xT_sb[:, 0:TOK], xT[:, 0:TOK]).then_inc(got["x0"], 16)
            sp.dma_start(gru_f[0][:, :, :], gru0).then_inc(got["gru0"], 16)
            sp.wait_ge(bias_cleared, 1)
            for p in (0, 32, 64):
                sp.dma_start(bias_raw[p:p + 1, :, :, :], biases).then_inc(got["bias"], 16)
            sp.dma_start(gru_f[1][:, :, :], gru1).then_inc(got["gru1"], 16)
            sp.dma_start(xT_sb[:, TOK:N], xT[:, TOK:N]).then_inc(got["x"], 16)
            sp.dma_start(proj_sb[:, :], proj).then_inc(got["proj"], 16)
            sp.dma_start(cond_sb[:, :], cond_rows).then_inc(got["cond"], 16)
            sp.dma_start(c_w2[:, :, :], cond_w2).then_inc(got["c_w2"], 16)
            for e in range(2):
                sp.dma_start(gu_f[:, e, :], gate_up[:, e, :]).then_inc(got_gu[e], 16)
            sp.dma_start(ffn_sb[:, :], ffn).then_inc(got["ffn"], 16)
            for e in range(2, E):
                sp.dma_start(gu_f[:, e, :], gate_up[:, e, :]).then_inc(got_gu[e], 16)
            sp.dma_start(down_f[:, :, :, :], down).then_inc(got["down"], 16)
            sp.dma_start(x1_tok[:, :, :], x_tok).then_inc(got["x_tok"], 16)
            for k in range(2):
                half = slice((1 - k) * CHUNKS // 2, (2 - k) * CHUNKS // 2)
                sp.wait_ge(out_ready, k + 1)
                sp.dma_start(out[:, half, :], o_sb[:, half, :]).then_inc(out_stored, 16)
            sp.wait_ge(out_stored, 32)

        @block.tensor
        def _(pe):
            def prefill(layer_no, n_tok, moving_hi, moving_lo):
                rz, nn = p_rz[layer_no], p_n[layer_no]
                steps = n_tok // B
                hi, lo, b3 = gru_hi[layer_no], gru_lo[layer_no], bias3[layer_no]
                for g in (R_, Z_, N_):
                    if g == N_:
                        dst = nn[:, 2:24 * steps:3]
                    else:
                        dst = rz[:, 0:16 * steps].rearrange("p (t k) -> p t k", k=16)[:, :, 8 * g:8 * g + 8]
                    pe.matmul(dst, b3[:, g * D:(g + 1) * D], ones_bf[:, 0:n_tok],
                              start=g in (R_, N_), stop=False, skip_group_check=True)
                    w = slice(g * D, (g + 1) * D)
                    pe.matmul(dst, hi[:, IH, w], moving_hi, start=False, stop=False, skip_group_check=True)
                    pe.matmul(dst, lo[:, IH, w], moving_hi, start=False, stop=False, skip_group_check=True)
                    pe.matmul(dst, hi[:, IH, w], moving_lo, start=False, stop=False, skip_group_check=True)
                pe.matmul(nn[:, 0:24 * steps:3], b3[:, 3 * D:4 * D], ones_bf[:, 0:n_tok],
                          start=False, stop=False, skip_group_check=True)

            def step(layer_no, count, ring, at):
                hi, lo = gru_hi[layer_no], gru_lo[layer_no]
                rz, nn, h = p_rz[layer_no], p_n[layer_no], parts[layer_no]
                h_hi, h_lo, h_both = h[:, ring, 2:24:3], h[:, ring, 1:24:3], \
                    h[:, ring, :].rearrange("p (b k) -> p b k", k=3)[:, :, 1:3]
                wait_count(pe, hi_ready[layer_no], count)
                for g in (R_, Z_):
                    dst = rz[:, 16 * at + 8 * g:16 * at + 8 * g + 8]
                    for w in (hi, lo):
                        pe.matmul(dst, w[:, HH, g * D:(g + 1) * D], h_hi,
                                  start=False, stop=False, skip_group_check=True)
                pe.matmul(nn[:, 24 * at:24 * at + 24:3], lo[:, HH, 2 * D:3 * D], h_hi,
                          start=False, stop=False, skip_group_check=True)
                wait_count(pe, lo_ready[layer_no], count)
                for g in (R_, Z_):
                    dst = rz[:, 16 * at + 8 * g:16 * at + 8 * g + 8]
                    last = pe.matmul(dst, hi[:, HH, g * D:(g + 1) * D], h_lo,
                                     start=False, stop=False, skip_group_check=True)
                last.then_inc(rz_ready[layer_no], 1)
                both = nn[:, 24 * at:24 * at + 24].rearrange("p (b k) -> p b k", k=3)[:, :, 0:2]
                pe.matmul(both, hi[:, HH, 2 * D:3 * D], h_both,
                          start=False, stop=False, skip_group_check=True).then_inc(nsum_ready[layer_no], 1)

            def mixed(k):
                wait_count(pe, misc_taken, k)
                pe.matmul(p_misc[:, 0:TOK], w_in, xT_sb[:, k * TOK:(k + 1) * TOK],
                          start=True, stop=True).then_inc(misc_written, 1)

            def gate_or_up(which, chunk, e, blocks, done):
                bank_, ready = (p_gate, gate_ready) if which == 0 else (p_up, up_ready)
                x_hi, x_lo = o_hi[:, bass.ds(chunk * TOK, TOK)], o_lo[:, bass.ds(chunk * TOK, TOK)]
                for f in blocks:
                    w = slice(which * F + f * D, which * F + (f + 1) * D)
                    dst = bank_[:, f * D:(f + 1) * D]
                    pe.matmul(dst, gu_hi[:, e, w], x_hi, start=True, stop=False)
                    pe.matmul(dst, gu_lo[:, e, w], x_hi, start=False, stop=False)
                    last = pe.matmul(dst, gu_hi[:, e, w], x_lo, start=False, stop=True)
                if done:
                    last.then_inc(ready, 1)

            def gate(c, s):
                chunk, e, _ = expert_of(c, s)
                if is_chunk(chunk):
                    j = chunk * E + e
                    if e == 0:
                        pe.wait_ge(o_lo_ready, chunk + 1)
                    if isinstance(chunk, int) and chunk == 0:
                        pe.wait_ge(gu_lo_ready, 4 * (e + 1))
                    wait_count(pe, gate_read, 2 * j)
                    gate_or_up(0, chunk, e, range(FB), True)

            def up(c, s, blocks):
                chunk, e, _ = expert_of(c, s)
                if is_chunk(chunk):
                    if blocks[0] == 0:
                        wait_count(pe, hidden_ready, 2 * (chunk * E + e))
                    gate_or_up(1, chunk, e, blocks, blocks[-1] == FB - 1)

            def down_proj(c, s, blocks):
                chunk, e, _ = expert_of(c, s)
                chunk, e = (chunk, e - 1) if e else (chunk - 1, E - 1)
                if is_chunk(chunk):
                    j = chunk * E + e
                    pe.wait_ge(hidden_ready, 2 * j + 1 + blocks[0] // 2)
                    if blocks[0] == 0:
                        wait_count(pe, acc_ready, j)
                        if isinstance(chunk, int) and chunk == 0 and e == 0:
                            pe.wait_ge(got["down"], 16)
                    for f in blocks:
                        last = pe.matmul(p_y[:, 0:D], hidden[:, e % 2, f * D:(f + 1) * D], down_f[:, e, f, :],
                                         start=f == 0, stop=f == FB - 1)
                    if blocks[-1] == FB - 1:
                        last.then_inc(y_ready, 1)

            def cond_step(n):
                if n == 0:
                    pe.wait_ge(c_dve, 7)
                    pe.transpose(p_gate[:, 0:B], ln_x[:, :], ident[0:B, 0:B]).then_inc(c_pe, 1)
                elif n == 1:
                    pe.wait_ge(c_dve, 8)
                    pe.matmul(p_gate[:, 0:B], c_w1, ae[:, :], start=True, stop=True).then_inc(c_pe, 1)
                elif n == 2:
                    pe.wait_ge(c_act, 1)
                    pe.wait_ge(got["c_w2"], 16)
                    pe.wait_ge(hi_ready[0], T)
                    for k in range(2 * R):
                        at = (k // R) * B * R + k % R
                        last = pe.matmul(p_rz[0][:, at:at + B * R - R + 1:R], c_w2[:, k, :], ch[:, :],
                                         start=True, stop=True)
                    last.then_inc(c_pe, 1)
                elif n == 3:
                    pe.wait_ge(c_dve, 11)
                    for k in range(2):
                        last = pe.transpose(p_n[0][0:B * R, k * D:(k + 1) * D],
                                            ab[:, k, :, :].rearrange("p b r -> p (b r)"), ident[:, :])
                    last.then_inc(c_pe, 1)
                else:
                    half = n - 4
                    pe.wait_ge(c_dve, 13 + half)
                    bank_ = (p_rz[0], p_n[0])[half]
                    for b in range(4):
                        last = pe.matmul(bank_[:, b * D:(b + 1) * D], a_T[:, :], b_T[:, 4 * half + b, :],
                                         start=True, stop=True)
                    last.then_inc(c_pe, 1)

            def slot(c, s):
                if is_chunk(c):
                    if s == 0:
                        if isinstance(c, int):
                            pe.wait_ge(mix_ready, c + 1)
                        wait_count(pe, hi_ready[0], c * STEPS)
                        prefill(0, TOK, mix_hi[:, bass.ds(c * TOK, TOK)], mix_lo[:, bass.ds(c * TOK, TOK)])
                    step(0, c * STEPS + s, (s + 7) % 8, s)
                if isinstance(c, int) and c == 0:
                    if s == 1:
                        pe.wait_ge(got["x"], 16)
                        pe.wait_ge(got["proj"], 16)
                        pe.matmul(p_y[:, 0:B], w_gate, condT, start=True, stop=True).then_inc(gate_done, 1)
                    if 1 <= s < CHUNKS:
                        mixed(s)
                if s == START + 2 and is_chunk(c - 2):
                    pe.wait_ge(acc_ready, (c - 1) * E)
                    pe.wait_ge(misc_taken, misc_before(c) + (2 if is_chunk(c - 1) else 0))
                    pe.transpose(p_misc[:, 0:D], acc[:, :], ident[:, :]).then_inc(x1_transposed, 1)
                if s == LAG and is_chunk(c - 1):
                    pe.wait_ge(gated_ready, c * STEPS)
                    pe.wait_ge(misc_taken, misc_before(c))
                    pe.matmul(p_misc[:, 0:TOK], w_out, gated[:, :, :].rearrange("p t b -> p (t b)"),
                              start=True, stop=True).then_inc(o_projected, 1)
                if s == START and is_chunk(c - 1):
                    pe.wait_ge(misc_taken, misc_before(c) + 1)
                    pe.matmul(p_misc[:, 0:E], oT[:, :], w_router, start=True, stop=True)\
                        .then_inc(logits_ready, 1)
                half = expert_of(c, s)[2]
                if half == 0:
                    gate(c, s)
                else:
                    down_proj(c, s, (2, 3))
                    up(c, s, (0,))
                if has_l1(c, s):
                    if s % LAG == 0:
                        g = s // LAG % 2
                        group = slice(4 * (1 - g), 4 * (1 - g) + 4)
                        if isinstance(c, int) and c * STEPS + s == LAG:
                            pe.wait_ge(split_lo, 4)
                            pe.wait_ge(bias_step[1], 10)
                        pe.wait_ge(lo_ready[0], c * STEPS + s)
                        wait_count(pe, hi_ready[1], c * STEPS + s - LAG)
                        h = parts[0][:, group, :].rearrange("p t k -> p (t k)")
                        prefill(1, LAG * B, h[:, 2:96:3], h[:, 1:96:3])
                    step(1, c * STEPS + s - LAG, s % 2, s % LAG)
                if half == 0:
                    down_proj(c, s, (0, 1))
                else:
                    up(c, s, (1, 2, 3))
                if isinstance(c, int):
                    for n in COND_PE.get(c, {}).get(s, ()):
                        cond_step(n)

            pe.wait_ge(got["first"], 16)
            pe.wait_ge(got["x0"], 16)
            mixed(0)
            pe.wait_ge(iota_ready, 1)
            pe.wait_ge(init_done, 1)
            pe.wait_ge(split_lo, 2)
            pe.wait_ge(bias_step[0], 10)
            for s in range(16):
                slot(0, s)
            for s in range(16):
                slot(1, s)
            with pe.Fori(2, CHUNKS) as c:
                for s in range(16):
                    slot(c, s)
            for s in range(16):
                slot(CHUNKS, s)
            for s in range(START + 3):
                slot(CHUNKS + 1, s)

            pe.wait_ge(misc_taken, misc_before(CHUNKS + 1) + 1)
            pe.wait_ge(c_dve, 18)
            for b in range(B):
                last = pe.matmul((p_gate, p_up)[b // 4][:, b % 4 * T:(b % 4 + 1) * T], layer[:, b, :],
                                 x1T[:, b:N:B], start=True, stop=True)
                if b % 4 == 3:
                    last.then_inc(layer_applied, 1)

            def all_max(k):
                pe.wait_ge(part_max_ready, k + 1)
                pe.transpose(p_y[0:1, 0:D], part_top[:, k:k + 1], ident[:, :]).then_inc(max_turned, 1)
                pe.wait_ge(row_max_ready, k + 1)
                pe.matmul(p_y[:, 256:257], ones_f[:, :], row_top[:, k:k + 1], start=True, stop=True)\
                    .then_inc(max_spread, 1)

            all_max(0)
            for h in range(2):
                pe.wait_ge(y_q_ready, h + 1)
                for f in range(FB):
                    if h:
                        pe.wait_ge(gelu_ready, f + 1)
                    pe.matmul(ffn1_banks[f][:, :], w_q[:, 0, f * D:(f + 1) * D], y_q[:, h * F:(h + 1) * F],
                              start=True, stop=True).then_inc(ffn1_ready, 1)
            all_max(1)
            for k in (4, 5, 6, 7, 0, 1, 2, 3):
                pe.wait_ge(ffn_q_ready, 1 if k >= CHUNKS // 2 else 2)
                for f in range(FB):
                    last = pe.matmul((p_gate, p_up)[k // 4][:, k % 4 * D:(k % 4 + 1) * D],
                                     ffn_q[:, f, k * TOK:(k + 1) * TOK], w_q[:, 1, f * D:(f + 1) * D],
                                     start=f == 0, stop=f == FB - 1)
                if k % 4 == 3:
                    last.then_inc(ffn2_ready, 1)

        @block.scalar
        def _(act):
            def gru(layer_no, count, buf, at):
                rz = p_rz[layer_no]
                fa = factors[layer_no]
                act.wait_ge(rz_ready[layer_no], count + 1)
                act.activation(fa[:, :].rearrange("p (g b k) -> p g b k", g=2, k=3)[:, :, :, 2],
                               rz[:, 16 * at:16 * at + 16].rearrange("p (g b) -> p g b", g=2),
                               ACT.Sigmoid, scale=GRU_UNSCALE).then_inc(gates_ready[layer_no], 1)
                act.wait_ge(pre_ready[layer_no], count + 1)
                act.activation(state[layer_no][:, buf, 0:24:3], pre[layer_no][:, 2:24:3], ACT.Tanh,
                               scale=GRU_UNSCALE).then_inc(cand_ready[layer_no], 1)

            def negate(layer_no, count, buf):
                wait_count(act, state_ready[layer_no], count)
                act.activation(state[layer_no][:, buf, 1:24:3], state[layer_no][:, buf, 2:24:3], ACT.Copy,
                               scale=-1.0).then_inc(neg_ready[layer_no], 1)

            def mixed(k):
                act.wait_ge(misc_taken, k + 1)
                wait_count(act, mix_ready, k)
                act.activation(mix[:, :], mix_sum[:, :], ACT.Tanh, bias=vec(V_BIN)).then_inc(mix_done, 1)
                act.wait_ge(mix_done, k + 1)
                act.activation(mix_hi[:, k * TOK:(k + 1) * TOK], mix[:, :], ACT.Copy,
                               scale=H_SCALE).then_inc(mix_hi_ready, 1)

            def split_weights(layer_no, kind):
                for cols, sign in (((0, D), 1.0), ((D, 2 * D), -1.0), ((2 * D, 3 * D), 1.0)):
                    last = act.activation(gru_hi[layer_no][:, kind, cols[0]:cols[1]],
                                          gru_f[layer_no][:, kind, cols[0]:cols[1]], ACT.Copy,
                                          scale=sign * W_SCALE)
                last.then_inc(split_hi, 1)

            def split_expert(piece):
                e, q = piece // 4, piece % 4
                if q == 0:
                    act.wait_ge(got_gu[e], 16)
                act.activation(gu_hi[:, e, q * 256:(q + 1) * 256], gu_f[:, e, q * 256:(q + 1) * 256], ACT.Copy,
                               scale=EW_SCALE).then_inc(gu_hi_ready, 1)

            def out_of_gate(c, s, part):
                chunk, e, _ = expert_of(c, s)
                if is_chunk(chunk):
                    j = chunk * E + e
                    half = part // 2
                    cols = slice(half * 256, half * 256 + 256)
                    if part == 0:
                        act.wait_ge(gate_ready, j + 1)
                    if part % 2 == 0:
                        wait_count(act, silu_ready, 2 * (j - 1) + half + 1)
                        act.activation(sig[:, cols], p_gate[:, cols], ACT.Sigmoid, scale=MOE_UNSCALE)
                    else:
                        act.activation(gate_c[:, cols], p_gate[:, cols], ACT.Copy, scale=MOE_UNSCALE)\
                            .then_inc(gate_read, 1)

            def slot(c, s):
                if is_chunk(c):
                    gru(0, c * STEPS + s, s % 2, s)
                half = expert_of(c, s)[2]
                if half == 1:
                    out_of_gate(c, s, 2)
                if s == START + 2 and is_chunk(c - 2):
                    act.wait_ge(x1_transposed, c - 1)
                    act.activation(x1T[:, bass.ds((c - 2) * TOK, TOK)], p_misc[:, 0:TOK], ACT.Copy)\
                        .then_inc(misc_taken, 1)
                if s == LAG and is_chunk(c - 1):
                    act.wait_ge(o_projected, c)
                    if not (isinstance(c, int) and c == 1):
                        act.wait_ge(logits_ready, c - 1)
                        act.wait_ge(o_lo_ready, c - 1)
                    act.activation(oT[:, :], p_misc[:, 0:TOK], ACT.Identity, bias=vec(V_BOUT))\
                        .then_inc(misc_taken, 1)
                if s == LAG + 1 and is_chunk(c - 1):
                    act.wait_ge(misc_taken, misc_before(c) + 1)
                    act.activation(o_hi[:, bass.ds((c - 1) * TOK, TOK)], oT[:, :], ACT.Copy, scale=O_SCALE)\
                        .then_inc(o_hi_ready, 1)
                if s == START + 2 and is_chunk(c - 1):
                    act.wait_ge(gap_ready, c)
                    act.activation(top_w[:, 0:1], top_gap[:, :], ACT.Sigmoid, scale=-1.0)
                    act.activation(top_w[:, 1:2], top_gap[:, :], ACT.Sigmoid).then_inc(top_w_ready, 1)
                if is_chunk(c):
                    negate(0, c * STEPS + s + 1, (s + 1) % 2)
                if has_l1(c, s):
                    gru(1, c * STEPS + s - LAG, s % 2, s % LAG)
                if half == 0:
                    out_of_gate(c, s, 0)
                    out_of_gate(c, s, 1)
                else:
                    out_of_gate(c, s, 3)
                if isinstance(c, int) and c < 2:
                    if c == 0 and 1 <= s < CHUNKS:
                        mixed(s)
                    if c == 0 and s == 1:
                        act.wait_ge(got["gru1"], 16)
                        split_weights(1, IH)
                        split_weights(1, HH)
                        act.wait_ge(gate_done, 1)
                        act.activation(cond_gate[:, :], p_y[:, 0:B], ACT.Sigmoid, bias=vec(V_BGATE))\
                            .then_inc(gain_ready, 1)
                    for piece in pieces_of(c, s):
                        split_expert(piece)
                if has_l1(c, s):
                    negate(1, c * STEPS + s - LAG + 1, (s + 1) % 2)
                if isinstance(c, int) and c == CHUNKS and s == COND_GELU:
                    act.wait_ge(c_dve, 9)
                    act.activation(ch[:, :], cv[:, :], ACT.Gelu).then_inc(c_act, 1)

            act.wait_ge(const_ready, 1)
            act.activation(warm[:, :], warm[:, :], ACT.Sigmoid)
            act.wait_ge(init_done, 1)
            negate(0, 0, 0)
            negate(1, 0, 0)
            act.wait_ge(got["first"], 16)
            act.wait_ge(got["gru0"], 16)
            split_weights(0, IH)
            mixed(0)
            split_weights(0, HH)
            for s in range(16):
                slot(0, s)
            for s in range(16):
                slot(1, s)
            with act.Fori(2, CHUNKS) as c:
                for s in range(16):
                    slot(c, s)
            for s in range(16):
                slot(CHUNKS, s)
            for s in range(START + 3):
                slot(CHUNKS + 1, s)

            act.wait_ge(gelu_bias_ready, 1)
            for k in range(2 * FB):
                h, f = k // FB, k % FB
                act.wait_ge(ffn1_ready, k + 1)
                act.activation(ffn_h[:, f, h * F:(h + 1) * F], ffn1_banks[f][:, :], ACT.Gelu,
                               scale=out_step[:, 0:1], bias=gelu_bias[:, f:f + 1]).then_inc(gelu_ready, 1)
            act.wait_ge(step_ready, 4)
            for f in range(FB):
                act.activation(q_round[:, f, 0:F], ffn_h[:, f, 0:F], ACT.Copy,
                               scale=q_inv[:, 1:2], bias=ROUND).then_inc(h_rounded_act, 1)

        @block.vector
        def _(dve):
            def gru(layer_no, count, buf, ring, at):
                fa, st, pa = factors[layer_no], state[layer_no], parts[layer_no]
                dve.wait_ge(gates_ready[layer_no], count + 1)
                dve.wait_ge(nsum_ready[layer_no], count + 1)
                dve.tensor_tensor_scan(pre[layer_no][:, :], fa[:, 0:24], p_n[layer_no][:, 24 * at:24 * at + 24],
                                       0.0, ALU.mult, ALU.add).then_inc(pre_ready[layer_no], 1)
                dve.wait_ge(neg_ready[layer_no], count + 1)
                dve.wait_ge(cand_ready[layer_no], count + 1)
                dve.tensor_tensor_scan(pa[:, ring, :], fa[:, 24:48], st[:, buf, :], 0.0, ALU.mult, ALU.add)\
                    .then_inc(hi_ready[layer_no], 1)
                if layer_no == 1:
                    wait_count(dve, gated_ready, count - 1)
                dve.tensor_tensor_scan(st[:, 1 - buf, :], fa[:, 24:48], st[:, buf, :], 0.0, ALU.mult, ALU.add)\
                    .then_inc(state_ready[layer_no], 1)
                dve.wait_ge(state_ready[layer_no], count + 1)
                dve.tensor_tensor(pa[:, ring, 1:24:3], st[:, 1 - buf, 2:24:3], pa[:, ring, 2:24:3], ALU.subtract)\
                    .then_inc(lo_ready[layer_no], 1)

            def mixed(k):
                dve.wait_ge(misc_written, k + 1)
                wait_count(dve, mix_done, k)
                dve.tensor_tensor(mix_sum[:, :].rearrange("p (t b) -> p t b", b=B),
                                  p_misc[:, 0:TOK].rearrange("p (t b) -> p t b", b=B),
                                  condT.rearrange("p (a b) -> p a b", a=1).to_broadcast([D, STEPS, B]),
                                  ALU.add).then_inc(misc_taken, 1)

            def mixed_lo(k):
                dve.wait_ge(mix_hi_ready, k + 1)
                cols = slice(k * TOK, (k + 1) * TOK)
                dve.scalar_tensor_tensor(out=mix_lo[:, cols], in0=mix[:, :], scalar=H_SCALE,
                                         in1=mix_hi[:, cols], op0=ALU.mult, op1=ALU.subtract)\
                    .then_inc(mix_ready, 1)

            def split_weights(layer_no, kind, n):
                dve.wait_ge(split_hi, n)
                for cols, sign in (((0, D), 1.0), ((D, 2 * D), -1.0), ((2 * D, 3 * D), 1.0)):
                    at = slice(*cols)
                    last = dve.scalar_tensor_tensor(
                        out=gru_lo[layer_no][:, kind, at], in0=gru_f[layer_no][:, kind, at],
                        scalar=sign * W_SCALE, in1=gru_hi[layer_no][:, kind, at],
                        op0=ALU.mult, op1=ALU.subtract)
                last.then_inc(split_lo, 1)

            def split_expert(piece):
                e, q = piece // 4, piece % 4
                at = slice(q * 256, (q + 1) * 256)
                dve.wait_ge(gu_hi_ready, piece + 1)
                dve.scalar_tensor_tensor(out=gu_lo[:, e, at], in0=gu_f[:, e, at], scalar=EW_SCALE,
                                         in1=gu_hi[:, e, at], op0=ALU.mult, op1=ALU.subtract)\
                    .then_inc(gu_lo_ready, 1)

            def hidden_half(c, s, half):
                chunk, e, _ = expert_of(c, s)
                chunk, e = (chunk, e - 1) if e else (chunk - 1, E - 1)
                if is_chunk(chunk):
                    j = chunk * E + e
                    at = slice(half * 256, half * 256 + 256)
                    dve.wait_ge(up_ready, j + 1)
                    dve.wait_ge(silu_ready, 2 * j + half + 1)
                    dve.scalar_tensor_tensor(out=hidden[:, e % 2, at], in0=p_up[:, at], scalar=MOE_UNSCALE,
                                             in1=silu[:, at], op0=ALU.mult, op1=ALU.mult)\
                        .then_inc(hidden_ready, 1)

            def add_expert(c, s):
                chunk, e, _ = expert_of(c, s)
                chunk, e = (chunk, e - 1) if e else (chunk - 1, E - 1)
                if is_chunk(chunk):
                    j = chunk * E + e
                    dve.wait_ge(y_ready, j + 1)
                    if e == 0:
                        dve.wait_ge(router_step, 7 * (chunk + 1))
                        if isinstance(chunk, int) and chunk == 0:
                            dve.wait_ge(got["x_tok"], 16)
                        else:
                            dve.wait_ge(x1_transposed, chunk)
                            dve.wait_ge(x1_kept, chunk)
                        old = x1_tok[:, bass.ds(chunk, 1), :].rearrange("p a d -> p (a d)")
                    else:
                        dve.wait_ge(acc_ready, j)
                        old = acc[:, :]
                    dve.scalar_tensor_tensor(out=acc[:, :], in0=p_y[:, 0:D], scalar=shares[:, e:e + 1],
                                             in1=old, op0=ALU.mult, op1=ALU.add).then_inc(acc_ready, 1)

            def router(c, part):
                n = 7 * (c - 1)
                if part == 0:
                    dve.wait_ge(logits_ready, c)
                    dve.tensor_copy(logits[:, :], p_misc[:, 0:E]).then_inc(misc_taken, 1)
                elif part == 1:
                    if not is_chunk(c):
                        dve.wait_ge(misc_taken, misc_before(c) + 2)
                    dve.max(top8[:, :], logits[:, :]).then_inc(router_step, 1)
                    dve.wait_ge(router_step, n + 1)
                    dve.tensor_tensor(top_gap[:, :], top8[:, 1:2], top8[:, 0:1], ALU.subtract)\
                        .then_inc(gap_ready, 1)
                elif part == 2:
                    if not is_chunk(c):
                        dve.wait_ge(router_step, n + 1)
                    dve.max_index(top8_at[:, :], top8[:, :], logits[:, :]).then_inc(router_step, 1)
                    dve.wait_ge(router_step, n + 2)
                    dve.tensor_copy(top8_no[:, :], top8_at[:, :]).then_inc(router_step, 1)
                else:
                    dve.wait_ge(router_step, n + 3)
                    dve.wait_ge(top_w_ready, c)
                    for k in range(2):
                        dve.tensor_scalar(share[:, k, :], expert_no[:, :], top8_no[:, k:k + 1], top_w[:, k:k + 1],
                                          ALU.is_equal, ALU.mult).then_inc(router_step, 1)
                    dve.wait_ge(router_step, n + 5)
                    dve.tensor_tensor(shares[:, :], share[:, 0, :], share[:, 1, :], ALU.add)\
                        .then_inc(router_step, 2)

            def bias_parts(layer_no):
                b, raw = bias_f[layer_no], bias_raw
                done = bias_step[layer_no]
                sk = W_SCALE * H_SCALE
                dve.tensor_tensor(b[:, 0:2 * D], raw[:, layer_no, IH, 0:2 * D], raw[:, layer_no, HH, 0:2 * D],
                                  ALU.add).then_inc(done, 1)
                dve.tensor_scalar(b[:, 2 * D:3 * D], raw[:, layer_no, IH, 2 * D:3 * D], sk, None, ALU.mult)\
                    .then_inc(done, 1)
                dve.tensor_scalar(b[:, 3 * D:4 * D], raw[:, layer_no, HH, 2 * D:3 * D], sk, None, ALU.mult)\
                    .then_inc(done, 1)
                dve.wait_ge(done, 3)
                dve.tensor_scalar(b[:, 0:D], b[:, 0:D], sk, None, ALU.mult)
                dve.tensor_scalar(b[:, D:2 * D], b[:, D:2 * D], -sk, None, ALU.mult).then_inc(done, 1)
                dve.wait_ge(done, 4)
                dve.tensor_copy(bias_p1[layer_no][:, :], b[:, :]).then_inc(done, 1)
                dve.wait_ge(done, 5)
                dve.tensor_tensor(bias_r1[layer_no][:, :], b[:, :], bias_p1[layer_no][:, :], ALU.subtract)\
                    .then_inc(done, 1)
                dve.wait_ge(done, 6)
                dve.tensor_copy(bias_p2[layer_no][:, :], bias_r1[layer_no][:, :]).then_inc(done, 1)
                dve.wait_ge(done, 7)
                dve.tensor_copy(bias3[layer_no][0:1, :], bias_p1[layer_no][0:1, :]).then_inc(done, 1)
                dve.tensor_copy(bias3[layer_no][32:33, :], bias_p2[layer_no][32:33, :]).then_inc(done, 1)
                dve.tensor_tensor(bias3[layer_no][64:65, :], bias_r1[layer_no][64:65, :],
                                  bias_p2[layer_no][64:65, :], ALU.subtract).then_inc(done, 1)

            def cond_step(n):
                if n == 0:
                    dve.wait_ge(got["cond"], 16)
                    dve.tensor_reduce(ln_sum[:, :], cond_sb[:, :], AX_X, ALU.add).then_inc(c_dve, 1)
                    dve.wait_ge(c_dve, 1)
                    dve.tensor_scalar(ln_sum[:, :], ln_sum[:, :], 1.0 / D, None, ALU.mult).then_inc(c_dve, 1)
                    dve.wait_ge(c_dve, 2)
                    dve.tensor_scalar(ln_x[:, :], cond_sb[:, :], ln_sum[:, 0:1], None, ALU.subtract)\
                        .then_inc(c_dve, 1)
                    dve.wait_ge(c_dve, 3)
                    dve.tensor_tensor(ln_sq[:, :], ln_x[:, :], ln_x[:, :], ALU.mult).then_inc(c_dve, 1)
                    dve.wait_ge(c_dve, 4)
                    dve.tensor_reduce(ln_var[:, :], ln_sq[:, :], AX_X, ALU.add).then_inc(c_dve, 1)
                    dve.wait_ge(c_dve, 5)
                    dve.tensor_scalar(ln_var[:, :], ln_var[:, :], 1.0 / D, EPS, ALU.mult, ALU.add)\
                        .then_inc(c_dve, 1)
                elif n == 1:
                    dve.wait_ge(c_pool, 1)
                    dve.tensor_scalar(ln_x[:, :], ln_x[:, :], ln_rstd[:, 0:1], None, ALU.mult)\
                        .then_inc(c_dve, 1)
                elif n == 2:
                    dve.wait_ge(c_pe, 1)
                    dve.tensor_scalar(ae[:, :], p_gate[:, 0:B], vec(V_LNG), vec(V_LNB), ALU.mult, ALU.add)\
                        .then_inc(c_dve, 1)
                elif n == 3:
                    dve.wait_ge(c_pe, 2)
                    dve.tensor_scalar(cv[:, :], p_gate[:, 0:B], vec(V_CB1), None, ALU.add).then_inc(c_dve, 1)
                elif n == 4:
                    dve.wait_ge(c_pe, 3)
                    for k in range(2):
                        dve.tensor_tensor(ab[:, k, :, :],
                                          p_rz[0][:, k * B * R:(k + 1) * B * R].rearrange("p (b r) -> p b r", r=R),
                                          vec(V_CB2 + k * R, R).rearrange("p (a r) -> p a r", a=1)
                                          .to_broadcast([D, B, R]), ALU.add).then_inc(c_dve, 1)
                elif n == 5:
                    dve.wait_ge(c_pe, 4)
                    dve.wait_ge(iota_ready, 3)
                    dve.tensor_copy(a_T[:, :], p_n[0][0:B * R, 0:D]).then_inc(c_dve, 1)
                    for b in range(B):
                        last = dve.tensor_scalar(b_T[:, b, :], p_n[0][0:B * R, D:2 * D], batch_mask[:, b:b + 1],
                                                 None, ALU.mult)
                        if b % 4 == 3:
                            last.then_inc(c_dve, 1)
                else:
                    half, quarter = (n - 6) // 2, (n - 6) % 2
                    dve.wait_ge(c_pe, 5 + half)
                    bank_ = (p_rz[0], p_n[0])[half]
                    at = 4 * half + 2 * quarter
                    dve.tensor_tensor(layer[:, at:at + 2, :],
                                      bank_[:, quarter * 2 * D:(quarter + 1) * 2 * D]
                                      .rearrange("p (b o) -> p b o", b=2),
                                      base.rearrange("p (a o) -> p a o", a=1).to_broadcast([D, 2, D]),
                                      ALU.add).then_inc(c_dve, 1)

            def quant_weights(n):
                if n == 0:
                    dve.wait_ge(got["ffn"], 16)
                    for k in range(2):
                        dve.tensor_reduce(w_max[:, k:k + 1], ffn_sb[:, k * F:(k + 1) * F], AX_X, ALU.max,
                                          apply_absolute_value=True).then_inc(wq_dve, 1)
                elif n == 1:
                    dve.wait_ge(wq_pool, 1)
                    dve.tensor_scalar(w_step[:, :], w_amax[:, :], MIN_RANGE, 1.0 / QP, ALU.max, ALU.mult)\
                        .then_inc(wq_dve, 1)
                    dve.wait_ge(wq_dve, 3)
                    dve.reciprocal(w_inv[:, :], w_step[:, :]).then_inc(wq_dve, 1)
                    dve.wait_ge(wq_dve, 4)
                elif n < 4:
                    k = n - 2
                    dve.tensor_scalar(w_round[:, k, :], ffn_sb[:, k * F:(k + 1) * F], w_inv[:, k:k + 1], ROUND,
                                      ALU.mult, ALU.add).then_inc(wq_dve, 1)
                else:
                    k = n - 4
                    dve.wait_ge(wq_dve, 5 + k)
                    dve.tensor_scalar(w_q[:, k, :], w_round[:, k, :], -ROUND, None, ALU.add).then_inc(wq_dve, 1)

            def slot(c, s):
                if is_chunk(c):
                    gru(0, c * STEPS + s, s % 2, s % 8, s)
                half = expert_of(c, s)[2]
                if half == 0:
                    hidden_half(c, s, 0)
                if START < s <= START + 3 and is_chunk(c - 1):
                    router(c, s - START)
                if s == LAG + 1 and is_chunk(c - 1):
                    dve.wait_ge(o_hi_ready, c)
                    at = bass.ds((c - 1) * TOK, TOK)
                    dve.scalar_tensor_tensor(out=o_lo[:, at], in0=oT[:, :], scalar=O_SCALE, in1=o_hi[:, at],
                                             op0=ALU.mult, op1=ALU.subtract).then_inc(o_lo_ready, 1)
                if has_l1(c, s):
                    gru(1, c * STEPS + s - LAG, s % 2, (s + 1) % 2, s % LAG)
                if half == 0:
                    hidden_half(c, s, 1)
                else:
                    add_expert(c, s)
                if s == START and is_chunk(c - 1):
                    router(c, 0)
                if isinstance(c, int) and c < 2:
                    if c == 0:
                        if 1 <= s < CHUNKS:
                            mixed(s)
                        if 2 <= s <= CHUNKS:
                            mixed_lo(s - 1)
                        if s == 1:
                            bias_parts(1)
                        if s == 2:
                            split_weights(1, IH, 3)
                            split_weights(1, HH, 4)
                            dve.wait_ge(gain_ready, 1)
                            dve.tensor_scalar(gain[:, :], cond_gate[:, :], 1.0, 1.0 / H_SCALE, ALU.add, ALU.mult)\
                                .then_inc(gain_ready, 1)
                    elif s in QUANT_DVE:
                        quant_weights(QUANT_DVE[s])
                    for piece in pieces_of(c, s):
                        split_expert(piece)
                if isinstance(c, int):
                    for n in COND_DVE.get(c, {}).get(s, ()):
                        cond_step(n)

            for layer_no in range(2):
                dve.memset(factors[layer_no][:, :], 0.0)
                dve.memset(state[layer_no][:, 0, :], 0.0)
                dve.memset(parts[layer_no][:, (7, 0)[layer_no], :], 0.0)
            dve.memset(bias3[0][:, :], 0.0)
            dve.memset(bias3[1][:, :], 0.0).then_inc(cleared, 1)
            dve.wait_ge(cleared, 1)
            for layer_no in range(2):
                dve.memset(factors[layer_no][:, 1:24:3], 1.0)
                last = dve.memset(factors[layer_no][:, 25:48:3], H_SCALE)
            last.then_inc(init_done, 1)
            dve.wait_ge(got["first"], 16)
            mixed(0)
            dve.wait_ge(got["bias"], 48)
            bias_parts(0)
            mixed_lo(0)
            split_weights(0, IH, 1)
            split_weights(0, HH, 2)
            for s in range(16):
                slot(0, s)
            for s in range(16):
                slot(1, s)
            with dve.Fori(2, CHUNKS) as c:
                for s in range(16):
                    slot(c, s)
            for s in range(16):
                slot(CHUNKS, s)
            for s in range(START + 3):
                slot(CHUNKS + 1, s)

            x1T_by_seq = x1T[:, :].rearrange("p (t b) -> p b t", b=B)
            yT_by_seq = yT[:, :].rearrange("p (t b) -> p b t", b=B)
            dve.wait_ge(misc_taken, misc_before(CHUNKS + 1) + 1)
            for h in range(2):
                dve.wait_ge(layer_applied, h + 1)
                at = slice(4 * h, 4 * h + 4)
                dve.tensor_tensor(yT_by_seq[:, at, :], (p_gate, p_up)[h][:, :].rearrange("p (b t) -> p b t", b=4),
                                  x1T_by_seq[:, at, :], ALU.add).then_inc(y_added, 1)
            dve.wait_ge(y_added, 2)
            dve.tensor_reduce(part_top[:, 0:1], yT[:, :], AX_X, ALU.max, apply_absolute_value=True)\
                .then_inc(part_max_ready, 1)

            def all_max(k):
                dve.wait_ge(max_turned, k + 1)
                dve.tensor_reduce(row_top[:, k:k + 1], p_y[0:1, 0:D], AX_X, ALU.max).then_inc(row_max_ready, 1)
                dve.wait_ge(max_spread, k + 1)
                dve.tensor_scalar(q_step[:, k:k + 1], p_y[:, 256:257], MIN_RANGE, 1.0 / QP, ALU.max, ALU.mult)\
                    .then_inc(step_ready, 1)
                dve.wait_ge(step_ready, 2 * k + 1)
                dve.reciprocal(q_inv[:, k:k + 1], q_step[:, k:k + 1])
                dve.tensor_tensor(out_step[:, k:k + 1], w_step[:, k:k + 1], q_step[:, k:k + 1], ALU.mult)\
                    .then_inc(step_ready, 1)
                dve.wait_ge(step_ready, 2 * k + 2)

            all_max(0)
            for h in range(2):
                at = slice(h * F, (h + 1) * F)
                dve.tensor_scalar(q_round[:, 0, at], yT[:, at], q_inv[:, 0:1], ROUND, ALU.mult, ALU.add)\
                    .then_inc(y_rounded, 1)
                dve.wait_ge(y_rounded, h + 1)
                dve.tensor_scalar(y_q[:, at], q_round[:, 0, at], -ROUND, None, ALU.add).then_inc(y_q_ready, 1)
                if h == 0:
                    dve.tensor_scalar(gelu_bias[:, :], vec(V_B1, FB), out_step[:, 0:1], None, ALU.mult)\
                        .then_inc(gelu_bias_ready, 1)
            for k in range(2 * FB):
                h, f = k // FB, k % FB
                dve.wait_ge(gelu_ready, k + 1)
                dve.tensor_reduce(part_max[:, k:k + 1], ffn_h[:, f, h * F:(h + 1) * F], AX_X, ALU.max, apply_absolute_value=True)\
                    .then_inc(tile_max_ready, 1)
            dve.wait_ge(tile_max_ready, 2 * FB)
            dve.tensor_reduce(part_top[:, 1:2], part_max[:, :], AX_X, ALU.max).then_inc(part_max_ready, 1)
            all_max(1)
            for f in range(FB):
                dve.tensor_scalar(q_round[:, f, F:N], ffn_h[:, f, F:N], q_inv[:, 1:2], ROUND, ALU.mult, ALU.add)\
                    .then_inc(h_rounded_dve, 1)
            for f in range(FB):
                dve.wait_ge(h_rounded_dve, f + 1)
                last = dve.tensor_scalar(ffn_q[:, f, F:N], q_round[:, f, F:N], -ROUND, None, ALU.add)
            last.then_inc(ffn_q_ready, 1)
            for f in range(FB):
                dve.wait_ge(h_rounded_act, f + 1)
                last = dve.tensor_scalar(ffn_q[:, f, 0:F], q_round[:, f, 0:F], -ROUND, None, ALU.add)
            last.then_inc(ffn_q_ready, 1)
            dve.wait_ge(x1_kept, CHUNKS)
            for k, h in enumerate((1, 0)):
                at = slice(4 * h, 4 * h + 4)
                dve.wait_ge(ffn2_ready, k + 1)
                dve.tensor_tensor(o_sb[:, at, :], (p_gate, p_up)[h][:, :].rearrange("p (c d) -> p c d", c=4),
                                  ffn_b2.rearrange("p (a d) -> p a d", a=1).to_broadcast([D, 4, D]), ALU.add)\
                    .then_inc(out_biased, 1)
                dve.wait_ge(out_biased, k + 1)
                dve.scalar_tensor_tensor(out=o_sb[:, at, :], in0=o_sb[:, at, :], scalar=out_step[:, 1:2],
                                         in1=x1_tok[:, at, :], op0=ALU.mult, op1=ALU.add)\
                    .then_inc(out_ready, 1)

        @block.gpsimd
        def _(pool):
            def silu_half(c, s, half):
                chunk, e, _ = expert_of(c, s)
                if is_chunk(chunk):
                    j = chunk * E + e
                    at = slice(half * 256, half * 256 + 256)
                    pool.wait_ge(gate_read, 2 * j + half + 1)
                    wait_count(pool, hidden_ready, 2 * (j - 1) + half + 1)
                    pool.tensor_tensor(silu[:, at], gate_c[:, at], sig[:, at], ALU.mult).then_inc(silu_ready, 1)

            def slot(c, s):
                if isinstance(c, int) and c == 0 and s == 2:
                    pool.wait_ge(c_dve, 6)
                    pool.tensor_tensor(ln_rstd[:, :], ln_var[:, :], pow_half[:, :], ALU.pow).then_inc(c_pool, 1)
                if isinstance(c, int) and c == 1 and s == 0:
                    pool.wait_ge(wq_dve, 2)
                    pool.partition_all_reduce(w_amax[:, :], w_max[:, :], D, bass.bass_isa.ReduceOp.absmax)\
                        .then_inc(wq_pool, 1)
                if has_l1(c, s):
                    count = c * STEPS + s - LAG
                    if isinstance(c, int) and count == 0:
                        pool.wait_ge(gain_ready, 2)
                    if s == LAG and not (isinstance(c, int) and c == 0):
                        pool.wait_ge(o_projected, c)
                    pool.wait_ge(state_ready[1], count + 1)
                    pool.tensor_tensor(gated[:, (s - LAG) % STEPS, :], state[1][:, (s + 1) % 2, 2:24:3],
                                       gain[:, :], ALU.mult).then_inc(gated_ready, 1)
                half = expert_of(c, s)[2]
                silu_half(c, s, half)
                if s == START + 2 and is_chunk(c - 2):
                    pool.wait_ge(acc_ready, (c - 1) * E)
                    pool.tensor_copy(x1_tok[:, bass.ds(c - 2, 1), :].rearrange("p a d -> p (a d)"), acc[:, :])\
                        .then_inc(x1_kept, 1)

            pool.memset(bias_raw[:, :, :, :], 0.0).then_inc(bias_cleared, 1)
            pool.memset(warm[:, :], 0.0)
            pool.memset(ones_bf[:, :], 1.0)
            pool.memset(ones_f[:, :], 1.0)
            pool.memset(pow_half[:, :], -0.5)
            pool.memset(batch_mask[:, :], 1.0)
            pool.memset(ident[:, :], 0.0).then_inc(const_ready, 1)
            pool.wait_ge(const_ready, 1)
            pool.affine_select(out=ident[:, :], in_=ident[:, :], compare_op=ALU.not_equal, fill=1.0, base=0,
                               pattern=[[-1, D]], channel_multiplier=1)
            pool.affine_select(out=batch_mask[:, :], in_=batch_mask[:, :], compare_op=ALU.is_ge, fill=0.0,
                               base=0, pattern=[[-R, B]], channel_multiplier=1).then_inc(iota_ready, 1)
            pool.wait_ge(iota_ready, 1)
            pool.affine_select(out=batch_mask[:, :], in_=batch_mask[:, :], compare_op=ALU.is_ge, fill=0.0,
                               base=R - 1, pattern=[[R, B]], channel_multiplier=-1)
            pool.iota(expert_no_i[:, :], pattern=[[1, E]], base=0, channel_multiplier=0).then_inc(iota_ready, 1)
            pool.wait_ge(iota_ready, 2)
            pool.tensor_copy(expert_no[:, :], expert_no_i[:, :]).then_inc(iota_ready, 1)
            for s in range(16):
                slot(0, s)
            for s in range(16):
                slot(1, s)
            with pool.Fori(2, CHUNKS) as c:
                for s in range(16):
                    slot(c, s)
            for s in range(16):
                slot(CHUNKS, s)
            for s in range(START + 3):
                slot(CHUNKS + 1, s)


def kernel(x, cond_1024, **w):
    import numpy as np
    from concourse import bacc
    from concourse.bass_utils import run_bass_kernel_spmd

    c = {k: np.asarray(v) for k, v in w.items()}
    x, cond = np.asarray(x), np.asarray(cond_1024)

    def col(v):
        return v.reshape(-1, D).T

    x_time = x.transpose(1, 0, 2).reshape(N, D)

    def gru(i):
        return np.stack([c[f"L0_cond_Wih{i}"].T, c[f"L0_cond_Whh{i}"].T], axis=1)

    arrays = {
        "xT": x_time.T,
        "x_tok": x_time.reshape(CHUNKS, TOK, D).transpose(1, 0, 2),
        "first": np.concatenate([
            c["L0_cond_W_in"].T, cond.T, col(c["L0_cond_b_in"]), col(c["L0_cond_b_gate"]),
            col(c["L0_cond_b_out"]), col(c["L1_cond_ln_g"]), col(c["L1_cond_ln_b"]), col(c["L1_cond_b1"]),
            col(c["L1_ffn_b1"]),
            c["L1_cond_b2"].reshape(2, D, R).transpose(1, 0, 2).reshape(D, 2 * R)], axis=1),
        "gru0": gru(0),
        "gru1": gru(1),
        "proj": np.concatenate([
            c["L0_cond_W_gate"].T, c["L0_cond_W_out"].T, c["L1_cond_w1"], c["L1_cond_base_layer"],
            c["L0_ffn_W_router"].T], axis=1),
        "gate_up": np.concatenate([c["L0_ffn_W_gate"].transpose(2, 0, 1), c["L0_ffn_W_up"].transpose(2, 0, 1)],
                                  axis=2),
        "down": c["L0_ffn_W_down"].reshape(E, D, FB, D).transpose(3, 0, 2, 1),
        "cond_rows": cond,
        "biases": np.stack([np.stack([c[f"L0_cond_bih{i}"], c[f"L0_cond_bhh{i}"]]) for i in range(2)])[None],
        "cond_w2": c["L1_cond_w2"].reshape(D, 2, D, R).transpose(0, 1, 3, 2).reshape(D, 2 * R, D),
        "ffn": np.concatenate([
            c["L1_ffn_w1"].T, c["L1_ffn_w2"].reshape(D, FB, D).transpose(2, 1, 0).reshape(D, F),
            np.broadcast_to(c["L1_ffn_b2"], (D, D))], axis=1),
    }
    nc = bacc.Bacc("TRN2", target_bir_lowering=False, num_devices=1)
    arrays = {k: np.ascontiguousarray(v) for k, v in arrays.items()}
    args = [nc.dram_tensor(k, a.shape, mybir.dt.from_np(a.dtype), kind="ExternalInput").ap()
            for k, a in arrays.items()]
    out = nc.dram_tensor("out", (TOK, CHUNKS, D), F32, kind="ExternalOutput").ap()
    build(nc, *args, out)
    got = run_bass_kernel_spmd(nc, [arrays], core_ids=[0]).results[0]["out"]
    return got.reshape(STEPS, B, CHUNKS, D).transpose(1, 2, 0, 3).reshape(B, T, D)
```

```python
from contextlib import ExitStack

import concourse.bass as bass
from concourse import mybir

ALU = mybir.AluOpType
ACT = mybir.ActivationFunctionType
F32 = mybir.dt.float32
F16 = mybir.dt.float16
BF16 = mybir.dt.bfloat16
AX_X = mybir.AxisListType.X

B = 8
T = 128
D = 128
E = 8
F = 512
FB = F // D
R = 8
STEPS = 16
TOK = STEPS * B
CHUNKS = T // STEPS
N = T * B
LAG = 4
START = 6
PIECE = 256

W_SCALE = 2.0 ** 12
H_SCALE = 2.0 ** 14
GRU_UNSCALE = 1.0 / (W_SCALE * H_SCALE)
EW_SCALE = 2.0 ** 10
O_SCALE = 2.0 ** 8
MOE_UNSCALE = 1.0 / (EW_SCALE * O_SCALE)
ROUND = 1.5 * 2.0 ** 23
EPS = 1e-5
MIN_RANGE = 1e-6
QP = 127.0

V_BIN, V_BGATE, V_BOUT, V_LNG, V_LNB, V_CB1, V_B1, V_CB2 = 0, 1, 2, 3, 4, 5, 6, 10
VECS = 26
R_, Z_, N_ = 0, 1, 2
IH, HH = 0, 1


def wait_count(eng, semaphore, count):
    if not isinstance(count, int) or count > 0:
        eng.wait_ge(semaphore, count)


def expert_of(c, s):
    k = (s - START) % 16
    return (c - 1 if s >= START else c - 2), k // 2, k % 2


def experts_before(c, s, n):
    chunk, e, _ = expert_of(c, s)
    return (chunk, e - n) if e >= n else (chunk - 1, e - n + E)


def is_chunk(c):
    return not isinstance(c, int) or 0 <= c < CHUNKS


def has_l1(c, s):
    return not isinstance(c, int) or 0 <= c * STEPS + s - LAG < T


def misc_before(c):
    return CHUNKS + (3 * c - 4 if c > 1 else 0) if isinstance(c, int) else c * 3 + (CHUNKS + 2 - 6)


def pieces_of(c, s):
    k = c * STEPS + s - 4
    return range(2 * k, 2 * k + 2) if 0 <= k < E * 2 * F // PIECE // 2 else ()


COND_PE = {0: {4: (0,), 5: (1,)}, CHUNKS: {8: (2,), 10: (3,), 12: (4,), 13: (5,)}}
COND_DVE = {0: {2: (0,), 3: (1,), 4: (2,), 5: (3,)}, CHUNKS: {9: (4,), 11: (5,), 13: (6, 7), 14: (8, 9)}}
COND_GELU = 7
QUANT_DVE = {0: 0, 2: 1, 3: 2, 4: 3, 5: 4, 6: 5}


def build(nc, xT, x_tok, first, gru0, gru1, proj, gate_up, down, cond_rows, biases, cond_w2, ffn, out):
    with ExitStack() as ctx:
        def sb(name, shape, dt=F32):
            return ctx.enter_context(nc.sbuf_tensor(name, shape, dt))

        def bank(name):
            return ctx.enter_context(nc.psum_tensor(name, [D, 512], F32))

        def sem(name):
            return ctx.enter_context(nc.semaphore(name))

        first_sb = sb("first_sb", [D, D + B + VECS])
        w_in = first_sb[:, 0:D]
        condT = first_sb[:, D:D + B]

        def vec(k, n=1):
            return first_sb[:, D + B + k:D + B + k + n]

        xT_sb = sb("xT_sb", [D, N])
        x1_tok = sb("x1_tok", [D, CHUNKS, D])
        gru_f = [sb(f"gru_f{i}", [D, 2, 3 * D]) for i in range(2)]
        proj_sb = sb("proj_sb", [D, 4 * D + E])
        w_gate, w_out, c_w1, base = (proj_sb[:, k * D:(k + 1) * D] for k in range(4))
        w_router = proj_sb[:, 4 * D:4 * D + E]
        gu_f = sb("gu_f", [D, E, 2 * F])
        down_f = sb("down_f", [D, E, FB, D])
        cond_sb = sb("cond_sb", [B, D])
        bias_raw = sb("bias_raw", [D, 2, 2, 3 * D])
        c_w2 = sb("c_w2", [D, 2 * R, D])
        ffn_sb = sb("ffn_sb", [D, 2 * F + D])
        ffn_b2 = ffn_sb[:, 2 * F:2 * F + D]

        ones_bf = sb("ones_bf", [D, TOK], BF16)
        ones_f = sb("ones_f", [1, D])
        ident = sb("ident", [D, D])
        batch_mask = sb("batch_mask", [B * R, B])
        expert_no = sb("expert_no", [D, E])
        expert_no_i = sb("expert_no_i", [D, E], mybir.dt.int32)
        pow_half = sb("pow_half", [B, 1])
        warm = sb("warm", [D, 1])

        gru_hi = [sb(f"gru_hi{i}", [D, 2, 3 * D], F16) for i in range(2)]
        gru_lo = [sb(f"gru_lo{i}", [D, 2, 3 * D], F16) for i in range(2)]
        bias_f = [sb(f"bias_f{i}", [D, 4 * D]) for i in range(2)]
        bias_p1 = [sb(f"bias_p1{i}", [D, 4 * D], BF16) for i in range(2)]
        bias_r1 = [sb(f"bias_r1{i}", [D, 4 * D]) for i in range(2)]
        bias_p2 = [sb(f"bias_p2{i}", [D, 4 * D], BF16) for i in range(2)]
        bias3 = [sb(f"bias3{i}", [D, 4 * D], BF16) for i in range(2)]
        mix_sum = sb("mix_sum", [D, TOK])
        mix = sb("mix", [D, TOK])
        mix_hi = sb("mix_hi", [D, N], F16)
        mix_lo = sb("mix_lo", [D, N], F16)
        factors = [sb(f"factors{i}", [D, 48]) for i in range(2)]
        addends = [sb(f"addends{i}", [D, 24]) for i in range(2)]
        z_gate = [sb(f"z_gate{i}", [D, B]) for i in range(2)]
        state = [sb(f"state{i}", [D, 2, 24]) for i in range(2)]
        parts = [sb("parts0", [D, 8, 24], F16), sb("parts1", [D, 2, 24], F16)]
        gated = sb("gated", [D, STEPS, B])
        cond_gate = sb("cond_gate", [D, B])
        gain = sb("gain", [D, B])

        gu_hi = sb("gu_hi", [D, E, 2 * F], F16)
        gu_lo = sb("gu_lo", [D, E, 2 * F], F16)
        oT = sb("oT", [D, TOK])
        o_hi = sb("o_hi", [D, N], F16)
        o_lo = sb("o_lo", [D, N], F16)
        logits = sb("logits", [D, E])
        top8 = sb("top8", [D, 8])
        top8_at = sb("top8_at", [D, 8], mybir.dt.uint32)
        top8_no = sb("top8_no", [D, 8])
        top_gap = sb("top_gap", [D, 1])
        top_w = sb("top_w", [D, 2])
        share = sb("share", [D, 2, E])
        shares = sb("shares", [D, E])
        sig = sb("sig", [D, F])
        gate_c = sb("gate_c", [D, F])
        silu = sb("silu", [D, F])
        hidden = sb("hidden", [D, 2, F])
        acc = sb("acc", [D, 2, D])
        x1T = sb("x1T", [D, N])

        ln_sum = sb("ln_sum", [B, 1])
        ln_x = sb("ln_x", [B, D])
        ln_sq = sb("ln_sq", [B, D])
        ln_var = sb("ln_var", [B, 1])
        ln_rstd = sb("ln_rstd", [B, 1])
        ae = sb("ae", [D, B])
        cv = sb("cv", [D, B])
        ch = sb("ch", [D, B])
        ab = sb("ab", [D, 2, B, R])
        a_T = sb("a_T", [B * R, D])
        b_T = sb("b_T", [B * R, B, D])
        layer = sb("layer", [D, B, D])

        w_max = sb("w_max", [D, 2])
        w_amax = sb("w_amax", [D, 2])
        w_step = sb("w_step", [D, 2])
        w_inv = sb("w_inv", [D, 2])
        w_round = sb("w_round", [D, 2, F])
        w_q = sb("w_q", [D, 2, F], BF16)
        yT = sb("yT", [D, N])
        y_q = sb("y_q", [D, N], BF16)
        ffn_h = gu_f[:, 0:FB, :]
        q_round = gu_f[:, FB:2 * FB, :]
        ffn_q = sb("ffn_q", [D, FB, N], BF16)
        part_max = sb("part_max", [D, 2 * FB])
        part_top = sb("part_top", [D, 2])
        row_top = sb("row_top", [1, 2])
        q_step = sb("q_step", [D, 2])
        q_inv = sb("q_inv", [D, 2])
        out_step = sb("out_step", [D, 2])
        gelu_bias = sb("gelu_bias", [D, FB])
        o_sb = sb("o_sb", [D, CHUNKS, D])

        p_rz = [bank("p_rz0"), bank("p_rz1")]
        p_n = [bank("p_n0"), bank("p_n1")]
        pre = [p_n[i][:, 24 * STEPS:24 * STEPS + 24] for i in range(2)]
        p_gate, p_up, p_y, p_misc = bank("p_gate"), bank("p_up"), bank("p_y"), bank("p_misc")

        ffn1_banks = [p_rz[0], p_n[0], p_rz[1], p_n[1]]

        got = {k: sem(f"got_{k}") for k in
               ("first", "x0", "x", "gru0", "gru1", "proj", "cond", "c_w2", "ffn", "x_tok", "bias", "down")}
        got_gu = [sem(f"got_gu{e}") for e in range(E)]
        bias_cleared = sem("bias_cleared")
        const_ready = sem("const_ready")
        iota_ready = sem("iota_ready")
        split_hi = sem("split_hi")
        split_lo = sem("split_lo")
        bias_step = [sem("bias_step0"), sem("bias_step1")]
        cleared = sem("cleared")
        init_done = sem("init_done")
        gate_done = sem("gate_done")
        gain_ready = sem("gain_ready")
        misc_written = sem("misc_written")
        misc_taken = sem("misc_taken")
        mix_done = sem("mix_done")
        mix_hi_ready = sem("mix_hi_ready")
        mix_ready = sem("mix_ready")
        rz_ready = [sem("rz_ready0"), sem("rz_ready1")]
        nsum_ready = [sem("nsum_ready0"), sem("nsum_ready1")]
        z_ready = [sem("z_ready0"), sem("z_ready1")]
        gates_ready = [sem("gates_ready0"), sem("gates_ready1")]
        pre_ready = [sem("pre_ready0"), sem("pre_ready1")]
        cand_ready = [sem("cand_ready0"), sem("cand_ready1")]
        kept_ready = [sem("kept_ready0"), sem("kept_ready1")]
        hi_ready = [sem("hi_ready0"), sem("hi_ready1")]
        state_ready = [sem("state_ready0"), sem("state_ready1")]
        lo_ready = [sem("lo_ready0"), sem("lo_ready1")]
        gated_ready = sem("gated_ready")
        o_projected = sem("o_projected")
        o_hi_ready = sem("o_hi_ready")
        o_lo_ready = sem("o_lo_ready")
        logits_ready = sem("logits_ready")
        router_step = sem("router_step")
        gap_ready = sem("gap_ready")
        top_w_ready = sem("top_w_ready")
        gu_hi_ready = sem("gu_hi_ready")
        gu_lo_ready = sem("gu_lo_ready")
        gate_ready = sem("gate_ready")
        up_ready = sem("up_ready")
        gate_read = sem("gate_read")
        silu_ready = sem("silu_ready")
        hidden_ready = sem("hidden_ready")
        y_ready = sem("y_ready")
        acc_ready = sem("acc_ready")
        x1_transposed = sem("x1_transposed")
        x1_kept = sem("x1_kept")
        c_dve = sem("c_dve")
        c_pe = sem("c_pe")
        c_act = sem("c_act")
        c_pool = sem("c_pool")
        wq_dve = sem("wq_dve")
        wq_pool = sem("wq_pool")
        layer_applied = sem("layer_applied")
        y_added = sem("y_added")
        part_max_ready = sem("part_max_ready")
        max_turned = sem("max_turned")
        row_max_ready = sem("row_max_ready")
        max_spread = sem("max_spread")
        step_ready = sem("step_ready")
        y_rounded = sem("y_rounded")
        y_q_ready = sem("y_q_ready")
        gelu_bias_ready = sem("gelu_bias_ready")
        ffn1_ready = sem("ffn1_ready")
        gelu_ready = sem("gelu_ready")
        tile_max_ready = sem("tile_max_ready")
        h_rounded_act = sem("h_rounded_act")
        h_rounded_dve = sem("h_rounded_dve")
        ffn_q_ready = sem("ffn_q_ready")
        ffn2_ready = sem("ffn2_ready")
        out_biased = sem("out_biased")
        out_ready = sem("out_ready")
        out_stored = sem("out_stored")

        block = ctx.enter_context(nc.Block())

        @block.sync
        def _(sp):
            sp.dma_start(first_sb[:, :], first).then_inc(got["first"], 16)
            sp.dma_start(xT_sb[:, 0:TOK], xT[:, 0:TOK]).then_inc(got["x0"], 16)
            sp.dma_start(gru_f[0][:, :, :], gru0).then_inc(got["gru0"], 16)
            sp.wait_ge(bias_cleared, 1)
            for p in (0, 32, 64):
                sp.dma_start(bias_raw[p:p + 1, :, :, :], biases).then_inc(got["bias"], 16)
            sp.dma_start(gru_f[1][:, :, :], gru1).then_inc(got["gru1"], 16)
            sp.dma_start(xT_sb[:, TOK:N], xT[:, TOK:N]).then_inc(got["x"], 16)
            sp.dma_start(proj_sb[:, :], proj).then_inc(got["proj"], 16)
            sp.dma_start(cond_sb[:, :], cond_rows).then_inc(got["cond"], 16)
            sp.dma_start(c_w2[:, :, :], cond_w2).then_inc(got["c_w2"], 16)
            for e in range(2):
                sp.dma_start(gu_f[:, e, :], gate_up[:, e, :]).then_inc(got_gu[e], 16)
            sp.dma_start(ffn_sb[:, :], ffn).then_inc(got["ffn"], 16)
            for e in range(2, E):
                sp.dma_start(gu_f[:, e, :], gate_up[:, e, :]).then_inc(got_gu[e], 16)
            sp.dma_start(down_f[:, :, :, :], down).then_inc(got["down"], 16)
            sp.dma_start(x1_tok[:, :, :], x_tok).then_inc(got["x_tok"], 16)
            for k in range(2):
                half = slice((1 - k) * CHUNKS // 2, (2 - k) * CHUNKS // 2)
                sp.wait_ge(out_ready, k + 1)
                sp.dma_start(out[:, half, :], o_sb[:, half, :]).then_inc(out_stored, 16)
            sp.wait_ge(out_stored, 32)

        @block.tensor
        def _(pe):
            def prefill(layer_no, n_tok, moving_hi, moving_lo):
                rz, nn = p_rz[layer_no], p_n[layer_no]
                steps = n_tok // B
                hi, lo, b3 = gru_hi[layer_no], gru_lo[layer_no], bias3[layer_no]
                for g in (R_, Z_, N_):
                    if g == N_:
                        dst = nn[:, 2:24 * steps:3]
                    else:
                        dst = rz[:, 0:16 * steps].rearrange("p (t k) -> p t k", k=16)[:, :, 8 * g:8 * g + 8]
                    pe.matmul(dst, b3[:, g * D:(g + 1) * D], ones_bf[:, 0:n_tok],
                              start=g in (R_, N_), stop=False, skip_group_check=True)
                    w = slice(g * D, (g + 1) * D)
                    pe.matmul(dst, hi[:, IH, w], moving_hi, start=False, stop=False, skip_group_check=True)
                    pe.matmul(dst, lo[:, IH, w], moving_hi, start=False, stop=False, skip_group_check=True)
                    pe.matmul(dst, hi[:, IH, w], moving_lo, start=False, stop=False, skip_group_check=True)
                pe.matmul(nn[:, 0:24 * steps:3], b3[:, 3 * D:4 * D], ones_bf[:, 0:n_tok],
                          start=False, stop=False, skip_group_check=True)

            def step(layer_no, count, ring, at, between):
                hi, lo = gru_hi[layer_no], gru_lo[layer_no]
                rz, nn, h = p_rz[layer_no], p_n[layer_no], parts[layer_no]
                h_hi, h_lo, h_both = h[:, ring, 2:24:3], h[:, ring, 1:24:3], \
                    h[:, ring, :].rearrange("p (b k) -> p b k", k=3)[:, :, 1:3]
                wait_count(pe, hi_ready[layer_no], count)
                for g in (R_, Z_):
                    dst = rz[:, 16 * at + 8 * g:16 * at + 8 * g + 8]
                    for w in (hi, lo):
                        pe.matmul(dst, w[:, HH, g * D:(g + 1) * D], h_hi,
                                  start=False, stop=False, skip_group_check=True)
                pe.matmul(nn[:, 24 * at:24 * at + 24:3], lo[:, HH, 2 * D:3 * D], h_hi,
                          start=False, stop=False, skip_group_check=True)
                between()
                wait_count(pe, lo_ready[layer_no], count)
                for g in (R_, Z_):
                    dst = rz[:, 16 * at + 8 * g:16 * at + 8 * g + 8]
                    last = pe.matmul(dst, hi[:, HH, g * D:(g + 1) * D], h_lo,
                                     start=False, stop=False, skip_group_check=True)
                last.then_inc(rz_ready[layer_no], 1)
                both = nn[:, 24 * at:24 * at + 24].rearrange("p (b k) -> p b k", k=3)[:, :, 0:2]
                pe.matmul(both, hi[:, HH, 2 * D:3 * D], h_both,
                          start=False, stop=False, skip_group_check=True).then_inc(nsum_ready[layer_no], 1)

            def mixed(k):
                wait_count(pe, misc_taken, k)
                pe.matmul(p_misc[:, 0:TOK], w_in, xT_sb[:, k * TOK:(k + 1) * TOK],
                          start=True, stop=True).then_inc(misc_written, 1)

            def expert_products(which, c, s, numbers):
                chunk, e, _ = expert_of(c, s)
                if not is_chunk(chunk):
                    return
                bank_, ready = (p_gate, gate_ready) if which == 0 else (p_up, up_ready)
                j = chunk * E + e
                x_hi, x_lo = o_hi[:, bass.ds(chunk * TOK, TOK)], o_lo[:, bass.ds(chunk * TOK, TOK)]
                if numbers[0] == 0 and which == 0:
                    if e == 0:
                        pe.wait_ge(o_lo_ready, chunk + 1)
                    if isinstance(chunk, int) and chunk == 0:
                        pe.wait_ge(gu_lo_ready, 4 * (e + 1))
                    wait_count(pe, gate_read, 2 * j)
                elif numbers[0] == 0:
                    wait_count(pe, hidden_ready, 2 * j)
                for n in numbers:
                    f, product = n // 3, n % 3
                    w = slice(which * F + f * D, which * F + (f + 1) * D)
                    last = pe.matmul(bank_[:, f * D:(f + 1) * D], (gu_hi, gu_lo, gu_hi)[product][:, e, w],
                                     (x_hi, x_hi, x_lo)[product], start=product == 0, stop=product == 2)
                if numbers[-1] == 3 * FB - 1:
                    last.then_inc(ready, 1)

            def down_proj(c, s, before, f):
                chunk, e = experts_before(c, s, before)
                if is_chunk(chunk):
                    j = chunk * E + e
                    if f == 0:
                        wait_count(pe, acc_ready, j)
                        pe.wait_ge(hidden_ready, 2 * j + 1)
                        if isinstance(chunk, int) and chunk == 0 and e == 0:
                            pe.wait_ge(got["down"], 16)
                    if f == FB // 2:
                        pe.wait_ge(hidden_ready, 2 * j + 2)
                    last = pe.matmul(p_y[:, 0:D], hidden[:, e % 2, f * D:(f + 1) * D], down_f[:, e, f, :],
                                     start=f == 0, stop=f == FB - 1)
                    if f == FB - 1:
                        last.then_inc(y_ready, 1)

            def cond_step(n):
                if n == 0:
                    pe.wait_ge(c_dve, 7)
                    pe.transpose(p_gate[:, 0:B], ln_x[:, :], ident[0:B, 0:B]).then_inc(c_pe, 1)
                elif n == 1:
                    pe.wait_ge(c_dve, 8)
                    pe.matmul(p_gate[:, 0:B], c_w1, ae[:, :], start=True, stop=True).then_inc(c_pe, 1)
                elif n == 2:
                    pe.wait_ge(c_act, 1)
                    pe.wait_ge(got["c_w2"], 16)
                    pe.wait_ge(hi_ready[0], T)
                    for k in range(2 * R):
                        at = (k // R) * B * R + k % R
                        last = pe.matmul(p_rz[0][:, at:at + B * R - R + 1:R], c_w2[:, k, :], ch[:, :],
                                         start=True, stop=True)
                    last.then_inc(c_pe, 1)
                elif n == 3:
                    pe.wait_ge(c_dve, 11)
                    for k in range(2):
                        last = pe.transpose(p_n[0][0:B * R, k * D:(k + 1) * D],
                                            ab[:, k, :, :].rearrange("p b r -> p (b r)"), ident[:, :])
                    last.then_inc(c_pe, 1)
                else:
                    half = n - 4
                    pe.wait_ge(c_dve, 13 + half)
                    bank_ = (p_rz[0], p_n[0])[half]
                    for b in range(4):
                        last = pe.matmul(bank_[:, b * D:(b + 1) * D], a_T[:, :], b_T[:, 4 * half + b, :],
                                         start=True, stop=True)
                    last.then_inc(c_pe, 1)

            def during_layer0(c, s):
                if expert_of(c, s)[2] == 0:
                    down_proj(c, s, 2, 1)
                else:
                    down_proj(c, s, 2, 3)

            def after_layer0(c, s):
                if expert_of(c, s)[2] == 0:
                    expert_products(0, c, s, range(0, 6))
                else:
                    expert_products(1, c, s, range(0, 6))

            def during_layer1(c, s):
                if expert_of(c, s)[2] == 0:
                    expert_products(0, c, s, range(6, 10))
                else:
                    expert_products(1, c, s, range(6, 10))

            def after_layer1(c, s):
                if expert_of(c, s)[2] == 0:
                    expert_products(0, c, s, range(10, 12))
                    down_proj(c, s, 2, 2)
                else:
                    expert_products(1, c, s, range(10, 12))
                    down_proj(c, s, 1, 0)

            def slot(c, s):
                if is_chunk(c):
                    if s == 0:
                        if isinstance(c, int):
                            pe.wait_ge(mix_ready, c + 1)
                        wait_count(pe, hi_ready[0], c * STEPS)
                        prefill(0, TOK, mix_hi[:, bass.ds(c * TOK, TOK)], mix_lo[:, bass.ds(c * TOK, TOK)])
                    step(0, c * STEPS + s, (s + 7) % 8, s, lambda: during_layer0(c, s))
                else:
                    during_layer0(c, s)
                if isinstance(c, int) and c == 0:
                    if s == 1:
                        pe.wait_ge(got["x"], 16)
                        pe.wait_ge(got["proj"], 16)
                        pe.matmul(p_y[:, 0:B], w_gate, condT, start=True, stop=True).then_inc(gate_done, 1)
                    if 1 <= s < CHUNKS:
                        mixed(s)
                if s == START and is_chunk(c - 1):
                    pe.wait_ge(misc_taken, misc_before(c) + 1)
                    pe.matmul(p_misc[:, 0:E], oT[:, :], w_router, start=True, stop=True)\
                        .then_inc(logits_ready, 1)
                after_layer0(c, s)
                if has_l1(c, s):
                    if s % LAG == 0:
                        g = s // LAG % 2
                        group = slice(4 * (1 - g), 4 * (1 - g) + 4)
                        if isinstance(c, int) and c * STEPS + s == LAG:
                            pe.wait_ge(split_lo, 4)
                            pe.wait_ge(bias_step[1], 10)
                        pe.wait_ge(lo_ready[0], c * STEPS + s)
                        wait_count(pe, hi_ready[1], c * STEPS + s - LAG)
                        h = parts[0][:, group, :].rearrange("p t k -> p (t k)")
                        prefill(1, LAG * B, h[:, 2:96:3], h[:, 1:96:3])
                    step(1, c * STEPS + s - LAG, s % 2, s % LAG, lambda: during_layer1(c, s))
                else:
                    during_layer1(c, s)
                if s == LAG and is_chunk(c - 1):
                    pe.wait_ge(gated_ready, c * STEPS)
                    pe.wait_ge(misc_taken, misc_before(c))
                    pe.matmul(p_misc[:, 0:TOK], w_out, gated[:, :, :].rearrange("p t b -> p (t b)"),
                              start=True, stop=True).then_inc(o_projected, 1)
                if s == START + 4 and is_chunk(c - 2):
                    pe.wait_ge(acc_ready, (c - 1) * E)
                    pe.wait_ge(misc_taken, misc_before(c) + (2 if is_chunk(c - 1) else 0))
                    pe.transpose(p_misc[:, 0:D], acc[:, 1, :], ident[:, :]).then_inc(x1_transposed, 1)
                after_layer1(c, s)
                if isinstance(c, int):
                    for n in COND_PE.get(c, {}).get(s, ()):
                        cond_step(n)

            pe.wait_ge(got["first"], 16)
            pe.wait_ge(got["x0"], 16)
            mixed(0)
            pe.wait_ge(iota_ready, 1)
            pe.wait_ge(init_done, 1)
            pe.wait_ge(split_lo, 2)
            pe.wait_ge(bias_step[0], 10)
            for s in range(16):
                slot(0, s)
            for s in range(16):
                slot(1, s)
            with pe.Fori(2, CHUNKS) as c:
                for s in range(16):
                    slot(c, s)
            for s in range(16):
                slot(CHUNKS, s)
            for s in range(START + 6):
                slot(CHUNKS + 1, s)

            pe.wait_ge(misc_taken, misc_before(CHUNKS + 1) + 1)
            pe.wait_ge(c_dve, 18)
            for b in range(B):
                last = pe.matmul((p_gate, p_up)[b // 4][:, b % 4 * T:(b % 4 + 1) * T], layer[:, b, :],
                                 x1T[:, b:N:B], start=True, stop=True)
                if b % 4 == 3:
                    last.then_inc(layer_applied, 1)

            def all_max(k):
                pe.wait_ge(part_max_ready, k + 1)
                pe.transpose(p_y[0:1, 0:D], part_top[:, k:k + 1], ident[:, :]).then_inc(max_turned, 1)
                pe.wait_ge(row_max_ready, k + 1)
                pe.matmul(p_y[:, 256:257], ones_f[:, :], row_top[:, k:k + 1], start=True, stop=True)\
                    .then_inc(max_spread, 1)

            all_max(0)
            for h in range(2):
                pe.wait_ge(y_q_ready, h + 1)
                for f in range(FB):
                    if h:
                        pe.wait_ge(gelu_ready, f + 1)
                    pe.matmul(ffn1_banks[f][:, :], w_q[:, 0, f * D:(f + 1) * D], y_q[:, h * F:(h + 1) * F],
                              start=True, stop=True).then_inc(ffn1_ready, 1)
            all_max(1)
            for k in (4, 5, 6, 7, 0, 1, 2, 3):
                pe.wait_ge(ffn_q_ready, 1 if k >= CHUNKS // 2 else 2)
                for f in range(FB):
                    last = pe.matmul((p_gate, p_up)[k // 4][:, k % 4 * D:(k % 4 + 1) * D],
                                     ffn_q[:, f, k * TOK:(k + 1) * TOK], w_q[:, 1, f * D:(f + 1) * D],
                                     start=f == 0, stop=f == FB - 1)
                if k % 4 == 3:
                    last.then_inc(ffn2_ready, 1)

        @block.scalar
        def _(act):
            def gru(layer_no, count, at, between):
                rz, fa = p_rz[layer_no], factors[layer_no]
                act.wait_ge(rz_ready[layer_no], count + 1)
                act.activation(fa[:, :].rearrange("p (g b k) -> p g b k", g=2, k=3)[:, :, :, 2],
                               rz[:, 16 * at:16 * at + 16].rearrange("p (g b) -> p g b", g=2),
                               ACT.Sigmoid, scale=GRU_UNSCALE).then_inc(gates_ready[layer_no], 1)
                wait_count(act, kept_ready[layer_no], count)
                act.activation(z_gate[layer_no][:, :], rz[:, 16 * at + 8:16 * at + 16],
                               ACT.Sigmoid, scale=-GRU_UNSCALE).then_inc(z_ready[layer_no], 1)
                between()
                act.wait_ge(pre_ready[layer_no], count + 1)
                act.activation(addends[layer_no][:, 0:24:3], pre[layer_no][:, 2:24:3], ACT.Tanh,
                               scale=GRU_UNSCALE).then_inc(cand_ready[layer_no], 1)

            def mixed(k):
                act.wait_ge(misc_taken, k + 1)
                wait_count(act, mix_ready, k)
                act.activation(mix[:, :], mix_sum[:, :], ACT.Tanh, bias=vec(V_BIN)).then_inc(mix_done, 1)
                act.wait_ge(mix_done, k + 1)
                act.activation(mix_hi[:, k * TOK:(k + 1) * TOK], mix[:, :], ACT.Copy,
                               scale=H_SCALE).then_inc(mix_hi_ready, 1)

            def split_weights(layer_no, kind):
                for cols, sign in (((0, D), 1.0), ((D, 2 * D), -1.0), ((2 * D, 3 * D), 1.0)):
                    last = act.activation(gru_hi[layer_no][:, kind, cols[0]:cols[1]],
                                          gru_f[layer_no][:, kind, cols[0]:cols[1]], ACT.Copy,
                                          scale=sign * W_SCALE)
                last.then_inc(split_hi, 1)

            def split_expert(piece):
                e, q = piece // 4, piece % 4
                if q == 0:
                    act.wait_ge(got_gu[e], 16)
                act.activation(gu_hi[:, e, q * 256:(q + 1) * 256], gu_f[:, e, q * 256:(q + 1) * 256], ACT.Copy,
                               scale=EW_SCALE).then_inc(gu_hi_ready, 1)

            def out_of_gate(c, s, part):
                chunk, e, _ = expert_of(c, s)
                if is_chunk(chunk):
                    j = chunk * E + e
                    half = part // 2
                    cols = slice(half * 256, half * 256 + 256)
                    if part == 0:
                        act.wait_ge(gate_ready, j + 1)
                    if part % 2 == 0:
                        wait_count(act, silu_ready, 2 * (j - 1) + half + 1)
                        act.activation(sig[:, cols], p_gate[:, cols], ACT.Sigmoid, scale=MOE_UNSCALE)
                    else:
                        act.activation(gate_c[:, cols], p_gate[:, cols], ACT.Copy, scale=MOE_UNSCALE)\
                            .then_inc(gate_read, 1)

            def during_layer0(c, s):
                if s == LAG + 1:
                    if is_chunk(c - 1):
                        act.wait_ge(o_projected, c)
                        if not (isinstance(c, int) and c == 1):
                            act.wait_ge(logits_ready, c - 1)
                            act.wait_ge(o_lo_ready, c - 1)
                        act.activation(oT[:, :], p_misc[:, 0:TOK], ACT.Identity, bias=vec(V_BOUT))\
                            .then_inc(misc_taken, 1)
                elif expert_of(c, s)[2] == 1:
                    out_of_gate(c, s, 2)

            def after_layer0(c, s):
                if s == LAG + 1:
                    if is_chunk(c - 1):
                        act.wait_ge(misc_taken, misc_before(c) + 1)
                        act.activation(o_hi[:, bass.ds((c - 1) * TOK, TOK)], oT[:, :], ACT.Copy,
                                       scale=O_SCALE).then_inc(o_hi_ready, 1)
                    out_of_gate(c, s, 2)
                elif expert_of(c, s)[2] == 1:
                    out_of_gate(c, s, 3)
                if s == START + 2 and is_chunk(c - 1):
                    act.wait_ge(gap_ready, c)
                    act.activation(top_w[:, 0:1], top_gap[:, :], ACT.Sigmoid, scale=-1.0)
                    act.activation(top_w[:, 1:2], top_gap[:, :], ACT.Sigmoid).then_inc(top_w_ready, 1)

            def during_layer1(c, s):
                if s == LAG + 1:
                    out_of_gate(c, s, 3)
                elif expert_of(c, s)[2] == 0:
                    out_of_gate(c, s, 0)

            def after_layer1(c, s):
                if expert_of(c, s)[2] == 0:
                    out_of_gate(c, s, 1)
                if s == START + 5 and is_chunk(c - 2):
                    act.wait_ge(x1_transposed, c - 1)
                    act.activation(x1T[:, bass.ds((c - 2) * TOK, TOK)], p_misc[:, 0:TOK], ACT.Copy)\
                        .then_inc(misc_taken, 1)

            def slot(c, s):
                if is_chunk(c):
                    gru(0, c * STEPS + s, s, lambda: during_layer0(c, s))
                else:
                    during_layer0(c, s)
                after_layer0(c, s)
                if has_l1(c, s):
                    gru(1, c * STEPS + s - LAG, s % LAG, lambda: during_layer1(c, s))
                else:
                    during_layer1(c, s)
                after_layer1(c, s)
                if isinstance(c, int) and c < 2:
                    if c == 0 and 1 <= s < CHUNKS:
                        mixed(s)
                    if c == 0 and s == 1:
                        act.wait_ge(got["gru1"], 16)
                        split_weights(1, IH)
                        split_weights(1, HH)
                        act.wait_ge(gate_done, 1)
                        act.activation(cond_gate[:, :], p_y[:, 0:B], ACT.Sigmoid, bias=vec(V_BGATE))\
                            .then_inc(gain_ready, 1)
                    for piece in pieces_of(c, s):
                        split_expert(piece)
                if isinstance(c, int) and c == CHUNKS and s == COND_GELU:
                    act.wait_ge(c_dve, 9)
                    act.activation(ch[:, :], cv[:, :], ACT.Gelu).then_inc(c_act, 1)

            act.wait_ge(const_ready, 1)
            act.activation(warm[:, :], warm[:, :], ACT.Sigmoid)
            act.wait_ge(init_done, 1)
            act.wait_ge(got["first"], 16)
            act.wait_ge(got["gru0"], 16)
            split_weights(0, IH)
            mixed(0)
            split_weights(0, HH)
            for s in range(16):
                slot(0, s)
            for s in range(16):
                slot(1, s)
            with act.Fori(2, CHUNKS) as c:
                for s in range(16):
                    slot(c, s)
            for s in range(16):
                slot(CHUNKS, s)
            for s in range(START + 6):
                slot(CHUNKS + 1, s)

            act.wait_ge(gelu_bias_ready, 1)
            for k in range(2 * FB):
                h, f = k // FB, k % FB
                act.wait_ge(ffn1_ready, k + 1)
                act.activation(ffn_h[:, f, h * F:(h + 1) * F], ffn1_banks[f][:, :], ACT.Gelu,
                               scale=out_step[:, 0:1], bias=gelu_bias[:, f:f + 1]).then_inc(gelu_ready, 1)
            act.wait_ge(step_ready, 4)
            for f in range(FB):
                act.activation(q_round[:, f, 0:F], ffn_h[:, f, 0:F], ACT.Copy,
                               scale=q_inv[:, 1:2], bias=ROUND).then_inc(h_rounded_act, 1)

        @block.vector
        def _(dve):
            def gru(layer_no, count, buf, ring, at, between):
                fa, ad, st, pa = factors[layer_no], addends[layer_no], state[layer_no], parts[layer_no]
                dve.wait_ge(gates_ready[layer_no], count + 1)
                dve.wait_ge(nsum_ready[layer_no], count + 1)
                dve.tensor_tensor_scan(pre[layer_no], fa[:, 0:24], p_n[layer_no][:, 24 * at:24 * at + 24],
                                       0.0, ALU.mult, ALU.add).then_inc(pre_ready[layer_no], 1)
                dve.wait_ge(z_ready[layer_no], count + 1)
                dve.tensor_tensor(ad[:, 2:24:3], z_gate[layer_no][:, :], st[:, buf, 2:24:3], ALU.mult)\
                    .then_inc(kept_ready[layer_no], 1)
                between()
                dve.wait_ge(kept_ready[layer_no], count + 1)
                dve.wait_ge(cand_ready[layer_no], count + 1)
                dve.tensor_tensor_scan(pa[:, ring, :], fa[:, 24:48], ad[:, :], 0.0, ALU.mult, ALU.add)\
                    .then_inc(hi_ready[layer_no], 1)
                if layer_no == 1:
                    wait_count(dve, gated_ready, count - 1)
                dve.tensor_tensor_scan(st[:, 1 - buf, :], fa[:, 24:48], ad[:, :], 0.0, ALU.mult, ALU.add)\
                    .then_inc(state_ready[layer_no], 1)
                dve.wait_ge(state_ready[layer_no], count + 1)
                dve.tensor_tensor(pa[:, ring, 1:24:3], st[:, 1 - buf, 2:24:3], pa[:, ring, 2:24:3], ALU.subtract)\
                    .then_inc(lo_ready[layer_no], 1)

            def mixed(k):
                dve.wait_ge(misc_written, k + 1)
                wait_count(dve, mix_done, k)
                dve.tensor_tensor(mix_sum[:, :].rearrange("p (t b) -> p t b", b=B),
                                  p_misc[:, 0:TOK].rearrange("p (t b) -> p t b", b=B),
                                  condT.rearrange("p (a b) -> p a b", a=1).to_broadcast([D, STEPS, B]),
                                  ALU.add).then_inc(misc_taken, 1)

            def mixed_lo(k):
                dve.wait_ge(mix_hi_ready, k + 1)
                cols = slice(k * TOK, (k + 1) * TOK)
                dve.scalar_tensor_tensor(out=mix_lo[:, cols], in0=mix[:, :], scalar=H_SCALE,
                                         in1=mix_hi[:, cols], op0=ALU.mult, op1=ALU.subtract)\
                    .then_inc(mix_ready, 1)

            def split_weights(layer_no, kind, n):
                dve.wait_ge(split_hi, n)
                for cols, sign in (((0, D), 1.0), ((D, 2 * D), -1.0), ((2 * D, 3 * D), 1.0)):
                    at = slice(*cols)
                    last = dve.scalar_tensor_tensor(
                        out=gru_lo[layer_no][:, kind, at], in0=gru_f[layer_no][:, kind, at],
                        scalar=sign * W_SCALE, in1=gru_hi[layer_no][:, kind, at],
                        op0=ALU.mult, op1=ALU.subtract)
                last.then_inc(split_lo, 1)

            def split_expert(piece):
                e, q = piece // 4, piece % 4
                at = slice(q * 256, (q + 1) * 256)
                dve.wait_ge(gu_hi_ready, piece + 1)
                dve.scalar_tensor_tensor(out=gu_lo[:, e, at], in0=gu_f[:, e, at], scalar=EW_SCALE,
                                         in1=gu_hi[:, e, at], op0=ALU.mult, op1=ALU.subtract)\
                    .then_inc(gu_lo_ready, 1)

            def hidden_half(c, s, half):
                chunk, e = experts_before(c, s, 1)
                if is_chunk(chunk):
                    j = chunk * E + e
                    at = slice(half * 256, half * 256 + 256)
                    dve.wait_ge(up_ready, j + 1)
                    dve.wait_ge(silu_ready, 2 * j + half + 1)
                    dve.scalar_tensor_tensor(out=hidden[:, e % 2, at], in0=p_up[:, at], scalar=MOE_UNSCALE,
                                             in1=silu[:, at], op0=ALU.mult, op1=ALU.mult)\
                        .then_inc(hidden_ready, 1)

            def add_expert(c, s):
                chunk, e = experts_before(c, s, 2)
                if is_chunk(chunk):
                    j = chunk * E + e
                    dve.wait_ge(y_ready, j + 1)
                    if e == 0:
                        dve.wait_ge(router_step, 7 * (chunk + 1))
                        if isinstance(chunk, int) and chunk == 0:
                            dve.wait_ge(got["x_tok"], 16)
                        old = x1_tok[:, bass.ds(chunk, 1), :].rearrange("p a d -> p (a d)")
                    else:
                        dve.wait_ge(acc_ready, j)
                        old = acc[:, 1 - e % 2, :]
                    if e == 1 and not (isinstance(chunk, int) and chunk == 0):
                        dve.wait_ge(x1_transposed, chunk)
                        dve.wait_ge(x1_kept, chunk)
                    dve.scalar_tensor_tensor(out=acc[:, e % 2, :], in0=p_y[:, 0:D], scalar=shares[:, e:e + 1],
                                             in1=old, op0=ALU.mult, op1=ALU.add).then_inc(acc_ready, 1)

            def router(c, part):
                n = 7 * (c - 1)
                if part == 0:
                    dve.wait_ge(logits_ready, c)
                    dve.tensor_copy(logits[:, :], p_misc[:, 0:E]).then_inc(misc_taken, 1)
                elif part == 1:
                    if not is_chunk(c):
                        dve.wait_ge(misc_taken, misc_before(c) + 2)
                    dve.max(top8[:, :], logits[:, :]).then_inc(router_step, 1)
                    dve.wait_ge(router_step, n + 1)
                    dve.tensor_tensor(top_gap[:, :], top8[:, 1:2], top8[:, 0:1], ALU.subtract)\
                        .then_inc(gap_ready, 1)
                elif part == 2:
                    if not is_chunk(c):
                        dve.wait_ge(router_step, n + 1)
                    dve.max_index(top8_at[:, :], top8[:, :], logits[:, :]).then_inc(router_step, 1)
                    dve.wait_ge(router_step, n + 2)
                    dve.tensor_copy(top8_no[:, :], top8_at[:, :]).then_inc(router_step, 1)
                else:
                    dve.wait_ge(router_step, n + 3)
                    dve.wait_ge(top_w_ready, c)
                    for k in range(2):
                        dve.tensor_scalar(share[:, k, :], expert_no[:, :], top8_no[:, k:k + 1], top_w[:, k:k + 1],
                                          ALU.is_equal, ALU.mult).then_inc(router_step, 1)
                    dve.wait_ge(router_step, n + 5)
                    dve.tensor_tensor(shares[:, :], share[:, 0, :], share[:, 1, :], ALU.add)\
                        .then_inc(router_step, 2)

            def bias_parts(layer_no):
                b, raw = bias_f[layer_no], bias_raw
                done = bias_step[layer_no]
                sk = W_SCALE * H_SCALE
                dve.tensor_tensor(b[:, 0:2 * D], raw[:, layer_no, IH, 0:2 * D], raw[:, layer_no, HH, 0:2 * D],
                                  ALU.add).then_inc(done, 1)
                dve.tensor_scalar(b[:, 2 * D:3 * D], raw[:, layer_no, IH, 2 * D:3 * D], sk, None, ALU.mult)\
                    .then_inc(done, 1)
                dve.tensor_scalar(b[:, 3 * D:4 * D], raw[:, layer_no, HH, 2 * D:3 * D], sk, None, ALU.mult)\
                    .then_inc(done, 1)
                dve.wait_ge(done, 3)
                dve.tensor_scalar(b[:, 0:D], b[:, 0:D], sk, None, ALU.mult)
                dve.tensor_scalar(b[:, D:2 * D], b[:, D:2 * D], -sk, None, ALU.mult).then_inc(done, 1)
                dve.wait_ge(done, 4)
                dve.tensor_copy(bias_p1[layer_no][:, :], b[:, :]).then_inc(done, 1)
                dve.wait_ge(done, 5)
                dve.tensor_tensor(bias_r1[layer_no][:, :], b[:, :], bias_p1[layer_no][:, :], ALU.subtract)\
                    .then_inc(done, 1)
                dve.wait_ge(done, 6)
                dve.tensor_copy(bias_p2[layer_no][:, :], bias_r1[layer_no][:, :]).then_inc(done, 1)
                dve.wait_ge(done, 7)
                dve.tensor_copy(bias3[layer_no][0:1, :], bias_p1[layer_no][0:1, :]).then_inc(done, 1)
                dve.tensor_copy(bias3[layer_no][32:33, :], bias_p2[layer_no][32:33, :]).then_inc(done, 1)
                dve.tensor_tensor(bias3[layer_no][64:65, :], bias_r1[layer_no][64:65, :],
                                  bias_p2[layer_no][64:65, :], ALU.subtract).then_inc(done, 1)

            def cond_step(n):
                if n == 0:
                    dve.wait_ge(got["cond"], 16)
                    dve.tensor_reduce(ln_sum[:, :], cond_sb[:, :], AX_X, ALU.add).then_inc(c_dve, 1)
                    dve.wait_ge(c_dve, 1)
                    dve.tensor_scalar(ln_sum[:, :], ln_sum[:, :], 1.0 / D, None, ALU.mult).then_inc(c_dve, 1)
                    dve.wait_ge(c_dve, 2)
                    dve.tensor_scalar(ln_x[:, :], cond_sb[:, :], ln_sum[:, 0:1], None, ALU.subtract)\
                        .then_inc(c_dve, 1)
                    dve.wait_ge(c_dve, 3)
                    dve.tensor_tensor(ln_sq[:, :], ln_x[:, :], ln_x[:, :], ALU.mult).then_inc(c_dve, 1)
                    dve.wait_ge(c_dve, 4)
                    dve.tensor_reduce(ln_var[:, :], ln_sq[:, :], AX_X, ALU.add).then_inc(c_dve, 1)
                    dve.wait_ge(c_dve, 5)
                    dve.tensor_scalar(ln_var[:, :], ln_var[:, :], 1.0 / D, EPS, ALU.mult, ALU.add)\
                        .then_inc(c_dve, 1)
                elif n == 1:
                    dve.wait_ge(c_pool, 1)
                    dve.tensor_scalar(ln_x[:, :], ln_x[:, :], ln_rstd[:, 0:1], None, ALU.mult)\
                        .then_inc(c_dve, 1)
                elif n == 2:
                    dve.wait_ge(c_pe, 1)
                    dve.tensor_scalar(ae[:, :], p_gate[:, 0:B], vec(V_LNG), vec(V_LNB), ALU.mult, ALU.add)\
                        .then_inc(c_dve, 1)
                elif n == 3:
                    dve.wait_ge(c_pe, 2)
                    dve.tensor_scalar(cv[:, :], p_gate[:, 0:B], vec(V_CB1), None, ALU.add).then_inc(c_dve, 1)
                elif n == 4:
                    dve.wait_ge(c_pe, 3)
                    for k in range(2):
                        dve.tensor_tensor(ab[:, k, :, :],
                                          p_rz[0][:, k * B * R:(k + 1) * B * R].rearrange("p (b r) -> p b r", r=R),
                                          vec(V_CB2 + k * R, R).rearrange("p (a r) -> p a r", a=1)
                                          .to_broadcast([D, B, R]), ALU.add).then_inc(c_dve, 1)
                elif n == 5:
                    dve.wait_ge(c_pe, 4)
                    dve.wait_ge(iota_ready, 3)
                    dve.tensor_copy(a_T[:, :], p_n[0][0:B * R, 0:D]).then_inc(c_dve, 1)
                    for b in range(B):
                        last = dve.tensor_scalar(b_T[:, b, :], p_n[0][0:B * R, D:2 * D], batch_mask[:, b:b + 1],
                                                 None, ALU.mult)
                        if b % 4 == 3:
                            last.then_inc(c_dve, 1)
                else:
                    half, quarter = (n - 6) // 2, (n - 6) % 2
                    dve.wait_ge(c_pe, 5 + half)
                    bank_ = (p_rz[0], p_n[0])[half]
                    at = 4 * half + 2 * quarter
                    dve.tensor_tensor(layer[:, at:at + 2, :],
                                      bank_[:, quarter * 2 * D:(quarter + 1) * 2 * D]
                                      .rearrange("p (b o) -> p b o", b=2),
                                      base.rearrange("p (a o) -> p a o", a=1).to_broadcast([D, 2, D]),
                                      ALU.add).then_inc(c_dve, 1)

            def quant_weights(n):
                if n == 0:
                    dve.wait_ge(got["ffn"], 16)
                    for k in range(2):
                        dve.tensor_reduce(w_max[:, k:k + 1], ffn_sb[:, k * F:(k + 1) * F], AX_X, ALU.max,
                                          apply_absolute_value=True).then_inc(wq_dve, 1)
                elif n == 1:
                    dve.wait_ge(wq_pool, 1)
                    dve.tensor_scalar(w_step[:, :], w_amax[:, :], MIN_RANGE, 1.0 / QP, ALU.max, ALU.mult)\
                        .then_inc(wq_dve, 1)
                    dve.wait_ge(wq_dve, 3)
                    dve.reciprocal(w_inv[:, :], w_step[:, :]).then_inc(wq_dve, 1)
                    dve.wait_ge(wq_dve, 4)
                elif n < 4:
                    k = n - 2
                    dve.tensor_scalar(w_round[:, k, :], ffn_sb[:, k * F:(k + 1) * F], w_inv[:, k:k + 1], ROUND,
                                      ALU.mult, ALU.add).then_inc(wq_dve, 1)
                else:
                    k = n - 4
                    dve.wait_ge(wq_dve, 5 + k)
                    dve.tensor_scalar(w_q[:, k, :], w_round[:, k, :], -ROUND, None, ALU.add).then_inc(wq_dve, 1)

            def during_layer0(c, s):
                if expert_of(c, s)[2] == 0:
                    hidden_half(c, s, 0)
                else:
                    add_expert(c, s)

            def during_layer1(c, s):
                if expert_of(c, s)[2] == 0:
                    hidden_half(c, s, 1)
                if s == LAG + 1 and is_chunk(c - 1):
                    dve.wait_ge(o_hi_ready, c)
                    at = bass.ds((c - 1) * TOK, TOK)
                    dve.scalar_tensor_tensor(out=o_lo[:, at], in0=oT[:, :], scalar=O_SCALE, in1=o_hi[:, at],
                                             op0=ALU.mult, op1=ALU.subtract).then_inc(o_lo_ready, 1)

            def slot(c, s):
                if is_chunk(c):
                    gru(0, c * STEPS + s, s % 2, s % 8, s, lambda: during_layer0(c, s))
                else:
                    during_layer0(c, s)
                if START <= s <= START + 3 and is_chunk(c - 1):
                    router(c, s - START)
                if has_l1(c, s):
                    gru(1, c * STEPS + s - LAG, s % 2, (s + 1) % 2, s % LAG, lambda: during_layer1(c, s))
                else:
                    during_layer1(c, s)
                if isinstance(c, int) and c < 2:
                    if c == 0:
                        if 1 <= s < CHUNKS:
                            mixed(s)
                        if 2 <= s <= CHUNKS:
                            mixed_lo(s - 1)
                        if s == 1:
                            bias_parts(1)
                        if s == 2:
                            split_weights(1, IH, 3)
                            split_weights(1, HH, 4)
                            dve.wait_ge(gain_ready, 1)
                            dve.tensor_scalar(gain[:, :], cond_gate[:, :], 1.0, 1.0 / H_SCALE, ALU.add, ALU.mult)\
                                .then_inc(gain_ready, 1)
                    elif s in QUANT_DVE:
                        quant_weights(QUANT_DVE[s])
                    for piece in pieces_of(c, s):
                        split_expert(piece)
                if isinstance(c, int):
                    for n in COND_DVE.get(c, {}).get(s, ()):
                        cond_step(n)

            for layer_no in range(2):
                dve.memset(factors[layer_no][:, :], 0.0)
                dve.memset(state[layer_no][:, 0, :], 0.0)
                dve.memset(addends[layer_no][:, :], 0.0)
                dve.memset(parts[layer_no][:, (7, 0)[layer_no], :], 0.0)
            dve.memset(bias3[0][:, :], 0.0)
            dve.memset(bias3[1][:, :], 0.0).then_inc(cleared, 1)
            dve.wait_ge(cleared, 1)
            for layer_no in range(2):
                dve.memset(factors[layer_no][:, 1:24:3], 1.0)
                last = dve.memset(factors[layer_no][:, 25:48:3], H_SCALE)
            last.then_inc(init_done, 1)
            dve.wait_ge(got["first"], 16)
            mixed(0)
            dve.wait_ge(got["bias"], 48)
            bias_parts(0)
            mixed_lo(0)
            split_weights(0, IH, 1)
            split_weights(0, HH, 2)
            for s in range(16):
                slot(0, s)
            for s in range(16):
                slot(1, s)
            with dve.Fori(2, CHUNKS) as c:
                for s in range(16):
                    slot(c, s)
            for s in range(16):
                slot(CHUNKS, s)
            for s in range(START + 6):
                slot(CHUNKS + 1, s)

            x1T_by_seq = x1T[:, :].rearrange("p (t b) -> p b t", b=B)
            yT_by_seq = yT[:, :].rearrange("p (t b) -> p b t", b=B)
            dve.wait_ge(misc_taken, misc_before(CHUNKS + 1) + 1)
            for h in range(2):
                dve.wait_ge(layer_applied, h + 1)
                at = slice(4 * h, 4 * h + 4)
                dve.tensor_tensor(yT_by_seq[:, at, :], (p_gate, p_up)[h][:, :].rearrange("p (b t) -> p b t", b=4),
                                  x1T_by_seq[:, at, :], ALU.add).then_inc(y_added, 1)
            dve.wait_ge(y_added, 2)
            dve.tensor_reduce(part_top[:, 0:1], yT[:, :], AX_X, ALU.max, apply_absolute_value=True)\
                .then_inc(part_max_ready, 1)

            def all_max(k):
                dve.wait_ge(max_turned, k + 1)
                dve.tensor_reduce(row_top[:, k:k + 1], p_y[0:1, 0:D], AX_X, ALU.max).then_inc(row_max_ready, 1)
                dve.wait_ge(max_spread, k + 1)
                dve.tensor_scalar(q_step[:, k:k + 1], p_y[:, 256:257], MIN_RANGE, 1.0 / QP, ALU.max, ALU.mult)\
                    .then_inc(step_ready, 1)
                dve.wait_ge(step_ready, 2 * k + 1)
                dve.reciprocal(q_inv[:, k:k + 1], q_step[:, k:k + 1])
                dve.tensor_tensor(out_step[:, k:k + 1], w_step[:, k:k + 1], q_step[:, k:k + 1], ALU.mult)\
                    .then_inc(step_ready, 1)
                dve.wait_ge(step_ready, 2 * k + 2)

            all_max(0)
            for h in range(2):
                at = slice(h * F, (h + 1) * F)
                dve.tensor_scalar(q_round[:, 0, at], yT[:, at], q_inv[:, 0:1], ROUND, ALU.mult, ALU.add)\
                    .then_inc(y_rounded, 1)
                dve.wait_ge(y_rounded, h + 1)
                dve.tensor_scalar(y_q[:, at], q_round[:, 0, at], -ROUND, None, ALU.add).then_inc(y_q_ready, 1)
                if h == 0:
                    dve.tensor_scalar(gelu_bias[:, :], vec(V_B1, FB), out_step[:, 0:1], None, ALU.mult)\
                        .then_inc(gelu_bias_ready, 1)
            for k in range(2 * FB):
                h, f = k // FB, k % FB
                dve.wait_ge(gelu_ready, k + 1)
                dve.tensor_reduce(part_max[:, k:k + 1], ffn_h[:, f, h * F:(h + 1) * F], AX_X, ALU.max, apply_absolute_value=True)\
                    .then_inc(tile_max_ready, 1)
            dve.wait_ge(tile_max_ready, 2 * FB)
            dve.tensor_reduce(part_top[:, 1:2], part_max[:, :], AX_X, ALU.max).then_inc(part_max_ready, 1)
            all_max(1)
            for f in range(FB):
                dve.tensor_scalar(q_round[:, f, F:N], ffn_h[:, f, F:N], q_inv[:, 1:2], ROUND, ALU.mult, ALU.add)\
                    .then_inc(h_rounded_dve, 1)
            for f in range(FB):
                dve.wait_ge(h_rounded_dve, f + 1)
                last = dve.tensor_scalar(ffn_q[:, f, F:N], q_round[:, f, F:N], -ROUND, None, ALU.add)
            last.then_inc(ffn_q_ready, 1)
            for f in range(FB):
                dve.wait_ge(h_rounded_act, f + 1)
                last = dve.tensor_scalar(ffn_q[:, f, 0:F], q_round[:, f, 0:F], -ROUND, None, ALU.add)
            last.then_inc(ffn_q_ready, 1)
            dve.wait_ge(x1_kept, CHUNKS)
            for k, h in enumerate((1, 0)):
                at = slice(4 * h, 4 * h + 4)
                dve.wait_ge(ffn2_ready, k + 1)
                dve.tensor_tensor(o_sb[:, at, :], (p_gate, p_up)[h][:, :].rearrange("p (c d) -> p c d", c=4),
                                  ffn_b2.rearrange("p (a d) -> p a d", a=1).to_broadcast([D, 4, D]), ALU.add)\
                    .then_inc(out_biased, 1)
                dve.wait_ge(out_biased, k + 1)
                dve.scalar_tensor_tensor(out=o_sb[:, at, :], in0=o_sb[:, at, :], scalar=out_step[:, 1:2],
                                         in1=x1_tok[:, at, :], op0=ALU.mult, op1=ALU.add)\
                    .then_inc(out_ready, 1)

        @block.gpsimd
        def _(pool):
            def silu_half(c, s, half):
                chunk, e, _ = expert_of(c, s)
                if is_chunk(chunk):
                    j = chunk * E + e
                    at = slice(half * 256, half * 256 + 256)
                    pool.wait_ge(gate_read, 2 * j + half + 1)
                    wait_count(pool, hidden_ready, 2 * (j - 1) + half + 1)
                    pool.tensor_tensor(silu[:, at], gate_c[:, at], sig[:, at], ALU.mult).then_inc(silu_ready, 1)

            def slot(c, s):
                if isinstance(c, int) and c == 0 and s == 2:
                    pool.wait_ge(c_dve, 6)
                    pool.tensor_tensor(ln_rstd[:, :], ln_var[:, :], pow_half[:, :], ALU.pow).then_inc(c_pool, 1)
                if isinstance(c, int) and c == 1 and s == 0:
                    pool.wait_ge(wq_dve, 2)
                    pool.partition_all_reduce(w_amax[:, :], w_max[:, :], D, bass.bass_isa.ReduceOp.absmax)\
                        .then_inc(wq_pool, 1)
                if expert_of(c, s)[2] == 1:
                    silu_half(c, s, 0)
                    silu_half(c, s, 1)
                if has_l1(c, s):
                    count = c * STEPS + s - LAG
                    if isinstance(c, int) and count == 0:
                        pool.wait_ge(gain_ready, 2)
                    if s == LAG and not (isinstance(c, int) and c == 0):
                        pool.wait_ge(o_projected, c)
                    pool.wait_ge(state_ready[1], count + 1)
                    pool.tensor_tensor(gated[:, (s - LAG) % STEPS, :], state[1][:, (s + 1) % 2, 2:24:3],
                                       gain[:, :], ALU.mult).then_inc(gated_ready, 1)
                if s == START + 4 and is_chunk(c - 2):
                    pool.wait_ge(acc_ready, (c - 1) * E)
                    pool.tensor_copy(x1_tok[:, bass.ds(c - 2, 1), :].rearrange("p a d -> p (a d)"), acc[:, 1, :])\
                        .then_inc(x1_kept, 1)

            pool.memset(bias_raw[:, :, :, :], 0.0).then_inc(bias_cleared, 1)
            pool.memset(warm[:, :], 0.0)
            pool.memset(ones_bf[:, :], 1.0)
            pool.memset(ones_f[:, :], 1.0)
            pool.memset(pow_half[:, :], -0.5)
            pool.memset(batch_mask[:, :], 1.0)
            pool.memset(ident[:, :], 0.0).then_inc(const_ready, 1)
            pool.wait_ge(const_ready, 1)
            pool.affine_select(out=ident[:, :], in_=ident[:, :], compare_op=ALU.not_equal, fill=1.0, base=0,
                               pattern=[[-1, D]], channel_multiplier=1)
            pool.affine_select(out=batch_mask[:, :], in_=batch_mask[:, :], compare_op=ALU.is_ge, fill=0.0,
                               base=0, pattern=[[-R, B]], channel_multiplier=1).then_inc(iota_ready, 1)
            pool.wait_ge(iota_ready, 1)
            pool.affine_select(out=batch_mask[:, :], in_=batch_mask[:, :], compare_op=ALU.is_ge, fill=0.0,
                               base=R - 1, pattern=[[R, B]], channel_multiplier=-1)
            pool.iota(expert_no_i[:, :], pattern=[[1, E]], base=0, channel_multiplier=0).then_inc(iota_ready, 1)
            pool.wait_ge(iota_ready, 2)
            pool.tensor_copy(expert_no[:, :], expert_no_i[:, :]).then_inc(iota_ready, 1)
            for s in range(16):
                slot(0, s)
            for s in range(16):
                slot(1, s)
            with pool.Fori(2, CHUNKS) as c:
                for s in range(16):
                    slot(c, s)
            for s in range(16):
                slot(CHUNKS, s)
            for s in range(START + 6):
                slot(CHUNKS + 1, s)


def kernel(x, cond_1024, **w):
    import numpy as np
    from concourse import bacc
    from concourse.bass_utils import run_bass_kernel_spmd

    c = {k: np.asarray(v) for k, v in w.items()}
    x, cond = np.asarray(x), np.asarray(cond_1024)

    def col(v):
        return v.reshape(-1, D).T

    x_time = x.transpose(1, 0, 2).reshape(N, D)

    def gru(i):
        return np.stack([c[f"L0_cond_Wih{i}"].T, c[f"L0_cond_Whh{i}"].T], axis=1)

    arrays = {
        "xT": x_time.T,
        "x_tok": x_time.reshape(CHUNKS, TOK, D).transpose(1, 0, 2),
        "first": np.concatenate([
            c["L0_cond_W_in"].T, cond.T, col(c["L0_cond_b_in"]), col(c["L0_cond_b_gate"]),
            col(c["L0_cond_b_out"]), col(c["L1_cond_ln_g"]), col(c["L1_cond_ln_b"]), col(c["L1_cond_b1"]),
            col(c["L1_ffn_b1"]),
            c["L1_cond_b2"].reshape(2, D, R).transpose(1, 0, 2).reshape(D, 2 * R)], axis=1),
        "gru0": gru(0),
        "gru1": gru(1),
        "proj": np.concatenate([
            c["L0_cond_W_gate"].T, c["L0_cond_W_out"].T, c["L1_cond_w1"], c["L1_cond_base_layer"],
            c["L0_ffn_W_router"].T], axis=1),
        "gate_up": np.concatenate([c["L0_ffn_W_gate"].transpose(2, 0, 1), c["L0_ffn_W_up"].transpose(2, 0, 1)],
                                  axis=2),
        "down": c["L0_ffn_W_down"].reshape(E, D, FB, D).transpose(3, 0, 2, 1),
        "cond_rows": cond,
        "biases": np.stack([np.stack([c[f"L0_cond_bih{i}"], c[f"L0_cond_bhh{i}"]]) for i in range(2)])[None],
        "cond_w2": c["L1_cond_w2"].reshape(D, 2, D, R).transpose(0, 1, 3, 2).reshape(D, 2 * R, D),
        "ffn": np.concatenate([
            c["L1_ffn_w1"].T, c["L1_ffn_w2"].reshape(D, FB, D).transpose(2, 1, 0).reshape(D, F),
            np.broadcast_to(c["L1_ffn_b2"], (D, D))], axis=1),
    }
    nc = bacc.Bacc("TRN2", target_bir_lowering=False, num_devices=1)
    arrays = {k: np.ascontiguousarray(v) for k, v in arrays.items()}
    args = [nc.dram_tensor(k, a.shape, mybir.dt.from_np(a.dtype), kind="ExternalInput").ap()
            for k, a in arrays.items()]
    out = nc.dram_tensor("out", (TOK, CHUNKS, D), F32, kind="ExternalOutput").ap()
    build(nc, *args, out)
    got = run_bass_kernel_spmd(nc, [arrays], core_ids=[0]).results[0]["out"]
    return got.reshape(STEPS, B, CHUNKS, D).transpose(1, 2, 0, 3).reshape(B, T, D)
```

```python
from contextlib import ExitStack

import concourse.bass as bass
from concourse import mybir

ALU = mybir.AluOpType
ACT = mybir.ActivationFunctionType
F32 = mybir.dt.float32
F16 = mybir.dt.float16
BF16 = mybir.dt.bfloat16
AX_X = mybir.AxisListType.X

B = 8
T = 128
D = 128
E = 8
F = 512
FB = F // D
R = 8
STEPS = 16
TOK = STEPS * B
CHUNKS = T // STEPS
N = T * B
LAG = 5
GROUP = 4
SPAN = 2 * GROUP
SLOTS = T + LAG
START = 6
PIECE = 512
PIECES = 2 * F // PIECE
DOWN_SPLIT = (11, 13, 15, 17, 20, 23, 25, 27)
DRAIN_FROM = (CHUNKS - 1) * E - 1

W_SCALE = 2.0 ** 12
H_SCALE = 2.0 ** 14
GRU_UNSCALE = 1.0 / (W_SCALE * H_SCALE)
EW_SCALE = 2.0 ** 10
O_SCALE = 2.0 ** 8
MOE_UNSCALE = 1.0 / (EW_SCALE * O_SCALE)
DW_SCALE = 2.0 ** 5
ROUND = 1.5 * 2.0 ** 23
EPS = 1e-5
MIN_RANGE = 1e-6
QP = 127.0

assert LAG == GROUP + 1
PAD = (SPAN + 1) * B

V_BIN, V_BGATE, V_BOUT, V_LNG, V_LNB, V_CB1, V_B1, V_CB2 = 0, 1, 2, 3, 4, 5, 6, 10
VECS = 26
R_, Z_, N_ = 0, 1, 2
IH, HH = 0, 1


def wait_count(eng, semaphore, count):
    if not isinstance(count, int) or count > 0:
        eng.wait_ge(semaphore, count)


def expert_of(c, s):
    k = (s - START) % 16
    return (c - 1 if s >= START else c - 2), k // 2, k % 2


def experts_before(c, s, n):
    chunk, e, _ = expert_of(c, s)
    return (chunk, e - n) if e >= n else (chunk - 1, e - n + E)


def in_drain(chunk, e):
    return isinstance(chunk, int) and chunk * E + e >= DRAIN_FROM


def is_last(chunk, e):
    return isinstance(chunk, int) and chunk * E + e == CHUNKS * E - 1


def is_chunk(c):
    return not isinstance(c, int) or 0 <= c < CHUNKS


def has_l1(c, s):
    return not isinstance(c, int) or 0 <= c * STEPS + s - LAG < T


def active(c, s):
    return 0 if is_chunk(c) else 1, 2 if has_l1(c, s) else 1


def has_step(c, s):
    return is_chunk(c) or has_l1(c, s)


def place(s):
    return (s - 1) // SPAN % 2, (s - 1) % SPAN


def by_gate(weights):
    return weights[:, :, :].rearrange("p k (g d) -> p k g d", g=3)


def misc_before(c):
    return CHUNKS + (3 * c - 4 if c > 1 else 0) if isinstance(c, int) else c * 3 + (CHUNKS + 2 - 6)


def down_of(c, s):
    k = c * STEPS + s
    return (DOWN_SPLIT.index(k),) if k in DOWN_SPLIT else ()


def pieces_of(c, s):
    k = c * STEPS + s - 4
    return (k,) if 0 <= k < E * PIECES else ()


COND_PE = {-1: (0, 1), **{s: (2 * s - 14, 2 * s - 13) for s in range(8, 16)}, 17: (18,),
           18: (19,), 20: (20, 21), 21: (22,), 22: (23,), 24: (24, 25), 25: (26, 27)}
COND_DVE = {-1: (0, 1, 2), 16: (3,), 18: (4,), 22: (5,), 23: (6,), 26: (7, 8)}
COND_POOL = 19
BUSY = {s: 3 for s in range(17, 21)}
BUSY_Y_IN, BUSY_Y_BEHIND = 2, 4
BUSY_H_BEFORE, BUSY_H_IN, BUSY_H_BEHIND = 8, 2, 7
TIMES = [slice(0, T // 2), slice(T // 2, T)]
HALVES = [slice(0, 1), slice(1, 2)]
GELU_TILES = [(0, h) for h in HALVES] + [(f, slice(0, 2)) for f in range(1, FB - 1)] + [(FB - 1, h) for h in HALVES]
QUANT_DVE = {5: 0, 7: 1, 11: 2, 13: 3, 15: 4, 17: 5, 19: 6}
QUANT_POOL = 9
QUARTERS = (0, 1, 2, 3)


def build(nc, xT, x_tok, first, gru0, gru1, proj, gate_up, down, cond_rows, biases, cond_w2, ffn, out):
    with ExitStack() as ctx:
        def sb(name, shape, dt=F32):
            return ctx.enter_context(nc.sbuf_tensor(name, shape, dt))

        def sem(name):
            return ctx.enter_context(nc.semaphore(name))

        first_sb = sb("first_sb", [D, 2 * D + B + VECS])
        w_in = first_sb[:, 0:D]
        condT = first_sb[:, D:D + B]

        c_w1 = first_sb[:, D + B + VECS:]

        def vec(k, n=1):
            return first_sb[:, D + B + k:D + B + k + n]

        xT_sb = sb("xT_sb", [D, N])
        x1_tok = sb("x1_tok", [D, CHUNKS, D])
        gru_f = [sb(f"gru_f{i}", [D, 2, 3 * D]) for i in range(2)]
        proj_sb = sb("proj_sb", [D, 3 * D + E])
        w_gate, w_out, base = (proj_sb[:, k * D:(k + 1) * D] for k in range(3))
        w_router = proj_sb[:, 3 * D:3 * D + E]
        gu_f = sb("gu_f", [D, E, 2 * F])
        down_f = sb("down_f", [D, E, FB, D])
        cond_sb = sb("cond_sb", [B, D])
        bias_raw = sb("bias_raw", [D, 2, 3 * D])
        c_w2 = sb("c_w2", [D, 2 * R, D])
        ffn_sb = sb("ffn_sb", [D, 2 * F + D])
        ffn_b2 = ffn_sb[:, 2 * F:2 * F + D]

        ones_f = sb("ones_f", [1, D])
        ident = sb("ident", [D, D])
        batch_mask = sb("batch_mask", [B * R, B])
        expert_no = sb("expert_no", [D, E])
        expert_no_i = sb("expert_no_i", [D, E], mybir.dt.int32)
        pow_half = sb("pow_half", [B, 1])
        warm = sb("warm", [D, 1])

        gru_hi = [sb(f"gru_hi{i}", [D, 2, 3 * D], F16) for i in range(2)]
        gru_lo = [sb(f"gru_lo{i}", [D, 2, 3 * D], F16) for i in range(2)]
        bias_f = sb("bias_f", [D, 4 * D])
        bias_hi = sb("bias_hi", [D, 4 * D], F16)
        bias_parts = sb("bias_parts", [D, 4 * D], F16)
        bias_on = sb("bias_on", [D, 2, SPAN * B], F16)
        mix = sb("mix", [D, 2, TOK])
        mix_hi = sb("mix_hi", [D, N + PAD], F16)
        mix_lo = sb("mix_lo", [D, N + PAD], F16)
        factors = sb("factors", [D, 2, 2, 24])
        addends = sb("addends", [D, 2, 24])
        z_gate = sb("z_gate", [D, 2, B])
        state = sb("state", [D, 2, 2, 24])
        parts = sb("parts", [D, 2 * GROUP, 2, 24], F16)
        gated = sb("gated", [D, STEPS, B])
        cond_gate = sb("cond_gate", [D, B])
        gain = sb("gain", [D, B])

        gu_hi = sb("gu_hi", [D, E, 2 * F], F16)
        gu_lo = sb("gu_lo", [D, E, 2 * F], F16)
        oT = sb("oT", [D, TOK])
        o_hi = sb("o_hi", [D, N], F16)
        o_lo = sb("o_lo", [D, N], F16)
        logits = sb("logits", [D, E])
        top8 = sb("top8", [D, 8])
        top8_at = sb("top8_at", [D, 8], mybir.dt.uint32)
        top8_no = sb("top8_no", [D, 8])
        top_gap = sb("top_gap", [D, 1])
        top_w = sb("top_w", [D, 2])
        share = sb("share", [D, 2, E])
        shares = sb("shares", [D, E])
        sig = sb("sig", [D, 2, F])
        gate_c = sb("gate_c", [D, 2, F])
        silu = sb("silu", [D, 2, F])
        hidden = sb("hidden", [D, 2, F])
        hidden_hi = sb("hidden_hi", [D, 2, F], F16)
        hidden_lo = sb("hidden_lo", [D, 2, F], F16)
        down_hi = sb("down_hi", [D, E, FB, D], F16)
        down_lo = sb("down_lo", [D, E, FB, D], F16)
        acc = sb("acc", [D, 2, D])
        x1T = sb("x1T", [D, N])

        ln_sum = sb("ln_sum", [B, 1])
        ln_x = sb("ln_x", [B, D])
        ln_sq = sb("ln_sq", [B, D])
        ln_var = sb("ln_var", [B, 1])
        ln_rstd = sb("ln_rstd", [B, 1])
        ae = sb("ae", [D, B])
        ch = sb("ch", [D, B])
        ab = sb("ab", [D, 2, B, R])
        ab_T = sb("ab_T", [B * R, 2 * D])
        base_id = sb("base_id", [D, D])
        b_T = sb("b_T", [B * R, B, D])
        layer = sb("layer", [D, B, D])

        w_max = sb("w_max", [D, 2])
        w_amax = sb("w_amax", [D, 2])
        w_step = sb("w_step", [D, 2])
        w_inv = sb("w_inv", [D, 2])
        w_round = sb("w_round", [D, 2, F])
        w_q = sb("w_q", [D, 2, F], BF16)
        y_round = down_f[:, 4:6, :, :].rearrange("p e f d -> p (e f) d")
        y_q = sb("y_q", [D, B, T], BF16)
        ffn_h = gu_f[:, 0:FB, :]
        q_round = gu_f[:, FB:2 * FB, :]
        ffn_q = sb("ffn_q", [D, FB, N], BF16)
        part_max = sb("part_max", [D, len(GELU_TILES)])
        y_max = sb("y_max", [D, 2 * B])
        part_top = sb("part_top", [D, 2])
        row_top = sb("row_top", [1, 2])
        q_step = sb("q_step", [D, 2])
        q_inv = sb("q_inv", [D, 2])
        out_step = sb("out_step", [D, 2])
        gelu_bias = sb("gelu_bias", [D, FB])
        b2_step = sb("b2_step", [D, D])
        x1_b2 = down_f[:, 2:4, :, :].rearrange("p e f d -> p (e f) d")
        o_sb = down_f[:, 0:2, :, :].rearrange("p e f d -> p (e f) d")

        p_rz = ctx.enter_context(nc.psum_tensor("p_rz", [D, 2, 512], F32))
        p_n = ctx.enter_context(nc.psum_tensor("p_n", [D, 2, 512], F32))
        rz_at = p_rz[:, :, 0:32 * SPAN].rearrange("p k (t g l b) -> p k t g l b", g=2, l=2, b=B)
        n_at = p_n[:, :, 0:48 * SPAN].rearrange("p k (t l b a) -> p k t l b a", l=2, b=B, a=3)
        PRE = 48 * SPAN
        p_gu = ctx.enter_context(nc.psum_tensor("p_gu", [D, 2, 512], F32))
        p_ym = ctx.enter_context(nc.psum_tensor("p_ym", [D, 2, 512], F32))
        p_gate, p_up, p_y, p_misc = p_gu[:, 0, :], p_gu[:, 1, :], p_ym[:, 0, :], p_ym[:, 1, :]
        mix_banks = [p_misc, p_up]
        y_banks = p_rz[:, :, :].rearrange("p k (b t) -> p (k b) t", t=T)
        ffn1_banks = [p_gu, p_n, p_ym, p_rz]
        ffn2_banks = [p_rz[:, 0, :], p_rz[:, 1, :], p_n[:, 0, :], p_n[:, 1, :]]

        got = {k: sem(f"got_{k}") for k in
               ("first", "x0", "x", "gru0", "gru1", "proj", "cond", "c_w2", "ffn", "x_tok", "bias", "down")}
        got_gu = [sem(f"got_gu{e}") for e in range(E)]
        bias_cleared = sem("bias_cleared")
        const_ready = sem("const_ready")
        iota_ready = sem("iota_ready")
        split_hi = sem("split_hi")
        split_lo = sem("split_lo")
        bias_scaled = sem("bias_scaled")
        bias_step = sem("bias_step")
        cleared = sem("cleared")
        init_done = sem("init_done")
        gate_done = sem("gate_done")
        gain_ready = sem("gain_ready")
        misc_written = sem("misc_written")
        misc_taken = sem("misc_taken")
        mix_hi_ready = sem("mix_hi_ready")
        mix_ready = sem("mix_ready")
        rz_ready = sem("rz_ready")
        nsum_ready = sem("nsum_ready")
        gates_ready = sem("gates_ready")
        z_ready = sem("z_ready")
        pre_ready = sem("pre_ready")
        kept_ready = sem("kept_ready")
        cand_ready = sem("cand_ready")
        hi_ready = sem("hi_ready")
        state_ready = sem("state_ready")
        lo_ready = sem("lo_ready")
        gated_ready = sem("gated_ready")
        o_projected = sem("o_projected")
        o_hi_ready = sem("o_hi_ready")
        o_lo_ready = sem("o_lo_ready")
        logits_ready = sem("logits_ready")
        router_step = sem("router_step")
        gap_ready = sem("gap_ready")
        top_w_ready = sem("top_w_ready")
        gu_hi_ready = sem("gu_hi_ready")
        gu_lo_ready = sem("gu_lo_ready")
        gate_ready = sem("gate_ready")
        up_ready = sem("up_ready")
        gate_read = sem("gate_read")
        silu_ready = sem("silu_ready")
        last_silu_ready = sem("last_silu_ready")
        hidden_ready = sem("hidden_ready")
        hidden_hi_ready = sem("hidden_hi_ready")
        hidden_lo_pool = sem("hidden_lo_pool")
        hidden_lo_dve = sem("hidden_lo_dve")
        down_scaled = sem("down_scaled")
        down_hi_ready = sem("down_hi_ready")
        down_lo_ready = sem("down_lo_ready")
        y_ready = sem("y_ready")
        acc_ready = sem("acc_ready")
        x1_transposed = sem("x1_transposed")
        x1_kept = sem("x1_kept")
        c_dve = sem("c_dve")
        c_pe = sem("c_pe")
        c_act = sem("c_act")
        c_pool = sem("c_pool")
        wq_dve = sem("wq_dve")
        wq_pool = sem("wq_pool")
        layer_applied = sem("layer_applied")
        y_max_ready = sem("y_max_ready")
        part_max_ready = sem("part_max_ready")
        max_turned = sem("max_turned")
        row_max_ready = sem("row_max_ready")
        max_spread = sem("max_spread")
        q_step_ready = sem("q_step_ready")
        step_ready = sem("step_ready")
        y_rounded_act = sem("y_rounded_act")
        y_rounded_dve = sem("y_rounded_dve")
        y_q_ready = sem("y_q_ready")
        gelu_bias_ready = sem("gelu_bias_ready")
        ffn1_ready = sem("ffn1_ready")
        gelu_ready = sem("gelu_ready")
        tile_max_ready = sem("tile_max_ready")
        h_rounded_act = sem("h_rounded_act")
        h_rounded_dve = sem("h_rounded_dve")
        q_ready_act = sem("q_ready_act")
        q_ready_dve = sem("q_ready_dve")
        b2_ready = sem("b2_ready")
        x1_b2_ready = sem("x1_b2_ready")
        ffn2_ready = sem("ffn2_ready")
        out_ready = sem("out_ready")
        out_stored = sem("out_stored")

        block = ctx.enter_context(nc.Block())

        @block.sync
        def _(sp):
            sp.dma_start(cond_sb[:, :], cond_rows).then_inc(got["cond"], 16)
            sp.dma_start(first_sb[:, :], first).then_inc(got["first"], 16)
            sp.dma_start(xT_sb[:, 0:TOK], xT[:, 0:TOK]).then_inc(got["x0"], 16)
            sp.dma_start(gru_f[0][:, :, :], gru0).then_inc(got["gru0"], 16)
            sp.wait_ge(bias_cleared, 1)
            for p in (0, D // 2):
                sp.dma_start(bias_raw[p:p + 33:32, :, :], biases).then_inc(got["bias"], 16)
            sp.dma_start(xT_sb[:, TOK:N], xT[:, TOK:N]).then_inc(got["x"], 16)
            sp.dma_start(gru_f[1][:, :, :], gru1).then_inc(got["gru1"], 16)
            sp.dma_start(proj_sb[:, :], proj).then_inc(got["proj"], 16)
            sp.dma_start(c_w2[:, :, :], cond_w2).then_inc(got["c_w2"], 16)
            for e in range(2):
                sp.dma_start(gu_f[:, e, :], gate_up[:, e, :]).then_inc(got_gu[e], 16)
            sp.dma_start(ffn_sb[:, :], ffn).then_inc(got["ffn"], 16)
            for e in range(2, E):
                if e == E // 2:
                    sp.dma_start(down_f[:, :, :, :], down).then_inc(got["down"], 16)
                sp.dma_start(gu_f[:, e, :], gate_up[:, e, :]).then_inc(got_gu[e], 16)
            sp.dma_start(x1_tok[:, :, :], x_tok).then_inc(got["x_tok"], 16)
            for k, q in enumerate(QUARTERS):
                at = slice(2 * q, 2 * q + 2)
                sp.wait_ge(out_ready, k + 1)
                sp.dma_start(out[:, at, :], o_sb[:, at, :]).then_inc(out_stored, 16)
            sp.wait_ge(out_stored, 16 * len(QUARTERS))

        @block.tensor
        def _(pe):
            def prefill(layer_no, s, slots, moving_hi, moving_lo, first):
                bank_no, at = place(s)
                hi, lo, on = gru_hi[layer_no], gru_lo[layer_no], bias_on[:, layer_no, 0:slots * B]
                for g in (R_, Z_, N_):
                    if g == N_:
                        dst = n_at[:, bank_no, at:at + slots, layer_no, :, 2]
                    else:
                        dst = rz_at[:, bank_no, at:at + slots, g, layer_no, :]
                    pe.matmul(dst, bias_parts[:, g * D:(g + 1) * D], on,
                              start=first and g in (R_, N_), stop=False, skip_group_check=True)
                    w = slice(g * D, (g + 1) * D)
                    pe.matmul(dst, hi[:, IH, w], moving_hi, start=False, stop=False, skip_group_check=True)
                    pe.matmul(dst, lo[:, IH, w], moving_hi, start=False, stop=False, skip_group_check=True)
                    pe.matmul(dst, hi[:, IH, w], moving_lo, start=False, stop=False, skip_group_check=True)
                pe.matmul(n_at[:, bank_no, at:at + slots, layer_no, :, 0], bias_parts[:, 3 * D:4 * D],
                          on, start=False, stop=False, skip_group_check=True)

            def input0(c, s, slots):
                at = bass.ds(c * TOK + s * B, slots * B)
                prefill(0, s, slots, mix_hi[:, at], mix_lo[:, at], True)

            def input1(c, s):
                k = c * STEPS + s
                if isinstance(c, int) and k == LAG:
                    pe.wait_ge(split_lo, 2)
                if place(s)[1]:
                    pe.wait_ge(z_ready, k)
                    pe.wait_ge(cand_ready, k)
                ring = (s - LAG) % (2 * GROUP)
                h = parts[:, ring:ring + GROUP, 0, :]
                prefill(1, s, GROUP, h[:, :, 2:24:3], h[:, :, 1:24:3], False)

            def step(c, s):
                k, ring = c * STEPS + s, (s - 1) % (2 * GROUP)
                bank_no, at = place(s)
                layers = range(*active(c, s))
                wait_count(pe, hi_ready, k)
                for i in layers:
                    h_hi = parts[:, ring, i, 2:24:3]
                    for g in (R_, Z_):
                        for w in (gru_hi[i], gru_lo[i]):
                            pe.matmul(rz_at[:, bank_no, at, g, i, :], w[:, HH, g * D:(g + 1) * D], h_hi,
                                      start=False, stop=False, skip_group_check=True)
                    pe.matmul(n_at[:, bank_no, at, i, :, 0], gru_lo[i][:, HH, 2 * D:3 * D], h_hi,
                              start=False, stop=False, skip_group_check=True)
                wait_count(pe, lo_ready, k)
                for i in layers:
                    for g in (R_, Z_):
                        last = pe.matmul(rz_at[:, bank_no, at, g, i, :],
                                         gru_hi[i][:, HH, g * D:(g + 1) * D], parts[:, ring, i, 1:24:3],
                                         start=False, stop=False, skip_group_check=True)
                last.then_inc(rz_ready, 1)
                for i in layers:
                    both = parts[:, ring, i, :].rearrange("p (b k) -> p b k", k=3)[:, :, 1:3]
                    last = pe.matmul(n_at[:, bank_no, at, i, :, 0:2], gru_hi[i][:, HH, 2 * D:3 * D], both,
                                     start=False, stop=False, skip_group_check=True)
                last.then_inc(nsum_ready, 1)

            def mixed(k):
                wait_count(pe, misc_taken, k - 1)
                dst = mix_banks[k % 2][:, 0:TOK]
                pe.matmul(dst, w_in, xT_sb[:, k * TOK:(k + 1) * TOK], start=True, stop=False)
                pe.matmul(dst.rearrange("p (t b) -> p t b", b=B), ident[:, :],
                          condT.rearrange("p (a b) -> p a b", a=1).to_broadcast([D, STEPS, B]),
                          start=False, stop=True).then_inc(misc_written, 1)

            def expert_products(which, c, s):
                chunk, e, _ = expert_of(c, s)
                if not is_chunk(chunk):
                    return
                bank_, ready = (p_gate, gate_ready) if which == 0 else (p_up, up_ready)
                j = chunk * E + e
                x_hi, x_lo = o_hi[:, bass.ds(chunk * TOK, TOK)], o_lo[:, bass.ds(chunk * TOK, TOK)]
                if which == 0:
                    if e == 0:
                        pe.wait_ge(o_lo_ready, chunk + 1)
                    if isinstance(chunk, int) and chunk == 0:
                        pe.wait_ge(gu_lo_ready, PIECES * (e + 1))
                    wait_count(pe, gate_read, j)
                else:
                    wait_count(pe, hidden_ready, j)
                for f, product in ((n // 3, n % 3) for n in range(3 * FB)):
                    w = slice(which * F + f * D, which * F + (f + 1) * D)
                    last = pe.matmul(bank_[:, f * D:(f + 1) * D], (gu_hi, gu_lo, gu_hi)[product][:, e, w],
                                     (x_hi, x_hi, x_lo)[product], start=product == 0, stop=product == 2)
                last.then_inc(ready, 1)

            def down_proj(c, s, before, blocks):
                chunk, e = experts_before(c, s, before)
                if is_chunk(chunk):
                    j = chunk * E + e
                    bank = p_y
                    if is_last(chunk, e):
                        bank = p_gate
                        pe.wait_ge(gate_read, CHUNKS * E)
                    elif blocks[0] == 0:
                        wait_count(pe, acc_ready, j)
                    if blocks[0] == 0:
                        pe.wait_ge(hidden_hi_ready, j + 1)
                        if in_drain(chunk, e):
                            pe.wait_ge(hidden_lo_dve, j - DRAIN_FROM + 1)
                        else:
                            pe.wait_ge(hidden_lo_pool, j + 1)
                        if isinstance(chunk, int) and chunk == 0:
                            pe.wait_ge(down_lo_ready, e + 1)
                            if e == 0:
                                pe.wait_ge(c_dve, 16)
                    for f in blocks:
                        at = slice(f * D, (f + 1) * D)
                        pe.matmul(bank[:, 0:D], hidden_hi[:, e % 2, at], down_hi[:, e, f, :],
                                  start=f == 0, stop=False)
                        pe.matmul(bank[:, 0:D], hidden_hi[:, e % 2, at], down_lo[:, e, f, :],
                                  start=False, stop=False)
                        last = pe.matmul(bank[:, 0:D], hidden_lo[:, e % 2, at], down_hi[:, e, f, :],
                                         start=False, stop=f == FB - 1)
                    if blocks[-1] == FB - 1:
                        last.then_inc(y_ready, 1)

            def cond_step(n):
                if n == 0:
                    pe.wait_ge(c_dve, 7)
                    pe.transpose(p_gate[:, 0:B], ln_x[:, :], ident[0:B, 0:B]).then_inc(c_pe, 1)
                elif n == 1:
                    pe.wait_ge(c_dve, 8)
                    pe.matmul(p_gate[:, 0:B], c_w1, ae[:, :], start=True, stop=True).then_inc(c_pe, 1)
                elif n < 18:
                    k = n - 2
                    if k == 0:
                        pe.wait_ge(c_act, 1)
                        pe.wait_ge(got["c_w2"], 16)
                    at = (k // R) * B * R + k % R
                    pe.matmul(p_gate[:, at:at + B * R - R + 1:R], c_w2[:, k, :], ch[:, :],
                              start=True, stop=True).then_inc(c_pe, 1)
                elif n < 20:
                    k = n - 18
                    if k == 0:
                        pe.wait_ge(c_dve, 10)
                    pe.transpose(p_y[0:B * R, k * D:(k + 1) * D],
                                 ab[:, k, :, :].rearrange("p b r -> p (b r)"), ident[:, :]).then_inc(c_pe, 1)
                else:
                    b = n - 20
                    if b == 0:
                        pe.wait_ge(c_pool, 2)
                    if b == 4:
                        pe.wait_ge(c_dve, 14)
                    pe.matmul(p_y[:, b % 4 * D:(b % 4 + 1) * D], ab_T[:, 0:D], b_T[:, b, :],
                              start=True, stop=True).then_inc(c_pe, 1)

            def apply_layer():
                pe.wait_ge(misc_taken, misc_before(CHUNKS + 1))
                pe.wait_ge(c_dve, 16)
                for b in range(B):
                    last = pe.matmul(y_banks[:, b, 0:T - STEPS], layer[:, b, :], x1T[:, b:N - TOK:B],
                                     start=True, stop=True)
                    if b % 4 == 3:
                        last.then_inc(layer_applied, 1)

            def keep_busy(n, bank):
                for _ in range(n):
                    pe.matmul(bank, bias_parts[:, 0:D], bias_parts[:, :], start=True, stop=True)

            def slot(c, s):
                if has_step(c, s):
                    step(c, s)
                if isinstance(c, int) and c < 2:
                    keep_busy(BUSY.get(c * STEPS + s, 0), p_up)
                if isinstance(c, int) and c == 0 and s == 0:
                    input0(0, 1, SPAN)
                if is_chunk(c) and s % SPAN == SPAN - 2:
                    if isinstance(c, int) and s == SPAN - 2:
                        pe.wait_ge(mix_ready, 2 if c == 0 else CHUNKS)
                    input0(c, s + 3, SPAN)
                if isinstance(c, int) and c == 0:
                    if s == 1:
                        pe.wait_ge(got["x"], 16)
                    if s == 2:
                        pe.wait_ge(got["proj"], 16)
                        pe.matmul(p_y[:, 0:B], w_gate, condT, start=True, stop=True).then_inc(gate_done, 1)
                    if 1 <= s < CHUNKS:
                        mixed(s)
                if s == LAG and is_chunk(c - 1):
                    pe.wait_ge(gated_ready, c * STEPS)
                    pe.wait_ge(misc_taken, misc_before(c))
                    pe.matmul(p_misc[:, 0:TOK], w_out, gated[:, :, :].rearrange("p t b -> p (t b)"),
                              start=True, stop=True).then_inc(o_projected, 1)
                if s == START and is_chunk(c - 1):
                    pe.wait_ge(misc_taken, misc_before(c) + 1)
                    pe.matmul(p_misc[:, 0:E], oT[:, :], w_router, start=True, stop=True)\
                        .then_inc(logits_ready, 1)
                if s == START + 6 and is_chunk(c - 2):
                    pe.wait_ge(acc_ready, (c - 1) * E)
                    pe.wait_ge(misc_taken, misc_before(c) + (2 if is_chunk(c - 1) else 0))
                    pe.transpose(p_misc[:, 0:D], acc[:, 1, :], ident[:, :]).then_inc(x1_transposed, 1)
                if expert_of(c, s)[2] == 0:
                    expert_products(0, c, s)
                    down_proj(c, s, 3, (0,))
                else:
                    down_proj(c, s, 3, (1, 2, 3))
                    if isinstance(c, int) and c == CHUNKS + 1 and s == START + 1:
                        apply_layer()
                    expert_products(1, c, s)
                if isinstance(c, int) and c < 2:
                    for n in COND_PE.get(c * STEPS + s, ()):
                        cond_step(n)
                if has_l1(c, s + 1) and (s + 1) % GROUP == LAG % GROUP:
                    input1(c, s + 1)

            pe.wait_ge(iota_ready, 1)
            pe.wait_ge(got["first"], 16)
            pe.wait_ge(got["x0"], 16)
            mixed(0)
            for n in COND_PE[-1]:
                cond_step(n)
            pe.wait_ge(init_done, 1)
            pe.wait_ge(split_lo, 1)
            pe.wait_ge(bias_step, 3)
            pe.wait_ge(mix_ready, 1)
            input0(0, 0, 1)
            for s in range(16):
                slot(0, s)
            for s in range(16):
                slot(1, s)
            with pe.Fori(2, CHUNKS) as c:
                for s in range(16):
                    slot(c, s)
            for s in range(16):
                slot(CHUNKS, s)
            for s in range(START + 7):
                slot(CHUNKS + 1, s)

            pe.wait_ge(misc_taken, misc_before(CHUNKS + 1) + 1)
            pe.wait_ge(y_max_ready, 2)
            for b in range(B):
                last = pe.matmul(y_banks[:, b, T - STEPS:T], layer[:, b, :], x1T[:, N - TOK + b:N:B],
                                 start=True, stop=True)
            last.then_inc(layer_applied, 1)

            def all_max(k, busy, bank):
                pe.wait_ge(part_max_ready, k + 1)
                pe.transpose(p_y[0:1, 0:D], part_top[:, k:k + 1], ident[:, :]).then_inc(max_turned, 1)
                keep_busy(busy, bank)
                pe.wait_ge(row_max_ready, k + 1)
                pe.matmul(p_y[:, 256:257], ones_f[:, :], row_top[:, k:k + 1], start=True, stop=True)\
                    .then_inc(max_spread, 1)

            all_max(0, BUSY_Y_IN, p_n[:, 1, :])
            keep_busy(BUSY_Y_BEHIND, p_n[:, 1, :])
            y_by_time = y_q[:, :, :].rearrange("p b t -> p t b")
            for f in range(FB):
                for h in range(2):
                    if f == 0:
                        pe.wait_ge(y_q_ready, h + 1)
                    last = pe.matmul(ffn1_banks[f][:, h, :].rearrange("p (t b) -> p t b", b=B),
                                     w_q[:, 0, f * D:(f + 1) * D], y_by_time[:, h * T // 2:(h + 1) * T // 2, :],
                                     start=True, stop=True)
                    last.then_inc(ffn1_ready, 1)
            pe.wait_ge(gelu_ready, len(HALVES) + 1)
            keep_busy(BUSY_H_BEFORE, p_n[:, 1, :])
            all_max(1, BUSY_H_IN, p_n[:, 1, :])
            keep_busy(BUSY_H_BEHIND, p_n[:, 1, :])
            for q in QUARTERS:
                if q < 3:
                    pe.wait_ge(q_ready_dve, q + 1)
                else:
                    pe.wait_ge(q_ready_act, 1)
                for k in range(2):
                    at = slice((2 * q + k) * TOK, (2 * q + k + 1) * TOK)
                    for f in range(FB):
                        last = pe.matmul(ffn2_banks[q][:, k * D:(k + 1) * D], ffn_q[:, f, at],
                                         w_q[:, 1, f * D:(f + 1) * D], start=f == 0, stop=f == FB - 1)
                last.then_inc(ffn2_ready, 1)

        @block.scalar
        def _(act):
            def gru(c, s):
                k, (bank_no, at) = c * STEPS + s, place(s)
                l0, l1 = active(c, s)
                act.wait_ge(rz_ready, k + 1)
                act.activation(factors[:, :, l0:l1, 2:24:3], rz_at[:, bank_no, at, :, l0:l1, :],
                               ACT.Sigmoid, scale=GRU_UNSCALE).then_inc(gates_ready, 1)
                wait_count(act, kept_ready, k)
                act.activation(z_gate[:, l0:l1, :], rz_at[:, bank_no, at, Z_, l0:l1, :],
                               ACT.Sigmoid, scale=-GRU_UNSCALE).then_inc(z_ready, 1)
                act.wait_ge(pre_ready, k + 1)
                act.activation(addends[:, l0:l1, 0:24:3],
                               p_n[:, bank_no, PRE + 24 * l0 + 2:PRE + 24 * l1:3], ACT.Tanh,
                               scale=GRU_UNSCALE).then_inc(cand_ready, 1)

            def mixed(k):
                act.wait_ge(misc_written, k + 1)
                wait_count(act, mix_ready, k - 1)
                act.activation(mix[:, k % 2, :], mix_banks[k % 2][:, 0:TOK], ACT.Tanh, bias=vec(V_BIN))\
                    .then_inc(misc_taken, 1)
                act.wait_ge(misc_taken, k + 1)
                act.activation(mix_hi[:, k * TOK:(k + 1) * TOK], mix[:, k % 2, :], ACT.Copy,
                               scale=H_SCALE).then_inc(mix_hi_ready, 1)

            def split_weights(layer_no):
                for gates, sign in ((slice(0, 3, 2), 1.0), (slice(1, 2), -1.0)):
                    last = act.activation(by_gate(gru_hi[layer_no])[:, :, gates, :],
                                          by_gate(gru_f[layer_no])[:, :, gates, :], ACT.Copy,
                                          scale=sign * W_SCALE)
                last.then_inc(split_hi, 1)

            def split_expert(piece):
                e, q = piece // PIECES, piece % PIECES
                at = slice(q * PIECE, (q + 1) * PIECE)
                if q == 0:
                    act.wait_ge(got_gu[e], 16)
                act.activation(gu_hi[:, e, at], gu_f[:, e, at], ACT.Copy,
                               scale=EW_SCALE).then_inc(gu_hi_ready, 1)

            def split_down(e):
                act.wait_ge(down_scaled, e + 1)
                act.activation(down_hi[:, e, :, :], down_f[:, e, :, :], ACT.Copy).then_inc(down_hi_ready, 1)

            def out_of_gate(c, s):
                chunk, e, part = expert_of(c, s)
                if is_chunk(chunk):
                    j = chunk * E + e
                    if part == 0:
                        act.wait_ge(gate_ready, j + 1)
                        wait_count(act, silu_ready, j - 1)
                        act.activation(sig[:, e % 2, :], p_gate[:, :], ACT.Sigmoid, scale=MOE_UNSCALE)
                    else:
                        act.activation(gate_c[:, e % 2, :], p_gate[:, :], ACT.Copy, scale=MOE_UNSCALE)\
                            .then_inc(gate_read, 1)

            def high_of_hidden(c, s):
                chunk, e = experts_before(c, s, 2)
                if is_chunk(chunk):
                    j = chunk * E + e
                    act.wait_ge(hidden_ready, j + 1)
                    wait_count(act, y_ready, j - 1)
                    act.activation(hidden_hi[:, e % 2, :], hidden[:, e % 2, :], ACT.Copy)\
                        .then_inc(hidden_hi_ready, 1)

            def slot(c, s):
                if has_step(c, s):
                    gru(c, s)
                if s == LAG and is_chunk(c - 1):
                    act.wait_ge(o_projected, c)
                    if not (isinstance(c, int) and c == 1):
                        act.wait_ge(logits_ready, c - 1)
                        act.wait_ge(o_lo_ready, c - 1)
                    act.activation(oT[:, :], p_misc[:, 0:TOK], ACT.Identity, bias=vec(V_BOUT))\
                        .then_inc(misc_taken, 1)
                    act.wait_ge(misc_taken, misc_before(c) + 1)
                    act.activation(o_hi[:, bass.ds((c - 1) * TOK, TOK)], oT[:, :], ACT.Copy, scale=O_SCALE)\
                        .then_inc(o_hi_ready, 1)
                if s == START + 2 and is_chunk(c - 1):
                    act.wait_ge(gap_ready, c)
                    act.activation(top_w[:, 0:1], top_gap[:, :], ACT.Sigmoid, scale=-1.0)
                    act.activation(top_w[:, 1:2], top_gap[:, :], ACT.Sigmoid).then_inc(top_w_ready, 1)
                if expert_of(c, s)[2] == 0:
                    high_of_hidden(c, s)
                out_of_gate(c, s)
                if s == START + 6 and is_chunk(c - 2):
                    act.wait_ge(x1_transposed, c - 1)
                    act.activation(x1T[:, bass.ds((c - 2) * TOK, TOK)], p_misc[:, 0:TOK], ACT.Copy)\
                        .then_inc(misc_taken, 1)
                if isinstance(c, int) and c < 2:
                    if c == 0 and 2 <= s <= CHUNKS:
                        mixed(s - 1)
                    if c == 0 and s == 1:
                        act.wait_ge(got["gru1"], 16)
                        split_weights(1)
                    if c == 0 and s == 3:
                        act.wait_ge(gate_done, 1)
                        act.activation(cond_gate[:, :], p_y[:, 0:B], ACT.Sigmoid, bias=vec(V_BGATE))\
                            .then_inc(gain_ready, 1)
                    for piece in pieces_of(c, s):
                        split_expert(piece)
                    for e in down_of(c, s):
                        split_down(e)

            act.wait_ge(const_ready, 1)
            act.activation(warm[:, :], warm[:, :], ACT.Gelu)
            act.wait_ge(got["gru0"], 16)
            split_weights(0)
            act.wait_ge(got["first"], 16)
            mixed(0)
            act.wait_ge(c_pe, 2)
            act.activation(ch[:, :], p_gate[:, 0:B], ACT.Gelu, bias=vec(V_CB1)).then_inc(c_act, 1)
            act.activation(warm[:, :], warm[:, :], ACT.Sigmoid)
            act.wait_ge(init_done, 1)
            for s in range(16):
                slot(0, s)
            for s in range(16):
                slot(1, s)
            with act.Fori(2, CHUNKS) as c:
                for s in range(16):
                    slot(c, s)
            for s in range(16):
                slot(CHUNKS, s)
            for s in range(START + 7):
                slot(CHUNKS + 1, s)

            act.activation(warm[:, :], warm[:, :], ACT.Gelu)
            act.wait_ge(step_ready, 1)
            for times in TIMES:
                act.activation(y_round[:, B // 2:B, times], y_banks[:, B // 2:B, times], ACT.Copy,
                               scale=q_inv[:, 0:1], bias=ROUND).then_inc(y_rounded_act, 1)
            act.wait_ge(gelu_bias_ready, 1)
            for k, (f, halves) in enumerate(GELU_TILES):
                act.wait_ge(ffn1_ready, 2 * f + halves.stop)
                act.activation(ffn_h[:, f, halves.start * F:halves.stop * F].rearrange("p (h n) -> p h n", n=F),
                               ffn1_banks[f][:, halves, :], ACT.Gelu,
                               scale=out_step[:, 0:1], bias=gelu_bias[:, f:f + 1]).then_inc(gelu_ready, 1)
            act.wait_ge(step_ready, 3)
            for k, q in enumerate((2, 3)):
                at = slice(q * N // 4, (q + 1) * N // 4)
                act.activation(q_round[:, :, at], ffn_h[:, :, at], ACT.Copy,
                               scale=q_inv[:, 1:2], bias=ROUND).then_inc(h_rounded_act, 1)
            act.wait_ge(h_rounded_act, 2)
            act.activation(ffn_q[:, :, at], q_round[:, :, at], ACT.Copy, bias=-ROUND).then_inc(q_ready_act, 1)

        @block.vector
        def _(dve):
            def gru(c, s, between):
                k, buf, ring, (bank_no, at) = c * STEPS + s, s % 2, s % (2 * GROUP), place(s)
                l0, l1 = active(c, s)

                def flat(x):
                    return x[:, l0:l1, :].rearrange("p l k -> p (l k)")

                dve.wait_ge(gates_ready, k + 1)
                dve.wait_ge(nsum_ready, k + 1)
                dve.tensor_tensor_scan(p_n[:, bank_no, PRE + 24 * l0:PRE + 24 * l1], flat(factors[:, 0, :, :]),
                                       p_n[:, bank_no, 48 * at + 24 * l0:48 * at + 24 * l1],
                                       0.0, ALU.mult, ALU.add).then_inc(pre_ready, 1)
                dve.wait_ge(z_ready, k + 1)
                dve.tensor_tensor(addends[:, l0:l1, 2:24:3], z_gate[:, l0:l1, :],
                                  state[:, buf, l0:l1, 2:24:3], ALU.mult).then_inc(kept_ready, 1)
                between()
                dve.wait_ge(kept_ready, k + 1)
                dve.wait_ge(cand_ready, k + 1)
                dve.tensor_tensor_scan(flat(parts[:, ring, :, :]), flat(factors[:, 1, :, :]),
                                       flat(addends[:, :, :]), 0.0, ALU.mult, ALU.add).then_inc(hi_ready, 1)
                if has_l1(c, s):
                    wait_count(dve, gated_ready, k - LAG - 1)
                dve.tensor_tensor_scan(flat(state[:, 1 - buf, :, :]), flat(factors[:, 1, :, :]),
                                       flat(addends[:, :, :]), 0.0, ALU.mult, ALU.add).then_inc(state_ready, 1)
                dve.wait_ge(state_ready, k + 1)
                dve.tensor_tensor(parts[:, ring, l0:l1, 1:24:3], state[:, 1 - buf, l0:l1, 2:24:3],
                                  parts[:, ring, l0:l1, 2:24:3], ALU.subtract).then_inc(lo_ready, 1)

            def mixed_lo(k):
                dve.wait_ge(mix_hi_ready, k + 1)
                cols = slice(k * TOK, (k + 1) * TOK)
                dve.scalar_tensor_tensor(out=mix_lo[:, cols], in0=mix[:, k % 2, :], scalar=H_SCALE,
                                         in1=mix_hi[:, cols], op0=ALU.mult, op1=ALU.subtract)\
                    .then_inc(mix_ready, 1)

            def split_weights(layer_no):
                dve.wait_ge(split_hi, layer_no + 1)
                for kind in (IH, HH):
                    for gates, sign in ((slice(0, 3, 2), 1.0), (slice(1, 2), -1.0)):
                        last = dve.scalar_tensor_tensor(
                            out=by_gate(gru_lo[layer_no])[:, kind, gates, :],
                            in0=by_gate(gru_f[layer_no])[:, kind, gates, :], scalar=sign * W_SCALE,
                            in1=by_gate(gru_hi[layer_no])[:, kind, gates, :],
                            op0=ALU.mult, op1=ALU.subtract)
                last.then_inc(split_lo, 1)

            def split_expert(piece):
                e, q = piece // PIECES, piece % PIECES
                at = slice(q * PIECE, (q + 1) * PIECE)
                dve.wait_ge(gu_hi_ready, piece + 1)
                dve.scalar_tensor_tensor(out=gu_lo[:, e, at], in0=gu_f[:, e, at], scalar=EW_SCALE,
                                         in1=gu_hi[:, e, at], op0=ALU.mult, op1=ALU.subtract)\
                    .then_inc(gu_lo_ready, 1)

            def gate_times_up(c, s):
                chunk, e = experts_before(c, s, 1)
                if is_chunk(chunk):
                    j = chunk * E + e
                    dve.wait_ge(up_ready, j + 1)
                    if is_last(chunk, e):
                        dve.wait_ge(last_silu_ready, 1)
                    else:
                        dve.wait_ge(silu_ready, j + 1)
                    if in_drain(chunk, e) and j - 2 >= DRAIN_FROM:
                        dve.wait_ge(hidden_lo_dve, j - 1 - DRAIN_FROM)
                    else:
                        wait_count(dve, hidden_lo_pool, j - 1)
                    dve.scalar_tensor_tensor(out=hidden[:, e % 2, :], in0=p_up[:, :], scalar=MOE_UNSCALE / DW_SCALE,
                                             in1=silu[:, e % 2, :], op0=ALU.mult, op1=ALU.mult)\
                        .then_inc(hidden_ready, 1)

            def low_of_hidden(c, s):
                chunk, e = experts_before(c, s, 2)
                if is_chunk(chunk) and in_drain(chunk, e):
                    j = chunk * E + e
                    dve.wait_ge(hidden_hi_ready, j + 1)
                    dve.tensor_tensor(hidden_lo[:, e % 2, :], hidden[:, e % 2, :], hidden_hi[:, e % 2, :],
                                      ALU.subtract).then_inc(hidden_lo_dve, 1)

            def last_silu():
                dve.wait_ge(gate_read, CHUNKS * E)
                dve.tensor_tensor(silu[:, (E - 1) % 2, :], gate_c[:, (E - 1) % 2, :], sig[:, (E - 1) % 2, :],
                                  ALU.mult).then_inc(last_silu_ready, 1)

            def max_of_y(h):
                at = slice(B // 2 * h, B // 2 * (h + 1))
                dve.wait_ge(layer_applied, h + 1)
                dve.tensor_reduce(y_max[:, at], y_banks[:, at, 0:T - STEPS], AX_X, ALU.max, apply_absolute_value=True).then_inc(y_max_ready, 1)

            def add_expert(c, s):
                chunk, e = experts_before(c, s, 3)
                if is_chunk(chunk):
                    j = chunk * E + e
                    dve.wait_ge(y_ready, j + 1)
                    if e == 0:
                        dve.wait_ge(router_step, 7 * (chunk + 1))
                        if isinstance(chunk, int) and chunk == 0:
                            dve.wait_ge(got["x_tok"], 16)
                        old = x1_tok[:, bass.ds(chunk, 1), :].rearrange("p a d -> p (a d)")
                    else:
                        dve.wait_ge(acc_ready, j)
                        old = acc[:, 1 - e % 2, :]
                    if e == 1 and not (isinstance(chunk, int) and chunk == 0):
                        dve.wait_ge(x1_transposed, chunk)
                        dve.wait_ge(x1_kept, chunk)
                    bank = p_gate if is_last(chunk, e) else p_y
                    dve.scalar_tensor_tensor(out=acc[:, e % 2, :], in0=bank[:, 0:D], scalar=shares[:, e:e + 1],
                                             in1=old, op0=ALU.mult, op1=ALU.add).then_inc(acc_ready, 1)

            def router(c, part):
                n = 7 * (c - 1)
                if part == 0:
                    dve.wait_ge(logits_ready, c)
                    dve.tensor_copy(logits[:, :], p_misc[:, 0:E]).then_inc(misc_taken, 1)
                elif part == 1:
                    if not is_chunk(c):
                        dve.wait_ge(misc_taken, misc_before(c) + 2)
                    dve.max(top8[:, :], logits[:, :]).then_inc(router_step, 1)
                    dve.wait_ge(router_step, n + 1)
                    dve.tensor_tensor(top_gap[:, :], top8[:, 1:2], top8[:, 0:1], ALU.subtract)\
                        .then_inc(gap_ready, 1)
                elif part == 2:
                    dve.max_index(top8_at[:, :], top8[:, :], logits[:, :]).then_inc(router_step, 1)
                    dve.wait_ge(router_step, n + 2)
                    dve.tensor_copy(top8_no[:, :], top8_at[:, :]).then_inc(router_step, 1)
                elif part == 3:
                    dve.wait_ge(router_step, n + 3)
                    dve.wait_ge(top_w_ready, c)
                    for k in range(2):
                        dve.tensor_scalar(share[:, k, :], expert_no[:, :], top8_no[:, k:k + 1], top_w[:, k:k + 1],
                                          ALU.is_equal, ALU.mult).then_inc(router_step, 1)
                else:
                    dve.wait_ge(router_step, n + 5)
                    if not (isinstance(c, int) and c == 1):
                        dve.wait_ge(acc_ready, (c - 1) * E)
                    dve.tensor_tensor(shares[:, :], share[:, 0, :], share[:, 1, :], ALU.add)\
                        .then_inc(router_step, 2)

            def split_biases():
                dve.wait_ge(bias_scaled, 4)
                dve.tensor_copy(bias_hi[:, :], bias_f[:, :]).then_inc(bias_step, 1)
                dve.wait_ge(bias_step, 1)
                dve.tensor_copy(bias_parts[0:D // 2, :], bias_hi[0:D // 2, :]).then_inc(bias_step, 1)
                dve.tensor_tensor(bias_parts[D // 2:D, :], bias_f[D // 2:D, :], bias_hi[D // 2:D, :],
                                  ALU.subtract).then_inc(bias_step, 1)

            def cond_step(n):
                if n == 0:
                    dve.wait_ge(got["cond"], 16)
                    dve.tensor_reduce(ln_sum[:, :], cond_sb[:, :], AX_X, ALU.add).then_inc(c_dve, 1)
                    dve.wait_ge(c_dve, 1)
                    dve.tensor_scalar(ln_sum[:, :], ln_sum[:, :], 1.0 / D, None, ALU.mult).then_inc(c_dve, 1)
                    dve.wait_ge(c_dve, 2)
                    dve.tensor_scalar(ln_x[:, :], cond_sb[:, :], ln_sum[:, 0:1], None, ALU.subtract)\
                        .then_inc(c_dve, 1)
                    dve.wait_ge(c_dve, 3)
                    dve.tensor_tensor(ln_sq[:, :], ln_x[:, :], ln_x[:, :], ALU.mult).then_inc(c_dve, 1)
                    dve.wait_ge(c_dve, 4)
                    dve.tensor_reduce(ln_var[:, :], ln_sq[:, :], AX_X, ALU.add).then_inc(c_dve, 1)
                    dve.wait_ge(c_dve, 5)
                    dve.tensor_scalar(ln_var[:, :], ln_var[:, :], 1.0 / D, EPS, ALU.mult, ALU.add)\
                        .then_inc(c_dve, 1)
                elif n == 1:
                    dve.wait_ge(c_pool, 1)
                    dve.tensor_scalar(ln_x[:, :], ln_x[:, :], ln_rstd[:, 0:1], None, ALU.mult)\
                        .then_inc(c_dve, 1)
                elif n == 2:
                    dve.wait_ge(c_pe, 1)
                    dve.wait_ge(got["first"], 16)
                    dve.tensor_scalar(ae[:, :], p_gate[:, 0:B], vec(V_LNG), vec(V_LNB), ALU.mult, ALU.add)\
                        .then_inc(c_dve, 1)
                elif n == 3:
                    dve.wait_ge(c_pe, 18)
                    for k in range(2):
                        dve.tensor_tensor(ab[:, k, :, :],
                                          p_gate[:, k * B * R:(k + 1) * B * R].rearrange("p (b r) -> p b r", r=R),
                                          vec(V_CB2 + k * R, R).rearrange("p (a r) -> p a r", a=1)
                                          .to_broadcast([D, B, R]), ALU.add).then_inc(c_dve, 1)
                    dve.wait_ge(got["proj"], 16)
                    dve.tensor_tensor(base_id[:, :], base, ident[:, :], ALU.add).then_inc(c_dve, 1)
                elif n == 4:
                    dve.wait_ge(c_pe, 20)
                    dve.tensor_copy(ab_T[:, :], p_y[0:B * R, 0:2 * D]).then_inc(c_dve, 1)
                else:
                    half, quarter = (n - 5) // 2, (n - 5) % 2
                    dve.wait_ge(c_pe, 24 + 4 * half)
                    if n == 5:
                        dve.wait_ge(c_dve, 11)
                    at = 4 * half + 2 * quarter
                    dve.tensor_tensor(layer[:, at:at + 2, :],
                                      p_y[:, quarter * 2 * D:(quarter + 1) * 2 * D]
                                      .rearrange("p (b o) -> p b o", b=2),
                                      base_id[:, :].rearrange("p (a o) -> p a o", a=1).to_broadcast([D, 2, D]),
                                      ALU.add).then_inc(c_dve, 1)

            def quant_weights(n):
                if n < 2:
                    dve.wait_ge(got["ffn"], 16)
                    dve.tensor_reduce(w_max[:, n:n + 1], ffn_sb[:, n * F:(n + 1) * F], AX_X, ALU.max,
                                      apply_absolute_value=True).then_inc(wq_dve, 1)
                elif n == 2:
                    dve.wait_ge(wq_pool, 1)
                    dve.tensor_scalar(w_step[:, :], w_amax[:, :], MIN_RANGE, 1.0 / QP, ALU.max, ALU.mult)\
                        .then_inc(wq_dve, 1)
                    dve.wait_ge(wq_dve, 3)
                    dve.reciprocal(w_inv[:, :], w_step[:, :]).then_inc(wq_dve, 1)
                    dve.wait_ge(wq_dve, 4)
                elif n < 5:
                    k = n - 3
                    dve.tensor_scalar(w_round[:, k, :], ffn_sb[:, k * F:(k + 1) * F], w_inv[:, k:k + 1], ROUND,
                                      ALU.mult, ALU.add).then_inc(wq_dve, 1)
                else:
                    k = n - 5
                    dve.wait_ge(wq_dve, 5 + k)
                    dve.tensor_scalar(w_q[:, k, :], w_round[:, k, :], -ROUND, None, ALU.add).then_inc(wq_dve, 1)

            def slot(c, s):
                def between():
                    if s in (START, START + 2, START + 6) and is_chunk(c - 1):
                        router(c, s - START)

                if has_step(c, s):
                    gru(c, s, between)
                else:
                    between()
                if s == LAG and is_chunk(c - 1):
                    dve.wait_ge(o_hi_ready, c)
                    at = bass.ds((c - 1) * TOK, TOK)
                    dve.scalar_tensor_tensor(out=o_lo[:, at], in0=oT[:, :], scalar=O_SCALE, in1=o_hi[:, at],
                                             op0=ALU.mult, op1=ALU.subtract).then_inc(o_lo_ready, 1)
                if expert_of(c, s)[2] == 1:
                    end = s if isinstance(c, int) and c == CHUNKS + 1 else None
                    if end != START + 1:
                        low_of_hidden(c, s)
                    if end == START + 3:
                        max_of_y(0)
                    add_expert(c, s)
                    if end == START + 1:
                        low_of_hidden(c, s)
                    if end == START - 1:
                        last_silu()
                if s in (START + 1, START + 3) and is_chunk(c - 1):
                    router(c, s - START)
                if expert_of(c, s)[2] == 0:
                    gate_times_up(c, s)
                if isinstance(c, int) and c < 2:
                    if c == 0:
                        if 3 <= s <= CHUNKS + 1:
                            mixed_lo(s - 2)
                        if s == 2:
                            split_weights(1)
                        if s == 4:
                            dve.wait_ge(gain_ready, 1)
                            dve.tensor_scalar(gain[:, :], cond_gate[:, :], 1.0, 1.0 / H_SCALE, ALU.add, ALU.mult)\
                                .then_inc(gain_ready, 1)
                    for piece in pieces_of(c, s - 1):
                        split_expert(piece)
                    for n in COND_DVE.get(c * STEPS + s, ()):
                        cond_step(n)
                if isinstance(c, int) and c >= CHUNKS and (c - CHUNKS) * STEPS + s in QUANT_DVE:
                    quant_weights(QUANT_DVE[(c - CHUNKS) * STEPS + s])

            dve.memset(factors[:, :, :, :], 0.0)
            dve.memset(addends[:, :, :], 0.0)
            dve.memset(state[:, 0, 0, :], 0.0)
            dve.memset(state[:, LAG % 2, 1, :], 0.0)
            dve.memset(parts[:, 2 * GROUP - 1, 0, :], 0.0)
            dve.memset(parts[:, LAG - 1, 1, :], 0.0)
            dve.memset(mix_hi[:, N:N + PAD], 0.0)
            dve.memset(mix_lo[:, N:N + PAD], 0.0)
            for k in range(4):
                for layer_no in range(2):
                    dve.memset(bias_on[32 * k:32 * (k + 1), layer_no, :], H_SCALE if k % 2 == layer_no else 0.0)
            dve.memset(z_gate[:, :, :], 0.0).then_inc(cleared, 1)
            dve.wait_ge(cleared, 1)
            dve.memset(factors[:, 0, :, 1:24:3], 1.0)
            dve.memset(factors[:, 1, :, 1:24:3], H_SCALE).then_inc(init_done, 1)
            for n in COND_DVE[-1]:
                cond_step(n)
            split_weights(0)
            split_biases()
            mixed_lo(0)
            for s in range(16):
                slot(0, s)
            for s in range(16):
                slot(1, s)
            with dve.Fori(2, CHUNKS) as c:
                for s in range(16):
                    slot(c, s)
            for s in range(16):
                slot(CHUNKS, s)
            for s in range(START + 7):
                slot(CHUNKS + 1, s)

            max_of_y(1)
            dve.wait_ge(layer_applied, 3)
            dve.tensor_reduce(y_max[:, B:2 * B], y_banks[:, :, T - STEPS:T], AX_X, ALU.max,
                              apply_absolute_value=True).then_inc(y_max_ready, 1)
            dve.wait_ge(y_max_ready, 3)
            dve.tensor_reduce(part_top[:, 0:1], y_max[:, :], AX_X, ALU.max).then_inc(part_max_ready, 1)

            def all_max(k):
                dve.wait_ge(max_turned, k + 1)
                dve.tensor_reduce(row_top[:, k:k + 1], p_y[0:1, 0:D], AX_X, ALU.max).then_inc(row_max_ready, 1)
                dve.wait_ge(max_spread, k + 1)
                dve.tensor_scalar(q_step[:, k:k + 1], p_y[:, 256:257], MIN_RANGE, 1.0 / QP, ALU.max, ALU.mult)\
                    .then_inc(q_step_ready, 1)
                dve.wait_ge(q_step_ready, k + 1)
                dve.reciprocal(q_inv[:, k:k + 1], q_step[:, k:k + 1]).then_inc(step_ready, 1)
                dve.tensor_tensor(out_step[:, k:k + 1], w_step[:, k:k + 1], q_step[:, k:k + 1], ALU.mult)\
                    .then_inc(step_ready, 1)
                dve.wait_ge(step_ready, 2 * k + 2)

            all_max(0)
            for h, times in enumerate(TIMES):
                dve.tensor_scalar(y_round[:, 0:B // 2, times], y_banks[:, 0:B // 2, times],
                                  q_inv[:, 0:1], ROUND, ALU.mult, ALU.add).then_inc(y_rounded_dve, 1)
                dve.wait_ge(y_rounded_dve, h + 1)
                dve.wait_ge(y_rounded_act, h + 1)
                dve.tensor_scalar(y_q[:, :, times], y_round[:, :, times], -ROUND, None, ALU.add)\
                    .then_inc(y_q_ready, 1)
            for k, (f, halves) in enumerate(GELU_TILES):
                dve.wait_ge(gelu_ready, k + 1)
                dve.tensor_reduce(part_max[:, k:k + 1], ffn_h[:, f, halves.start * F:halves.stop * F], AX_X,
                                  ALU.max, apply_absolute_value=True).then_inc(tile_max_ready, 1)
            dve.wait_ge(tile_max_ready, len(GELU_TILES))
            dve.tensor_reduce(part_top[:, 1:2], part_max[:, :], AX_X, ALU.max).then_inc(part_max_ready, 1)
            all_max(1)
            for k in range(2):
                at = slice(k * N // 4, (k + 1) * N // 4)
                dve.tensor_scalar(q_round[:, :, at], ffn_h[:, :, at], q_inv[:, 1:2], ROUND, ALU.mult, ALU.add)\
                    .then_inc(h_rounded_dve, 1)
                dve.wait_ge(h_rounded_dve, k + 1)
                dve.tensor_scalar(ffn_q[:, :, at], q_round[:, :, at], -ROUND, None, ALU.add)\
                    .then_inc(q_ready_dve, 1)
            at = slice(2 * N // 4, 3 * N // 4)
            dve.wait_ge(h_rounded_act, 1)
            dve.tensor_scalar(ffn_q[:, :, at], q_round[:, :, at], -ROUND, None, ALU.add).then_inc(q_ready_dve, 1)
            dve.wait_ge(x1_b2_ready, 1)
            for k, q in enumerate(QUARTERS):
                at = slice(2 * q, 2 * q + 2)
                dve.wait_ge(ffn2_ready, k + 1)
                dve.scalar_tensor_tensor(out=o_sb[:, at, :],
                                         in0=ffn2_banks[q][:, 0:2 * D].rearrange("p (c d) -> p c d", c=2),
                                         scalar=out_step[:, 1:2], in1=x1_b2[:, at, :],
                                         op0=ALU.mult, op1=ALU.add).then_inc(out_ready, 1)

        @block.gpsimd
        def _(pool):
            def scale_down(e):
                if e == 0:
                    pool.wait_ge(got["down"], 16)
                pool.tensor_scalar(down_f[:, e, :, :], down_f[:, e, :, :], DW_SCALE, 0.0, ALU.mult, ALU.add)\
                    .then_inc(down_scaled, 1)

            def low_of_down(e):
                pool.wait_ge(down_hi_ready, e + 1)
                pool.tensor_tensor(down_lo[:, e, :, :], down_f[:, e, :, :], down_hi[:, e, :, :], ALU.subtract)\
                    .then_inc(down_lo_ready, 1)

            def low_of_hidden(c, s):
                chunk, e = experts_before(c, s, 2)
                if is_chunk(chunk) and expert_of(c, s)[2] == 0 and not in_drain(chunk, e):
                    j = chunk * E + e
                    pool.wait_ge(hidden_hi_ready, j + 1)
                    wait_count(pool, y_ready, j - 1)
                    pool.tensor_tensor(hidden_lo[:, e % 2, :], hidden[:, e % 2, :], hidden_hi[:, e % 2, :],
                                       ALU.subtract).then_inc(hidden_lo_pool, 1)

            def silu_of_gate(c, s):
                chunk, e, part = expert_of(c, s)
                if is_chunk(chunk) and part == 1 and not is_last(chunk, e):
                    j = chunk * E + e
                    pool.wait_ge(gate_read, j + 1)
                    wait_count(pool, hidden_ready, j - 1)
                    pool.tensor_tensor(silu[:, e % 2, :], gate_c[:, e % 2, :], sig[:, e % 2, :], ALU.mult)\
                        .then_inc(silu_ready, 1)

            def slot(c, s):
                if isinstance(c, int) and c * STEPS + s == COND_POOL:
                    pool.wait_ge(c_dve, 12)
                    pool.tensor_tensor(b_T[:, :, :],
                                       ab_T[:, D:2 * D].rearrange("p (a d) -> p a d", a=1)
                                       .to_broadcast([B * R, B, D]),
                                       batch_mask[:, :].rearrange("p (b a) -> p b a", a=1)
                                       .to_broadcast([B * R, B, D]), ALU.mult).then_inc(c_pool, 1)
                if isinstance(c, int) and c == CHUNKS and s == QUANT_POOL:
                    pool.wait_ge(wq_dve, 2)
                    pool.partition_all_reduce(w_amax[:, :], w_max[:, :], D, bass.bass_isa.ReduceOp.absmax)\
                        .then_inc(wq_pool, 1)
                if has_l1(c, s):
                    count = c * STEPS + s - LAG
                    if isinstance(c, int) and count == 0:
                        pool.wait_ge(gain_ready, 2)
                    if s == LAG and not (isinstance(c, int) and c == 0):
                        pool.wait_ge(o_projected, c)
                    pool.wait_ge(state_ready, count + LAG + 1)
                    pool.tensor_tensor(gated[:, (s - LAG) % STEPS, :], state[:, (s + 1) % 2, 1, 2:24:3],
                                       gain[:, :], ALU.mult).then_inc(gated_ready, 1)
                if isinstance(c, int):
                    for e in down_of(c, s + 3):
                        scale_down(e)
                    for e in down_of(c, s - 1):
                        low_of_down(e)
                low_of_hidden(c, s)
                silu_of_gate(c, s)
                if s == START + 6 and is_chunk(c - 2):
                    pool.wait_ge(acc_ready, (c - 1) * E)
                    pool.tensor_copy(x1_tok[:, bass.ds(c - 2, 1), :].rearrange("p a d -> p (a d)"), acc[:, 1, :])\
                        .then_inc(x1_kept, 1)

            pool.memset(bias_raw[:, :, :], 0.0).then_inc(bias_cleared, 1)
            pool.memset(warm[:, :], 0.0)
            pool.memset(ones_f[:, :], 1.0)
            pool.memset(pow_half[:, :], -0.5)
            pool.memset(batch_mask[:, :], 1.0)
            pool.memset(ident[:, :], 0.0).then_inc(const_ready, 1)
            pool.wait_ge(const_ready, 1)
            pool.affine_select(out=ident[:, :], in_=ident[:, :], compare_op=ALU.not_equal, fill=1.0, base=0,
                               pattern=[[-1, D]], channel_multiplier=1)
            pool.affine_select(out=batch_mask[:, :], in_=batch_mask[:, :], compare_op=ALU.is_ge, fill=0.0,
                               base=0, pattern=[[-R, B]], channel_multiplier=1).then_inc(iota_ready, 1)
            pool.wait_ge(iota_ready, 1)
            pool.affine_select(out=batch_mask[:, :], in_=batch_mask[:, :], compare_op=ALU.is_ge, fill=0.0,
                               base=R - 1, pattern=[[R, B]], channel_multiplier=-1)
            pool.iota(expert_no_i[:, :], pattern=[[1, E]], base=0, channel_multiplier=0).then_inc(iota_ready, 1)
            pool.wait_ge(iota_ready, 2)
            pool.tensor_copy(expert_no[:, :], expert_no_i[:, :]).then_inc(iota_ready, 1)
            pool.wait_ge(c_dve, 6)
            pool.tensor_tensor(ln_rstd[:, :], ln_var[:, :], pow_half[:, :], ALU.pow).then_inc(c_pool, 1)
            b, raw = bias_f, bias_raw
            pool.wait_ge(got["bias"], 32)
            pool.tensor_tensor(b[:, 0:2 * D], raw[:, IH, 0:2 * D], raw[:, HH, 0:2 * D], ALU.add)\
                .then_inc(bias_scaled, 1)
            pool.tensor_scalar(b[:, 2 * D:4 * D].rearrange("p (k d) -> p k d", k=2), raw[:, :, 2 * D:3 * D],
                               W_SCALE, 0.0, ALU.mult, ALU.add).then_inc(bias_scaled, 1)
            pool.wait_ge(bias_scaled, 2)
            pool.tensor_scalar(b[:, 0:D], b[:, 0:D], W_SCALE, 0.0, ALU.mult, ALU.add).then_inc(bias_scaled, 1)
            pool.tensor_scalar(b[:, D:2 * D], b[:, D:2 * D], -W_SCALE, 0.0, ALU.mult, ALU.add)\
                .then_inc(bias_scaled, 1)
            for s in range(16):
                slot(0, s)
            for s in range(16):
                slot(1, s)
            with pool.Fori(2, CHUNKS) as c:
                for s in range(16):
                    slot(c, s)
            for s in range(16):
                slot(CHUNKS, s)
            for s in range(START + 7):
                slot(CHUNKS + 1, s)

            pool.wait_ge(step_ready, 2)
            pool.tensor_scalar(gelu_bias[:, :], vec(V_B1, FB), out_step[:, 0:1], None, ALU.mult)\
                .then_inc(gelu_bias_ready, 1)
            pool.wait_ge(step_ready, 4)
            pool.tensor_scalar(b2_step[:, :], ffn_b2, out_step[:, 1:2], None, ALU.mult).then_inc(b2_ready, 1)
            pool.wait_ge(b2_ready, 1)
            pool.wait_ge(x1_kept, CHUNKS)
            pool.tensor_tensor(x1_b2[:, :, :], x1_tok[:, :, :],
                               b2_step[:, :].rearrange("p (a d) -> p a d", a=1).to_broadcast([D, CHUNKS, D]),
                               ALU.add).then_inc(x1_b2_ready, 1)


def kernel(x, cond_1024, **w):
    import numpy as np
    from concourse import bacc
    from concourse.bass_utils import run_bass_kernel_spmd

    c = {k: np.asarray(v) for k, v in w.items()}
    x, cond = np.asarray(x), np.asarray(cond_1024)

    def col(v):
        return v.reshape(-1, D).T

    x_time = x.transpose(1, 0, 2).reshape(N, D)

    def gru(i):
        return np.stack([c[f"L0_cond_Wih{i}"].T, c[f"L0_cond_Whh{i}"].T], axis=1)

    arrays = {
        "xT": x_time.T,
        "x_tok": x_time.reshape(CHUNKS, TOK, D).transpose(1, 0, 2),
        "first": np.concatenate([
            c["L0_cond_W_in"].T, cond.T, col(c["L0_cond_b_in"]), col(c["L0_cond_b_gate"]),
            col(c["L0_cond_b_out"]), col(c["L1_cond_ln_g"]), col(c["L1_cond_ln_b"]), col(c["L1_cond_b1"]),
            col(c["L1_ffn_b1"]),
            c["L1_cond_b2"].reshape(2, D, R).transpose(1, 0, 2).reshape(D, 2 * R), c["L1_cond_w1"]], axis=1),
        "gru0": gru(0),
        "gru1": gru(1),
        "proj": np.concatenate([
            c["L0_cond_W_gate"].T, c["L0_cond_W_out"].T, c["L1_cond_base_layer"],
            c["L0_ffn_W_router"].T], axis=1),
        "gate_up": np.concatenate([c["L0_ffn_W_gate"].transpose(2, 0, 1), c["L0_ffn_W_up"].transpose(2, 0, 1)],
                                  axis=2),
        "down": c["L0_ffn_W_down"].reshape(E, D, FB, D).transpose(3, 0, 2, 1),
        "cond_rows": cond,
        "biases": np.stack([np.stack([c[f"L0_cond_bih{i}"], c[f"L0_cond_bhh{i}"]]) for i in range(2)]),
        "cond_w2": c["L1_cond_w2"].reshape(D, 2, D, R).transpose(0, 1, 3, 2).reshape(D, 2 * R, D),
        "ffn": np.concatenate([
            c["L1_ffn_w1"].T, c["L1_ffn_w2"].reshape(D, FB, D).transpose(2, 1, 0).reshape(D, F),
            np.broadcast_to(c["L1_ffn_b2"], (D, D))], axis=1),
    }
    nc = bacc.Bacc("TRN2", target_bir_lowering=False, num_devices=1)
    arrays = {k: np.ascontiguousarray(v) for k, v in arrays.items()}
    args = [nc.dram_tensor(k, a.shape, mybir.dt.from_np(a.dtype), kind="ExternalInput").ap()
            for k, a in arrays.items()]
    out = nc.dram_tensor("out", (TOK, CHUNKS, D), F32, kind="ExternalOutput").ap()
    build(nc, *args, out)
    got = run_bass_kernel_spmd(nc, [arrays], core_ids=[0]).results[0]["out"]
    return got.reshape(STEPS, B, CHUNKS, D).transpose(1, 2, 0, 3).reshape(B, T, D)
```
